# Optimizing a Trainium2 kernel written in Bass

```python
import numpy as np
import jax
import jax.numpy as jnp

def _softmax(x, axis=-1):
    return jax.nn.softmax(x, axis=axis)

def _gelu(x):
    return jax.nn.gelu(x, approximate=True)

def _silu(x):
    return jax.nn.silu(x)

def _sigmoid(x):
    return jax.nn.sigmoid(x)

def _layernorm(x, axis=-1, eps=1e-05):
    m = jnp.mean(x, axis=axis, keepdims=True)
    v = jnp.var(x, axis=axis, keepdims=True)
    return (x - m) / jnp.sqrt(v + eps)

def _scatter_add(tgt, idx, src, axis=0):
    return tgt.at[idx].add(src)

def _segment_sum(src, seg, n):
    return jax.ops.segment_sum(src, seg, n)
kernel_name = 'mk_cond_resid_d4_seqx_r8_238b59'

def setup_inputs(seed: int=0):
    np.random.seed(seed)
    _w = jnp.asarray

    def _rec_inputs():
        import jax
        import jax.numpy as jnp
        _rk = jax.random.key(seed)
        x = -0.000125 + 0.9999 * jax.random.normal(jax.random.fold_in(_rk, 1), (8, 128, 512), jnp.float32)
        _lenS = 128 - jax.random.randint(jax.random.fold_in(_rk, 7), (8,), 0, max(1, 128 // 4) + 1, jnp.int32)
        _lenS2 = 128 - jax.random.randint(jax.random.fold_in(_rk, 8), (8,), 0, max(1, 128 // 4) + 1, jnp.int32)
        itok_B_0_7 = jax.random.randint(jax.random.fold_in(_rk, 11), (8,), 0, 8, jnp.int32)
        itok_B_2_6 = jax.random.randint(jax.random.fold_in(_rk, 12), (8,), 2, 7, jnp.int32)
        itok_B_0_15 = jax.random.randint(jax.random.fold_in(_rk, 13), (8,), 0, 16, jnp.int32)
        itok_Bx16_0_63 = jax.random.randint(jax.random.fold_in(_rk, 14), (8, 16), 0, 64, jnp.int32)
        itok_B_207_1644 = jax.random.randint(jax.random.fold_in(_rk, 15), (8,), 207, 1645, jnp.int32)
        return (x, itok_B_0_7, itok_B_2_6, itok_B_0_15, itok_Bx16_0_63, itok_B_207_1644)
    x, itok_B_0_7, itok_B_2_6, itok_B_0_15, itok_Bx16_0_63, itok_B_207_1644 = _rec_inputs()

    def _L0_cond_setup():
        import jax, jax.numpy as jnp
        import numpy as np
        TOP_K = 2
        LANG_BIAS = 5.0
        SCALING = 32.0 / 16.0
        LANGUAGE_PAD_ID = -1
        key = jax.random.key(seed)
        ks = jax.random.split(key, 6)
        B, T, D, O, E, R = (4, 256, 512, 512, 8, 16)
        x = jax.random.normal(ks[0], (B, T, D), dtype=jnp.float32)
        language_ids = jax.random.randint(ks[1], (B,), 0, E).astype(jnp.int64)
        W = jax.random.normal(ks[2], (O, D), dtype=jnp.float32) * (1.0 / np.sqrt(D))
        Wr = jax.random.normal(ks[3], (E, D), dtype=jnp.float32) * (1.0 / np.sqrt(D))
        A = jax.random.normal(ks[4], (E, R, D), dtype=jnp.float32) * (1.0 / np.sqrt(D))
        Bm = jax.random.normal(ks[5], (O, R), dtype=jnp.float32) * 0.0
        Bm = jnp.broadcast_to(Bm, (E, O, R)) + jax.random.normal(ks[5], (E, O, R), dtype=jnp.float32) * 0.02
        return {'x': x, 'language_ids': language_ids, 'W': W, 'Wr': Wr, 'A': A, 'B': Bm}
    _L0_cond_all = _L0_cond_setup()
    _L0_cond_in = {k: v for k, v in _L0_cond_all.items() if k in ('W', 'Wr', 'A', 'B')}
    del _L0_cond_all

    def _L1_cond_setup():
        import jax, jax.numpy as jnp
        import numpy as np
        B, N, H, F = (4, 64, 512, 1376)
        L, R, RANK = (1, 16, 16)
        SCALE = 0.5
        key = jax.random.key(seed)
        ks = jax.random.split(key, 12)
        nrm = lambda k, shape, fan: jax.random.normal(k, shape, jnp.float32) * fan ** (-0.5)
        inp = {'x': jax.random.normal(ks[0], (B, N, H), jnp.float32), 'W_gate': nrm(ks[1], (F, H), H), 'W_up': nrm(ks[2], (F, H), H), 'W_down': nrm(ks[3], (H, F), F), 'A_gate': nrm(ks[4], (L, R, RANK, H), H), 'B_gate': nrm(ks[5], (L, R, F, RANK), RANK), 'A_up': nrm(ks[6], (L, R, RANK, H), H), 'B_up': nrm(ks[7], (L, R, F, RANK), RANK), 'A_down': nrm(ks[8], (L, R, RANK, F), F), 'B_down': nrm(ks[9], (L, R, H, RANK), RANK), 'lora_indices': jax.random.randint(ks[10], (B,), 0, R), 'layer_idx': 0}
        return inp
    _L1_cond_all = _L1_cond_setup()
    _L1_cond_in = {k: v for k, v in _L1_cond_all.items() if k in ('W_gate', 'W_up', 'W_down', 'A_gate', 'B_gate', 'A_up', 'B_up', 'A_down', 'B_down')}
    del _L1_cond_all

    def _L2_cond_setup():
        import jax, jax.numpy as jnp
        import numpy as np
        MAX_LORAS = 16
        IN, OUT = (512, 512)
        B, S = (8, 256)
        key = jax.random.key(seed)
        k1, k2, k3 = jax.random.split(key, 3)
        x = jax.random.normal(k1, (B, S, IN), dtype=jnp.float32)
        adapter_ids = jax.random.randint(k2, (B,), 0, MAX_LORAS)
        weight = jax.random.normal(k3, (MAX_LORAS, OUT, IN), dtype=jnp.float32) * 0.02
        return {'x': x, 'adapter_ids': adapter_ids, 'weight': weight}
    _L2_cond_all = _L2_cond_setup()
    _L2_cond_in = {k: v for k, v in _L2_cond_all.items() if k in ('weight',)}
    del _L2_cond_all

    def _L3_cond_setup():
        import jax, jax.numpy as jnp
        import numpy as np
        B, S, HID = (4, 128, 512)
        D, HQ, HK = (128, 32, 8)
        PAGES, PSIZE, NPP = (64, 32, 16)
        THETA = 10000.0
        EPS = 1e-06
        SCALE = 1.0 / float(np.sqrt(D))

        def _rmsnorm(t, w):
            var = jnp.mean(t * t, axis=-1, keepdims=True)
            return t * jax.lax.rsqrt(var + EPS) * w

        def _rope(t, pos):
            inv_freq = 1.0 / THETA ** (jnp.arange(0, D, 2, dtype=jnp.float32) / D)
            freqs = pos[..., None].astype(jnp.float32) * inv_freq
            cos = jnp.cos(freqs)[:, :, None, :]
            sin = jnp.sin(freqs)[:, :, None, :]
            t1, t2 = (t[..., :D // 2], t[..., D // 2:])
            return jnp.concatenate([t1 * cos - t2 * sin, t2 * cos + t1 * sin], axis=-1)
        key = jax.random.key(seed)
        ks = jax.random.split(key, 10)
        x = jax.random.normal(ks[0], (B, S, HID), jnp.float32)
        Wq = jax.random.normal(ks[1], (HQ * D, HID), jnp.float32) * 0.02
        Wk = jax.random.normal(ks[2], (HK * D, HID), jnp.float32) * 0.02
        Wv = jax.random.normal(ks[3], (HK * D, HID), jnp.float32) * 0.02
        Wo = jax.random.normal(ks[4], (HID, HQ * D), jnp.float32) * 0.02
        q_norm_w = jax.random.uniform(ks[5], (D,), jnp.float32)
        k_norm_w = jax.random.uniform(ks[6], (D,), jnp.float32)
        k_cache = jax.random.normal(ks[7], (PAGES, PSIZE, HK, D), jnp.float32)
        v_cache = jax.random.normal(ks[8], (PAGES, PSIZE, HK, D), jnp.float32)
        block_table = jnp.arange(B * NPP, dtype=jnp.int32).reshape(B, NPP)
        cache_seqlens = jax.random.randint(ks[9], (B,), 0, 475).astype(jnp.int32)
        return dict(x=x, Wq=Wq, Wk=Wk, Wv=Wv, Wo=Wo, q_norm_w=q_norm_w, k_norm_w=k_norm_w, k_cache=k_cache, v_cache=v_cache, block_table=block_table, cache_seqlens=cache_seqlens)
    _L3_cond_all = _L3_cond_setup()
    _L3_cond_in = {k: v for k, v in _L3_cond_all.items() if k in ('Wq', 'Wk', 'Wv', 'Wo', 'q_norm_w', 'k_norm_w', 'k_cache', 'v_cache')}
    del _L3_cond_all
    return {'x': x, 'itok_B_0_7': itok_B_0_7, 'itok_B_2_6': itok_B_2_6, 'itok_B_0_15': itok_B_0_15, 'itok_Bx16_0_63': itok_Bx16_0_63, 'itok_B_207_1644': itok_B_207_1644, 'L0_cond_W': _L0_cond_in['W'], 'L0_cond_Wr': _L0_cond_in['Wr'], 'L0_cond_A': _L0_cond_in['A'], 'L0_cond_B': _L0_cond_in['B'], 'L1_cond_W_gate': _L1_cond_in['W_gate'], 'L1_cond_W_up': _L1_cond_in['W_up'], 'L1_cond_W_down': _L1_cond_in['W_down'], 'L1_cond_A_gate': _L1_cond_in['A_gate'], 'L1_cond_B_gate': _L1_cond_in['B_gate'], 'L1_cond_A_up': _L1_cond_in['A_up'], 'L1_cond_B_up': _L1_cond_in['B_up'], 'L1_cond_A_down': _L1_cond_in['A_down'], 'L1_cond_B_down': _L1_cond_in['B_down'], 'L2_cond_weight': _L2_cond_in['weight'], 'L3_cond_Wq': _L3_cond_in['Wq'], 'L3_cond_Wk': _L3_cond_in['Wk'], 'L3_cond_Wv': _L3_cond_in['Wv'], 'L3_cond_Wo': _L3_cond_in['Wo'], 'L3_cond_q_norm_w': _L3_cond_in['q_norm_w'], 'L3_cond_k_norm_w': _L3_cond_in['k_norm_w'], 'L3_cond_k_cache': _L3_cond_in['k_cache'], 'L3_cond_v_cache': _L3_cond_in['v_cache']}

def reference(x, itok_B_0_7, itok_B_2_6, itok_B_0_15, itok_Bx16_0_63, itok_B_207_1644, L0_cond_W, L0_cond_Wr, L0_cond_A, L0_cond_B, L1_cond_W_gate, L1_cond_W_up, L1_cond_W_down, L1_cond_A_gate, L1_cond_B_gate, L1_cond_A_up, L1_cond_B_up, L1_cond_A_down, L1_cond_B_down, L2_cond_weight, L3_cond_Wq, L3_cond_Wk, L3_cond_Wv, L3_cond_Wo, L3_cond_q_norm_w, L3_cond_k_norm_w, L3_cond_k_cache, L3_cond_v_cache):
    import jax
    import jax.numpy as jnp

    def _L0_cond_ref(x, language_ids, W, Wr, A, B):
        import jax, jax.numpy as jnp
        import numpy as np
        TOP_K = 2
        LANG_BIAS = 5.0
        SCALING = 32.0 / 16.0
        LANGUAGE_PAD_ID = -1
        base = jnp.einsum('btd,od->bto', x, W)
        E = Wr.shape[0]
        logits = jnp.einsum('btd,ed->bte', x.astype(jnp.float32), Wr.astype(jnp.float32))
        expert_targets = language_ids
        valid = expert_targets >= 0
        tgt = jnp.where(valid, expert_targets, 0)
        bias = jax.nn.one_hot(tgt, E, dtype=logits.dtype) * LANG_BIAS
        bias = jnp.where(valid[:, None], bias, 0.0)
        logits = logits + bias[:, None, :]
        topw, topi = jax.lax.top_k(logits, TOP_K)
        weights = jax.nn.softmax(topw, axis=-1)
        gates = jnp.sum(jax.nn.one_hot(topi, E, dtype=weights.dtype) * weights[..., None], axis=-2)
        gates = gates.astype(x.dtype)
        h = jnp.einsum('btd,erd->bter', x, A)
        lora_out = jnp.einsum('bter,bte,eor->bto', h, gates, B)
        return base + SCALING * lora_out

    def _L1_cond_ref(x, W_gate, W_up, W_down, A_gate, B_gate, A_up, B_up, A_down, B_down, lora_indices, layer_idx):
        import jax, jax.numpy as jnp
        import numpy as np
        B, N, H, F = (4, 64, 512, 1376)
        L, R, RANK = (1, 16, 16)
        SCALE = 0.5

        def lora_add(base, inp, A, B):
            Ab = A[layer_idx][lora_indices]
            Bb = B[layer_idx][lora_indices]
            t = jnp.einsum('bri,bni->bnr', Ab, inp)
            return base + jnp.einsum('bor,bnr->bno', Bb, t) * SCALE
        gate = lora_add(jnp.einsum('bnh,fh->bnf', x, W_gate), x, A_gate, B_gate)
        up = lora_add(jnp.einsum('bnh,fh->bnf', x, W_up), x, A_up, B_up)
        act = jax.nn.silu(gate) * up
        down = lora_add(jnp.einsum('bnf,hf->bnh', act, W_down), act, A_down, B_down)
        return down

    def _L2_cond_ref(x, adapter_ids, weight):
        import jax, jax.numpy as jnp
        import numpy as np
        MAX_LORAS = 16
        IN, OUT = (512, 512)
        B, S = (8, 256)
        w = weight[adapter_ids]
        return jnp.einsum('bsi,boi->bso', x, w)

    def _L3_cond_ref(x, Wq, Wk, Wv, Wo, q_norm_w, k_norm_w, k_cache, v_cache, block_table, cache_seqlens):
        import jax, jax.numpy as jnp
        import numpy as np
        B, S, HID = (4, 128, 512)
        D, HQ, HK = (128, 32, 8)
        PAGES, PSIZE, NPP = (64, 32, 16)
        THETA = 10000.0
        EPS = 1e-06
        SCALE = 1.0 / float(np.sqrt(D))

        def _rmsnorm(t, w):
            var = jnp.mean(t * t, axis=-1, keepdims=True)
            return t * jax.lax.rsqrt(var + EPS) * w

        def _rope(t, pos):
            inv_freq = 1.0 / THETA ** (jnp.arange(0, D, 2, dtype=jnp.float32) / D)
            freqs = pos[..., None].astype(jnp.float32) * inv_freq
            cos = jnp.cos(freqs)[:, :, None, :]
            sin = jnp.sin(freqs)[:, :, None, :]
            t1, t2 = (t[..., :D // 2], t[..., D // 2:])
            return jnp.concatenate([t1 * cos - t2 * sin, t2 * cos + t1 * sin], axis=-1)
        bsz, seqlen, _ = x.shape
        q = jnp.einsum('bsd,ed->bse', x, Wq).reshape(bsz, seqlen, HQ, D)
        k = jnp.einsum('bsd,ed->bse', x, Wk).reshape(bsz, seqlen, HK, D)
        v = jnp.einsum('bsd,ed->bse', x, Wv).reshape(bsz, seqlen, HK, D)
        q = _rmsnorm(q, q_norm_w)
        k = _rmsnorm(k, k_norm_w)
        pos = cache_seqlens[:, None] + jnp.arange(seqlen)[None, :]
        q = _rope(q, pos)
        k = _rope(k, pos)
        L = NPP * PSIZE
        kc = k_cache[block_table].reshape(bsz, L, HK, D)
        vc = v_cache[block_table].reshape(bsz, L, HK, D)
        k_all = jnp.concatenate([kc, k], axis=1)
        v_all = jnp.concatenate([vc, v], axis=1)
        valid_c = jnp.arange(L)[None, :] < cache_seqlens[:, None]
        valid = jnp.concatenate([valid_c, jnp.ones((bsz, seqlen), dtype=bool)], axis=1)
        rep = HQ // HK
        k_all = jnp.repeat(k_all, rep, axis=2)
        v_all = jnp.repeat(v_all, rep, axis=2)
        scores = jnp.einsum('bqhd,bkhd->bhqk', q, k_all) * SCALE
        scores = jnp.where(valid[:, None, None, :], scores, -1e+30)
        probs = jax.nn.softmax(scores, axis=-1)
        o = jnp.einsum('bhqk,bkhd->bqhd', probs, v_all)
        o = o.reshape(bsz, seqlen, HQ * D)
        return jnp.einsum('bse,de->bsd', o, Wo)
    x = x + _L0_cond_ref(x, itok_B_0_7, L0_cond_W, L0_cond_Wr, L0_cond_A, L0_cond_B)
    x = x + _L1_cond_ref(x, L1_cond_W_gate, L1_cond_W_up, L1_cond_W_down, L1_cond_A_gate, L1_cond_B_gate, L1_cond_A_up, L1_cond_B_up, L1_cond_A_down, L1_cond_B_down, itok_B_2_6, 0)
    x = x + _L2_cond_ref(x, itok_B_0_15, L2_cond_weight)
    x = x + _L3_cond_ref(x, L3_cond_Wq, L3_cond_Wk, L3_cond_Wv, L3_cond_Wo, L3_cond_q_norm_w, L3_cond_k_norm_w, L3_cond_k_cache, L3_cond_v_cache, itok_Bx16_0_63, itok_B_207_1644)
    return x

_drawn_inputs = setup_inputs


def setup_inputs(seed=0):
    import zlib

    import numpy as np

    out = dict(_drawn_inputs(seed))
    spreads = {}
    factors = {'L0_cond_Wr': 4.223,
     'L3_cond_Wq': 4.308,
     'L3_cond_Wk': 8.0,
     'L3_cond_Wv': 4.807,
     'L3_cond_q_norm_w': 7.493,
     'L3_cond_k_norm_w': 8.0,
     'L3_cond_k_cache': 4.54}
    for name, (base, spread) in spreads.items():
        noise = np.random.default_rng([zlib.crc32(name.encode()), seed]).standard_normal(out[name].shape)
        drawn = base * np.exp(spread * noise) if base else spread * noise
        out[name] = jnp.asarray(drawn.astype(out[name].dtype))
    for name, factor in factors.items():
        out[name] = (out[name] * factor).astype(out[name].dtype)
    return out
```

```python
import math
from contextlib import ExitStack

import concourse.bass as bass
from concourse import mybir

ALU = mybir.AluOpType
ACT = mybir.ActivationFunctionType
AX = mybir.AxisListType
F32 = mybir.dt.float32
F16 = mybir.dt.float16
BF16 = mybir.dt.bfloat16
I32 = mybir.dt.int32

P = 128
NB, T, D = 8, 128, 512
NT = NB * T
HALF = NT // 2
KD = D // P
E, R = 8, 16
F = 1376
FT = -(-F // P)
FP = FT * P
HK, REP, DH = 8, 4, 128
PAGE, NPAGE = 32, 16
CACHED = PAGE * NPAGE
KEYS = CACHED + T
KT = KEYS // P
HB = 2
BLOCKS = HK // HB
STEPS = BLOCKS * NB
GROUPS = STEPS * HB
SCALE = 1.0 / math.sqrt(DH)
EPS = 1e-6
TWO_PI = 2 * math.pi
PI_A = 6.28125
PI_B = 0.0019350051879882812
PI_C = TWO_PI - PI_A - PI_B
ROUND = 12582912.0
NEG = -1e30


def build(nc, a, out):
    ds = bass.ds
    base = 16512
    KB = 1024

    class Region:
        def __init__(self, start, size):
            self.at, self.end = start, start + size

        def take(self, name, shape, dt=F32):
            size = 2 if dt in (F16, BF16) else 4
            for n in shape[1:]:
                size *= n
            t = nc.alloc_sbuf_tensor_at(name, shape, dt, offset=self.at)
            self.at += -(-size // 32) * 32
            assert self.at <= self.end, name
            return t

    at = [base]

    def region(size):
        at[0] += size
        return at[0] - size

    r_xa, r_xb, r_acc, r_rope, r_kv = (region(16 * KB) for _ in range(5))
    r_w = region(80 * KB)
    r_arena = region(38 * KB + 512)
    r_small = region(nc.sbuf_usable_end - at[0] - 32)

    xa = Region(r_xa, 16 * KB).take("x_even", [P, KD, NT])
    xb = Region(r_xb, 16 * KB).take("x_odd", [P, KD, NT])
    acc = Region(r_acc, 16 * KB).take("acc", [P, NB, D])
    rope = Region(r_rope, 16 * KB)
    cos_q, sin_q, cos_k, sin_k = (rope.take(n, [P, NB, DH]) for n in ("cos_q", "sin_q", "cos_k", "sin_k"))
    kv = Region(r_kv, 16 * KB)
    kc = [kv.take(f"kc{i}", [P, NPAGE, HB, PAGE]) for i in range(2)]
    vc = [kv.take(f"vc{i}", [P, CACHED // P, HB * DH]) for i in range(2)]
    w3 = Region(r_w, 80 * KB)
    W3 = {"wq": (KD, HB * REP * DH), "wkv": (KD, 2 * HB * DH), "wo": (HB * REP, D)}
    w3_at, set_size = {}, 0
    for name, (rows, cols) in W3.items():
        w3_at[name] = set_size
        set_size += rows * cols
    w3_all = w3.take("w3_all", [P, 2, set_size])
    r_w1 = r_w + 4 * set_size

    def w3_set(name, which):
        rows, cols = W3[name]
        one = w3_all[:, which, w3_at[name]:w3_at[name] + rows * cols]
        if len(one.shape) == 3:
            one = one.rearrange("p o n -> p (o n)")
        return one.rearrange("p (k n) -> p k n", n=cols)

    small = Region(r_small, nc.sbuf_usable_end - r_small)
    ident = small.take("ident", [P, P])
    iota = small.take("iota", [P, CACHED], F16)
    mask = [small.take(f"mask{i}", [P, KEYS], BF16) for i in range(2)]
    len_i = small.take("len_i", [P, NB], I32)
    len_f = small.take("len_f", [P, NB])
    lang_i = small.take("lang_i", [P, NB], I32)
    lang_f = small.take("lang_f", [P, NB])
    ids = small.take("ids", [1, 2 * NB + NB * NPAGE], I32)
    own = small.take("own", [P, NB])
    neghalf = small.take("neghalf", [P, REP])
    negmax = small.take("negmax", [P, HB, REP])
    den = small.take("den", [P, HB, REP])
    rden = small.take("rden", [P, HB, REP])
    ss_k = small.take("ss_k", [P, HB])
    ss_q = small.take("ss_q", [P, HB, REP])
    ms = small.take("ms", [P, REP])
    rs_k = small.take("rs_k", [P, HB])
    rs_q = small.take("rs_q", [P, HB, REP])
    part_ck = small.take("part_ck", [P, HB, DH])
    k_raw = small.take("k_raw", [P, HB, DH])
    q_raw = small.take("q_raw", [P, REP, DH])

    ar = Region(r_arena, 38 * KB + 512)
    prob = [ar.take(f"prob{i}", [P, REP, KEYS]) for i in range(2)]
    o_t = [ar.take(f"o_t{i}", [P, REP, T]) for i in range(2)]
    q_t = [ar.take(f"q_t{i}", [P, REP, T]) for i in range(2)]
    k_new = [ar.take(f"k_new{i}", [P, HB, T]) for i in range(2)]
    v_new = [ar.take(f"v_new{i}", [P, HB, DH]) for i in range(2)]
    x_now = [ar.take(f"x_now{i}", [P, KD, T]) for i in range(2)]
    k_rot = ar.take("k_rot", [P, HB, DH])
    junk = ar.take("junk", [P, 2, DH], BF16)
    part_sk = ar.take("part_sk", [P, HB, DH])
    ov = Region(r_xa, 16 * KB)
    prob_t = [ov.take(f"prob_t{i}", [P, REP * T]) for i in range(KT)]
    part_c = ov.take("part_c", [P, REP, DH])
    part_s = ov.take("part_s", [P, REP, DH])
    q_rot = ov.take("q_rot", [P, REP, DH])

    z = Region(r_w1, 44 * KB)
    w0 = z.take("w0", [P, KD, D])
    wr = z.take("wr", [P, KD, E])
    a0 = z.take("a0", [P, KD, E * R])
    b0 = z.take("b0", [P, D])
    gate_x = z.take("gate_x", [P, NB, E * R])
    h_sb = z.take("h_sb", [P, NT])
    h_gated = z.take("h_gated", [P, NT])
    ang, turns, red = (z.take(n, [P, NB, DH // 2]) for n in ("ang", "turns", "red"))
    trig = z.take("trig", [P, 2, NB, DH // 2])
    norm_w = z.take("norm_w", [P, 2, DH])
    inv_f = z.take("inv_f", [P, DH // 2])
    pos = z.take("pos", [P, NB])
    logit, cand, one1, one2, less, gates, lang = (
        z.take(n, [P, NB, E]) for n in ("logit", "cand", "one1", "one2", "less", "gates", "lang"))
    top1, top2, pick, gap, e_gap, g1, g2 = (
        z.take(n, [P, NB]) for n in ("top1", "top2", "pick", "gap", "e_gap", "g1", "g2"))
    act = Region(r_w1, 44 * KB).take("act", [P, FT, NT])
    y = Region(r_arena + 4 * KB, 34 * KB)
    w_gu = [y.take(f"w_gu{i}", [P, 2, KD, P]) for i in range(2)]
    t_gate, t_up = y.take("t_gate", [P, NT]), y.take("t_up", [P, NT])
    sil = [y.take(f"sil{i}", [P, HALF]) for i in range(2)]
    a_up, b_up = y.take("a_up", [P, KD, NB * R]), y.take("b_up", [P, FP])
    b_now = [y.take(f"b_now{i}", [P, 2, P]) for i in range(2)]
    y = Region(r_acc, 16 * KB)
    a_down, b_gate = y.take("a_down", [P, FT, NB * R]), y.take("b_gate", [P, FP])
    b_down, a_gate = y.take("b_down", [P, D]), y.take("a_gate", [P, KD, NB * R])
    y = Region(r_kv, 16 * KB)
    w_down = [y.take(f"w_down{i}", [P, FT, P]) for i in range(2)]
    y = Region(r_kv, 16 * KB)
    a_raw = {n: y.take(f"{n}_raw", [P, NB, k, R]) for n, k in (("a_gate", KD), ("a_up", KD), ("a_down", FT))}
    t_down = Region(r_arena + 12 * KB, 4 * KB).take("t_down", [P, NT])
    w2 = [Region(r_arena + 4 * KB, 8 * KB).take("w2_0", [P, KD, D]),
          Region(r_arena + 16 * KB, 8 * KB).take("w2_1", [P, KD, D])]
    y = Region(r_arena + 24 * KB, 4 * KB)
    x_sum = [y.take(f"x_sum{i}", [P, KD, T]) for i in range(2)]

    with ExitStack() as ctx:
        ps = ctx.enter_context(nc.psum_tensor("ps", [P, 8, 512], F32))
        s_ps = ps[:, 0:4, :].rearrange("p (s b) n -> p s (b n)", s=2)
        PT, OB, PJ = (4, 5), 6, 7

        def sem(name):
            return ctx.enter_context(nc.semaphore(name))

        x_loaded, l0_loaded, ids_loaded, rows_loaded = sem("x_loaded"), sem("l0_loaded"), sem("ids_loaded"), sem("rows_loaded")
        lora_loaded = sem("lora_loaded")
        gu_loaded = [sem(f"gu_loaded{i}") for i in range(2)]
        down_loaded = [sem(f"down_loaded{i}") for i in range(2)]
        w2_loaded = [sem(f"w2_loaded{i}") for i in range(2)]
        w3_loaded = sem("w3_loaded")
        k_loaded, v_loaded = ([sem(f"{n}_loaded{i}") for i in range(2)] for n in "kv")
        stored, passed = sem("stored"), sem("passed")
        pool_step, dve_step, act_step = sem("pool_step"), sem("dve_step"), sem("act_step")
        consts_ready, sin_ready, angle_ready, tables_ready = sem("consts_ready"), sem("sin_ready"), sem("angle_ready"), sem("tables_ready")
        logits_ready, gap_ready, gap_exp, gates_ready = sem("logits_ready"), sem("gap_ready"), sem("gap_exp"), sem("gates_ready")
        h0_ready, h0_copied, gate_t, h_ready, l0_out, x1_ready = (
            sem("h0_ready"), sem("h0_copied"), sem("gate_t"), sem("h_ready"), sem("l0_out"), sem("x1_ready"))
        t_full, t_ready, td_full, td_ready = sem("t_full"), sem("t_ready"), sem("td_full"), sem("td_ready")
        rows_laid = sem("rows_laid")
        slice_ready, gate_done, up_done, exp_g, silu_step, act_ready = (
            sem("slice_ready"), sem("gate_done"), sem("up_done"), sem("exp_g"), sem("silu_step"), sem("act_ready"))
        l1_out, x2_ready = sem("l1_out"), sem("x2_ready")
        l2_out, x3_summed, x3_copied, x3_turned, acc_ready = (
            sem("l2_out"), sem("x3_summed"), sem("x3_copied"), sem("x3_turned"), sem("acc_ready"))
        x_now_ready, mask_ready = sem("x_now_ready"), sem("mask_ready")
        kv_projected, q_projected = sem("kv_projected"), sem("q_projected")
        squared, ms_ready, rstd_ready = sem("squared"), sem("ms_ready"), sem("rstd_ready")
        v_taken, k_raw_ready, q_raw_ready, k_read, k_roped, q_sine, q_roped = sem("v_taken"), sem("k_raw_ready"), sem("q_raw_ready"), sem("k_read"), sem("k_roped"), sem("q_sine"), sem("q_roped")
        q_cosine = sem("q_cosine")
        k_turned, k_taken, q_turned, q_taken = sem("k_turned"), sem("k_taken"), sem("q_turned"), sem("q_taken")
        scored, masked, exp_done, rden_ready, prob_ready = (
            sem("scored"), sem("masked"), sem("exp_done"), sem("rden_ready"), sem("prob_ready"))
        pt_full, pt_act, pt_dve, pv_done = sem("pt_full"), sem("pt_act"), sem("pt_dve"), sem("pv_done")
        o_taken, out_projected, out_added = sem("o_taken"), sem("out_projected"), sem("out_added")

        def wait(eng, s, v):
            if not (isinstance(v, int) and v <= 0):
                eng.wait_ge(s, v)

        def settle(eng, n):
            if not isinstance(n, int):
                eng.sem_inc(passed)

        def over_steps(eng, step):
            step(0, 0, False)
            step(1, 1, False)
            with eng.Fori(1, STEPS // 2 - 1) as c:
                step(2 * c, 0, False)
                step(2 * c + 1, 1, False)
            step(STEPS - 2, 0, False)
            step(STEPS - 1, 1, True)

        def over_hidden(eng, tile):
            tile(0, 0)
            tile(1, 1)
            with eng.Fori(1, FT // 2) as c:
                tile(2 * c, 0)
                tile(2 * c + 1, 1)
            tile(FT - 1, 0)

        def over_batches(eng, batch):
            batch(0, 0)
            batch(1, 1)
            with eng.Fori(1, NB // 2) as c:
                batch(2 * c, 0)
                batch(2 * c + 1, 1)

        block = ctx.enter_context(nc.Block())

        @block.sync
        def _(sp):
            sp.dma_start(ids[:], a["ids"]).then_inc(rows_loaded, 16)
            sp.dma_start(xa[:], a["x"]).then_inc(x_loaded, 16)
            for dst, name in ((wr, "wr"), (a0, "a0"), (w0, "w0"), (b0, "b0")):
                sp.dma_start(dst[:], a[name]).then_inc(l0_loaded, 16)
            sp.wait_ge(rows_loaded, 16)
            for b in range(NB):
                row = sp.value_load(ids[0:1, b:b + 1], min_val=0, max_val=15)
                for name, dst in a_raw.items():
                    sp.dma_start(dst[:, b], a[name][ds(row, 1)].rearrange("o p k r -> (o p) k r")).then_inc(lora_loaded, 16)
                for dst, name in ((b_gate, "b_gate"), (b_up, "b_up"), (b_down, "b_down")):
                    sp.dma_start(dst[b * R:(b + 1) * R, :],
                                 a[name][ds(row, 1)].rearrange("o r f -> (o r) f")).then_inc(lora_loaded, 16)

            def load_gu(f, par):
                wait(sp, up_done, 2 * f - 2)
                sp.dma_start(w_gu[par][:], a["w_gu"][ds(f, 1)].rearrange("o p g k n -> (o p) g k n")
                             ).then_inc(gu_loaded[par], 16)

            def load_w3(k):
                for name in W3:
                    sp.dma_start(w3_set(name, k % 2), a[name][k]).then_inc(w3_loaded, 16)

            load_gu(0, 0)
            load_gu(1, 1)
            load_w3(0)
            with sp.Fori(1, FT // 2) as c:
                load_gu(2 * c, 0)
                load_gu(2 * c + 1, 1)
            load_gu(FT - 1, 0)
            sp.wait_ge(slice_ready, 1)
            for o in range(KD):
                wait(sp, l1_out, 2 * (o - 1))
                sp.dma_start(w_down[o % 2][:], a["w_down"][o]).then_inc(down_loaded[o % 2], 16)
                if o == 1:
                    sp.wait_ge(act_ready, 2 * FT)

            def load_w2(b, par):
                wait(sp, l2_out, b - 1)
                sp.wait_ge(rows_loaded, 16)
                row = sp.value_load(ids[0:1, ds(NB + b, 1)], min_val=0, max_val=15)
                sp.dma_start(w2[par][:], a["w2"][ds(row, 1)].rearrange("o p k n -> (o p) k n")
                             ).then_inc(w2_loaded[par], 16)

            sp.wait_ge(up_done, 2 * FT)
            over_batches(sp, load_w2)
            sp.wait_ge(l1_out, 2 * KD)

            def load_kv(m, par):
                wait(sp, scored, 8 * m - 8)
                settle(sp, m)
                sp.wait_ge(rows_loaded, 16)
                b, k = m % NB, m // NB
                for j in range(NPAGE):
                    page = sp.value_load(ids[0:1, ds(2 * NB + b * NPAGE + j, 1)], min_val=0, max_val=63)
                    sp.dma_start(kc[par][:, j], a["k_cache"][ds(page, 1), ds(k, 1)].rearrange("g o d s t -> (g o d) s t")
                                 ).then_inc(k_loaded[par], 16)
                wait(sp, pv_done, 2 * KT * (m - 1))
                settle(sp, m)
                for j in range(NPAGE):
                    page = sp.value_load(ids[0:1, ds(2 * NB + b * NPAGE + j, 1)], min_val=0, max_val=63)
                    q = j % 4 * PAGE
                    sp.dma_start(vc[par][q:q + PAGE, j // 4], a["v_cache"][ds(page, 1), ds(k, 1)].rearrange(
                        "g o t n -> (g o t) n")).then_inc(v_loaded[par], 16)

            load_kv(0, 0)
            load_kv(1, 1)
            for k in range(1, BLOCKS):
                sp.wait_ge(w3_loaded, 48 * k)
                wait(sp, out_projected, 16 * (k - 1))
                load_w3(k)
                with sp.Fori(4 * (k - 1) + 1, 4 * k + 1 if k < BLOCKS - 1 else STEPS // 2) as c:
                    load_kv(2 * c, 0)
                    load_kv(2 * c + 1, 1)
            sp.wait_ge(out_added, GROUPS)
            sp.dma_start(out, acc[:]).then_inc(stored, 16)
            sp.wait_ge(stored, 16)

        @block.gpsimd
        def _(pool):
            for dst, name in ((len_i, "lens"), (lang_i, "lang")):
                pool.dma_start(dst[:], a[name].partition_broadcast(P)).then_inc(ids_loaded, 16)
            pool.dma_start(inv_f[:], a["inv_f"].partition_broadcast(P)).then_inc(ids_loaded, 16)
            pool.dma_start(norm_w[:, 0, :], a["q_norm"].partition_broadcast(P)).then_inc(ids_loaded, 16)
            pool.dma_start(norm_w[:, 1, :], a["k_norm"].partition_broadcast(P)).then_inc(ids_loaded, 16)
            pool.iota(iota[:], [[1, CACHED]], base=0, channel_multiplier=0, allow_small_or_imprecise_dtypes=True)
            pool.iota(lang[:], [[0, NB], [1, E]], base=0, channel_multiplier=0, allow_small_or_imprecise_dtypes=True)
            pool.iota(pos[:], [[0, NB]], base=0, channel_multiplier=1, allow_small_or_imprecise_dtypes=True)
            pool.memset(neghalf[:], -0.5)
            for i in range(2):
                pool.memset(mask[i][:, CACHED:KEYS], 0.0)
            pool.memset(own[:], 0.5)
            pool.memset(ident[:], 0.0).then_inc(pool_step, 1)
            pool.wait_ge(pool_step, 1)
            pool.affine_select(out=ident[:], in_=ident[:], compare_op=ALU.not_equal, fill=1.0, base=0,
                               pattern=[[-1, P]], channel_multiplier=1)
            pool.affine_select(out=own[:], in_=own[:], compare_op=ALU.is_ge, fill=0.0, base=0,
                               pattern=[[-R, NB]], channel_multiplier=1).then_inc(pool_step, 1)
            pool.wait_ge(pool_step, 2)
            pool.affine_select(out=own[:], in_=own[:], compare_op=ALU.is_ge, fill=0.0, base=R - 1,
                               pattern=[[R, NB]], channel_multiplier=-1).then_inc(consts_ready, 1)

            def b_slices(f, par):
                wait(pool, up_done, 2 * f - 2)
                pool.tensor_copy(b_now[par][:, 0], b_gate[:, ds(f * P, P)])
                pool.tensor_copy(b_now[par][:, 1], b_up[:, ds(f * P, P)]).then_inc(slice_ready, 1)

            pool.wait_ge(lora_loaded, 16 * 6 * NB)
            for name, dst in (("a_gate", a_gate), ("a_up", a_up), ("a_down", a_down)):
                pool.tensor_scalar(dst[:].rearrange("p k (b r) -> p k b r", r=R),
                                   a_raw[name][:].rearrange("p b k r -> p k b r"),
                                   1.0, 1.0, ALU.mult, ALU.mult).then_inc(rows_laid, 1)
            over_hidden(pool, b_slices)

            def rstd_k(m):
                pool.wait_ge(squared, 10 * m + 2)
                wait(pool, rstd_ready, 3 * m)
                settle(pool, m)
                pool.tensor_scalar(ms[:, 0:HB], ss_k[:], 1.0 / DH, EPS, ALU.mult, ALU.add).then_inc(ms_ready, 1)
                pool.wait_ge(ms_ready, 5 * m + 1)
                pool.tensor_tensor(rs_k[:], ms[:, 0:HB], neghalf[:, 0:HB], ALU.pow).then_inc(rstd_ready, 1)

            def rstd_q(m, s):
                pool.wait_ge(squared, 10 * m + 6 + 4 * s)
                pool.wait_ge(rstd_ready, 3 * m + 1 + s)
                if s == 0 or not isinstance(m, int) or m > 0:
                    wait(pool, masked, 8 * m + 4 * s - 4)
                settle(pool, m)
                pool.tensor_scalar(ms[:], ss_q[:, s], 1.0, DH * EPS, ALU.mult, ALU.add).then_inc(ms_ready, 1)
                pool.wait_ge(ms_ready, 5 * m + 2 + 2 * s)
                pool.tensor_tensor(ms[:], ms[:], neghalf[:], ALU.pow).then_inc(ms_ready, 1)
                pool.wait_ge(ms_ready, 5 * m + 3 + 2 * s)
                settle(pool, m)
                pool.tensor_scalar(rs_q[:, s], ms[:], -1.0, 1.0, ALU.mult, ALU.mult).then_inc(rstd_ready, 1)

            def sine_q(m, s):
                pool.wait_ge(q_raw_ready, 2 * m + s + 1)
                wait(pool, q_roped, 2 * m + s)
                settle(pool, m)
                pool.tensor_tensor(part_s[:], q_raw[:], sin_q[:, ds(m % NB, 1), :].to_broadcast([P, REP, DH]), ALU.mult
                                   ).then_inc(q_sine, 1)

            def scale_probs(j, s, h):
                pool.wait_ge(rden_ready, 4 * j + h + 1)
                settle(pool, j)
                pool.tensor_scalar(prob[s][:, h], prob[s][:, h], rden[:, s, h:h + 1], 1.0, ALU.mult, ALU.mult
                                   ).then_inc(prob_ready, 1)

            rstd_k(0)
            sine_q(0, 0)
            rstd_q(0, 0)
            sine_q(0, 1)
            rstd_q(0, 1)
            for h in range(REP):
                scale_probs(0, 0, h)

            def step(n, par, last):
                if not last:
                    rstd_k(n + 1)
                scale_probs(2 * n + 1, 1, 0)
                if not last:
                    sine_q(n + 1, 0)
                    rstd_q(n + 1, 0)
                for h in range(1, REP):
                    scale_probs(2 * n + 1, 1, h)
                if not last:
                    scale_probs(2 * n + 2, 0, 0)
                    sine_q(n + 1, 1)
                    rstd_q(n + 1, 1)
                    for h in range(1, REP):
                        scale_probs(2 * n + 2, 0, h)

            over_steps(pool, step)

        @block.tensor
        def _(pe):
            pe.wait_ge(x_loaded, 16)
            pe.wait_ge(l0_loaded, 64)
            for b in range(NB):
                for k in range(KD):
                    mm = pe.matmul(ps[:, 6, b * E:(b + 1) * E], xa[:, k, b * T:(b + 1) * T], wr[:, k],
                                   start=k == 0, stop=k == KD - 1)
            mm.then_inc(logits_ready, 1)
            for hf in range(2):
                for k in range(KD):
                    mm = pe.matmul(ps[:, hf], a0[:, k], xa[:, k, hf * HALF:(hf + 1) * HALF],
                                   start=k == 0, stop=k == KD - 1)
                mm.then_inc(h0_ready, 1)
            pe.wait_ge(gates_ready, 1)
            pe.wait_ge(consts_ready, 1)
            for hf in range(2):
                for b in range(4 * hf, 4 * hf + 4):
                    mm = pe.transpose(ps[:, 2 + hf, b % 4 * T:(b % 4 + 1) * T], gate_x[:, b], ident[:])
                mm.then_inc(gate_t, 1)
            for hf in range(2):
                pe.wait_ge(h_ready, hf + 1)
                for o in range(KD):
                    n = KD * hf + o
                    wait(pe, x1_ready, n - 1)
                    for k in range(KD):
                        pe.matmul(ps[:, 4 + n % 2], w0[:, k, o * P:(o + 1) * P], xa[:, k, hf * HALF:(hf + 1) * HALF],
                                  start=k == 0, stop=False)
                    pe.matmul(ps[:, 4 + n % 2], b0[:, o * P:(o + 1) * P], h_gated[:, hf * HALF:(hf + 1) * HALF],
                              start=False, stop=True).then_inc(l0_out, 1)

            pe.wait_ge(rows_laid, 3)
            pe.wait_ge(x1_ready, 2 * KD)
            for w, bank in ((a_gate, 4), (a_up, 6)):
                for hf in range(2):
                    for k in range(KD):
                        mm = pe.matmul(ps[:, bank + hf], w[:, k], xb[:, k, hf * HALF:(hf + 1) * HALF],
                                       start=k == 0, stop=k == KD - 1)
                    mm.then_inc(t_full, 1)
            pe.wait_ge(t_ready, 4)

            def gate_up(f, par):
                pe.wait_ge(gu_loaded[par], 16 * (f // 2 + 1))
                pe.wait_ge(slice_ready, f + 1)
                for hf in range(2):
                    wait(pe, act_ready, 2 * f + hf - 1)
                    for g, t, done in ((0, t_gate, gate_done), (1, t_up, up_done)):
                        for k in range(KD):
                            pe.matmul(ps[:, 2 * g + hf], w_gu[par][:, g, k], xb[:, k, hf * HALF:(hf + 1) * HALF],
                                      start=k == 0, stop=False)
                        pe.matmul(ps[:, 2 * g + hf], b_now[par][:, g], t[:, hf * HALF:(hf + 1) * HALF],
                                  start=False, stop=True).then_inc(done, 1)

            over_hidden(pe, gate_up)
            pe.wait_ge(act_ready, 2 * FT)
            for hf in range(2):
                for f in range(FT):
                    mm = pe.matmul(ps[:, 4 + hf], a_down[:, f], act[:, f, hf * HALF:(hf + 1) * HALF],
                                   start=f == 0, stop=f == FT - 1)
                mm.then_inc(td_full, 1)
            for o in range(KD):
                pe.wait_ge(down_loaded[o % 2], 16 * (o // 2 + 1))
                for hf in range(2):
                    n = 2 * o + hf
                    wait(pe, x2_ready, n - 3)
                    for f in range(FT):
                        pe.matmul(ps[:, n % 4], w_down[o % 2][:, f], act[:, f, hf * HALF:(hf + 1) * HALF],
                                  start=f == 0, stop=False)
                    pe.wait_ge(td_ready, hf + 1)
                    pe.matmul(ps[:, n % 4], b_down[:, o * P:(o + 1) * P], t_down[:, hf * HALF:(hf + 1) * HALF],
                              start=False, stop=True).then_inc(l1_out, 1)

            pe.wait_ge(x2_ready, 2 * KD)

            def adapter(b, par):
                pe.wait_ge(w2_loaded[par], 16 * (b // 2 + 1))
                wait(pe, x3_summed, b - 1)
                for o in range(KD):
                    for k in range(KD):
                        mm = pe.matmul(ps[:, 4 + par, o * T:(o + 1) * T], w2[par][:, k, o * P:(o + 1) * P],
                                       xa[:, k, ds(b * T, T)], start=k == 0, stop=k == KD - 1)
                mm.then_inc(l2_out, 1)

            def turn_x(b, par):
                pe.wait_ge(x3_summed, b + 1)
                wait(pe, acc_ready, b - 1)
                for k in range(KD):
                    mm = pe.transpose(ps[:, 6 + par, k * P:(k + 1) * P], x_sum[par][:, k], ident[:])
                mm.then_inc(x3_turned, 1)

            def layer2(b, par):
                adapter(b, par)
                turn_x(b, par)

            over_batches(pe, layer2)

            pe.wait_ge(acc_ready, NB)

            def project_kv(m, par):
                blk = m // NB
                pe.wait_ge(w3_loaded, 48 * (blk + 1))
                pe.wait_ge(x_now_ready, m + 1)
                wait(pe, out_added, 2 * m - 2)
                wait(pe, q_taken, 2 * m)
                for k in range(KD):
                    mm = pe.matmul(ps[:, PJ], x_now[par][:, k], w_block("wkv", blk)[:, k, :], start=k == 0, stop=k == KD - 1)
                mm.then_inc(kv_projected, 1)

            def w_block(name, blk):
                return w3_set(name, ds(blk % 2, 1) if not isinstance(blk, int) else blk % 2)

            def project_q(m, par, s):
                if s == 0:
                    pe.wait_ge(k_raw_ready, m + 1)
                    pe.wait_ge(v_taken, m + 1)
                else:
                    wait(pe, out_added, 2 * m - 1)
                    pe.wait_ge(q_taken, 2 * m + 1)
                for k in range(KD):
                    mm = pe.matmul(ps[:, PJ], x_now[par][:, k],
                                   w_block("wq", m // NB)[:, k, s * REP * DH:(s + 1) * REP * DH],
                                   start=k == 0, stop=k == KD - 1)
                mm.then_inc(q_projected, 1)

            def turn_k(m):
                pe.wait_ge(q_raw_ready, 2 * m + 1)
                pe.wait_ge(k_roped, m + 1)
                for s in range(HB):
                    mm = pe.transpose(ps[:, PJ, s * T:(s + 1) * T], k_rot[:, s], ident[:])
                mm.then_inc(k_turned, 1)

            def turn_q(m, s):
                if s == 0:
                    pe.wait_ge(k_taken, m + 1)
                pe.wait_ge(q_raw_ready, 2 * m + s + 1)
                pe.wait_ge(q_roped, 2 * m + s + 1)
                for h in range(REP):
                    mm = pe.transpose(ps[:, PJ, h * T:(h + 1) * T], q_rot[:, h], ident[:])
                mm.then_inc(q_turned, 1)

            def score(j, m, par, s, h):
                if h == 0:
                    pe.wait_ge(q_taken, j + 1)
                    if s == 0:
                        pe.wait_ge(k_loaded[par], 16 * NPAGE * (m // 2 + 1))
                wait(pe, exp_done, 4 * j + h - 1)
                slot = h % 2
                pe.matmul(s_ps[:, slot, 0:CACHED], q_t[s][:, h], kc[par][:, :, s, :], start=True, stop=True)
                pe.matmul(s_ps[:, slot, CACHED:KEYS], q_t[s][:, h], k_new[par][:, s], start=True, stop=True
                          ).then_inc(scored, 1)

            def turn_probs(i, s, t):
                if t == 0:
                    pe.wait_ge(prob_ready, 4 * i + 4)
                wait(pe, *((pt_dve, 2 * i), (pt_act, 3 * i), (pt_act, 3 * i + 1), (pt_dve, 2 * i + 1), (pt_act, 3 * i + 2))[t])
                for h in range(REP):
                    mm = pe.transpose(ps[:, PT[(s + t) % 2], h * T:(h + 1) * T], prob[s][:, h, t * P:(t + 1) * P], ident[:])
                mm.then_inc(pt_full, 1)

            def weigh(i, par, s, t):
                if t == 0:
                    wait(pe, o_taken, i)
                    if s == 0:
                        pe.wait_ge(v_loaded[par], 16 * NPAGE * (i // 2 // 2 + 1))
                if t % 2 == 0:
                    pe.wait_ge(pt_act, 3 * i + t // 2 + 1)
                else:
                    pe.wait_ge(pt_dve, 2 * i + (t + 1) // 2)
                v = vc[par][:, t, s * DH:(s + 1) * DH] if t < KT - 1 else v_new[par][:, s]
                pe.matmul(ps[:, OB], v, prob_t[t][:], start=t == 0, stop=t == KT - 1).then_inc(pv_done, 1)

            def project_out(i, blk, s, before, value):
                pe.wait_ge(o_taken, i + 1)
                pe.wait_ge(before, value)
                for h in range(REP):
                    mm = pe.matmul(ps[:, PJ], o_t[s][:, h], w_block("wo", blk)[:, s * REP + h, :],
                                   start=h == 0, stop=h == REP - 1)
                mm.then_inc(out_projected, 1)

            project_kv(0, 0)
            project_q(0, 0, 0)
            turn_k(0)
            turn_q(0, 0)
            project_q(0, 0, 1)
            turn_q(0, 1)
            for h in range(REP):
                score(0, 0, 0, 0, h)

            def step(n, par, last):
                i, j, m = 2 * n, 2 * n + 1, n + 1
                score(j, n, par, 1, 0)
                if not (isinstance(n, int) and n == 0):
                    project_out(i - 1, (n - 1) // NB, 1, q_taken, 2 * n + 2)
                turn_probs(i, 0, 0)
                turn_probs(i, 0, 1)
                if not last:
                    project_kv(m, 1 - par)
                weigh(i, par, 0, 0)
                score(j, n, par, 1, 1)
                turn_probs(i, 0, 2)
                if not last:
                    project_q(m, 1 - par, 0)
                weigh(i, par, 0, 1)
                turn_probs(i, 0, 3)
                score(j, n, par, 1, 2)
                weigh(i, par, 0, 2)
                turn_probs(i, 0, 4)
                if not last:
                    turn_k(m)
                weigh(i, par, 0, 3)
                if not last:
                    turn_q(m, 0)
                score(j, n, par, 1, 3)
                weigh(i, par, 0, 4)
                if not last:
                    score(j + 1, m, 1 - par, 0, 0)
                    project_out(i, n // NB, 0, q_taken, 2 * n + 3)
                else:
                    project_out(i, n // NB, 0, out_added, 2 * n)
                turn_probs(i + 1, 1, 0)
                turn_probs(i + 1, 1, 1)
                if not last:
                    project_q(m, 1 - par, 1)
                weigh(i + 1, par, 1, 0)
                if not last:
                    score(j + 1, m, 1 - par, 0, 1)
                turn_probs(i + 1, 1, 2)
                weigh(i + 1, par, 1, 1)
                turn_probs(i + 1, 1, 3)
                if not last:
                    score(j + 1, m, 1 - par, 0, 2)
                weigh(i + 1, par, 1, 2)
                turn_probs(i + 1, 1, 4)
                weigh(i + 1, par, 1, 3)
                if not last:
                    turn_q(m, 1)
                    score(j + 1, m, 1 - par, 0, 3)
                weigh(i + 1, par, 1, 4)

            over_steps(pe, step)
            project_out(GROUPS - 1, BLOCKS - 1, 1, out_added, GROUPS - 1)

        @block.scalar
        def _(act_e):
            for i in range(2):
                act_e.wait_ge(angle_ready, i + 1)
                act_e.activation(trig[:, i], red[:], ACT.Sin).then_inc(sin_ready, 1)
            for hf in range(2):
                act_e.wait_ge(h0_ready, hf + 1)
                act_e.copy(h_sb[:, hf * HALF:(hf + 1) * HALF], ps[:, hf]).then_inc(h0_copied, 1)
            act_e.wait_ge(gap_ready, 1)
            act_e.activation(e_gap[:], gap[:], ACT.Exp).then_inc(gap_exp, 1)

            def exp_gate(f, par):
                for hf in range(2):
                    u = 2 * f + hf
                    act_e.wait_ge(gate_done, u + 1)
                    wait(act_e, act_ready, u - 1)
                    act_e.activation(sil[hf][:], ps[:, hf], ACT.Exp, scale=-1.0).then_inc(exp_g, 1)

            over_hidden(act_e, exp_gate)

            def keep_x(b, par):
                act_e.wait_ge(x3_summed, b + 1)
                act_e.copy(xb[:, :, ds(b * T, T)], x_sum[par][:]).then_inc(x3_copied, 1)
                act_e.wait_ge(x3_turned, b + 1)
                act_e.copy(acc[:, ds(b, 1), :].rearrange("p o n -> p (o n)"), ps[:, 6 + par]).then_inc(acc_ready, 1)

            over_batches(act_e, keep_x)

            def square(done, src, heads, dst):
                for h in range(heads):
                    wait(act_e, squared, done + h - 1)
                    act_e.activation(junk[:, h % 2], src[:, h], ACT.Square, accum_out=dst[:, h:h + 1]).then_inc(squared, 1)

            def take_kv(m, par):
                act_e.wait_ge(kv_projected, m + 1)
                wait(act_e, pv_done, 2 * KT * (m - 1))
                act_e.copy(v_new[par][:], ps[:, PJ, HB * DH:2 * HB * DH]).then_inc(v_taken, 1)
                wait(act_e, k_read, m)
                act_e.copy(k_raw[:], ps[:, PJ, 0:HB * DH]).then_inc(k_raw_ready, 1)
                act_e.wait_ge(k_raw_ready, m + 1)
                square(10 * m, k_raw, HB, ss_k[:])

            def take_raw_q(m, s):
                act_e.wait_ge(q_projected, 2 * m + s + 1)
                wait(act_e, q_roped, 2 * m + s)
                act_e.copy(q_raw[:], ps[:, PJ]).then_inc(q_raw_ready, 1)

            def square_q(m, s):
                act_e.wait_ge(q_raw_ready, 2 * m + s + 1)
                square(10 * m + 2 + 4 * s, q_raw, REP, ss_q[:, s])

            def take_k(m, par):
                act_e.wait_ge(k_turned, m + 1)
                wait(act_e, scored, 8 * m - 8)
                act_e.copy(k_new[par][:], ps[:, PJ, 0:HB * T]).then_inc(k_taken, 1)

            def take_q(m, s):
                act_e.wait_ge(q_turned, 2 * m + s + 1)
                wait(act_e, scored, 8 * m + 4 * s - 4)
                act_e.copy(q_t[s][:], ps[:, PJ]).then_inc(q_taken, 1)

            def exp_scores(j, s, h):
                act_e.wait_ge(masked, 4 * j + h + 1)
                if h == 0:
                    wait(act_e, pt_full, KT * (j - 1))
                act_e.activation(prob[s][:, h], s_ps[:, h % 2, 0:KEYS], ACT.Exp, bias=negmax[:, s, h:h + 1], scale=-1.0,
                                 accum_out=den[:, s, h:h + 1]).then_inc(exp_done, 1)

            def copy_probs(i, s, t):
                act_e.wait_ge(pt_full, KT * i + t + 1)
                wait(act_e, pv_done, KT * (i - 1) + t + 1)
                act_e.copy(prob_t[t][:], ps[:, PT[(s + t) % 2]]).then_inc(pt_act, 1)

            take_kv(0, 0)
            take_raw_q(0, 0)
            square_q(0, 0)
            take_k(0, 0)
            take_q(0, 0)
            take_raw_q(0, 1)
            square_q(0, 1)
            take_q(0, 1)
            for h in range(REP):
                exp_scores(0, 0, h)

            def step(n, par, last):
                i, j, m = 2 * n, 2 * n + 1, n + 1
                exp_scores(j, 1, 0)
                copy_probs(i, 0, 0)
                if not last:
                    take_kv(m, 1 - par)
                exp_scores(j, 1, 1)
                copy_probs(i, 0, 2)
                if not last:
                    take_raw_q(m, 0)
                    square_q(m, 0)
                exp_scores(j, 1, 2)
                copy_probs(i, 0, 4)
                if not last:
                    take_k(m, 1 - par)
                    take_q(m, 0)
                exp_scores(j, 1, 3)
                if not last:
                    exp_scores(j + 1, 0, 0)
                copy_probs(i + 1, 1, 0)
                if not last:
                    take_raw_q(m, 1)
                    exp_scores(j + 1, 0, 1)
                    square_q(m, 1)
                copy_probs(i + 1, 1, 2)
                if not last:
                    exp_scores(j + 1, 0, 2)
                copy_probs(i + 1, 1, 4)
                if not last:
                    take_q(m, 1)
                    exp_scores(j + 1, 0, 3)

            over_steps(act_e, step)

        @block.vector
        def _(dve):
            count = [0]

            def link(ins):
                count[0] += 1
                ins.then_inc(dve_step, 1)
                dve.wait_ge(dve_step, count[0])

            def bc(x, n):
                return x.unsqueeze(2).to_broadcast([P, NB, n])

            dve.wait_ge(ids_loaded, 80)
            dve.wait_ge(consts_ready, 1)
            dve.tensor_copy(len_f[:], len_i[:])
            link(dve.tensor_copy(lang_f[:], lang_i[:]))
            link(dve.tensor_tensor(pos[:], pos[:], len_f[:], ALU.add))
            link(dve.tensor_tensor(ang[:], bc(pos[:], DH // 2), inv_f[:].unsqueeze(1).to_broadcast([P, NB, DH // 2]), ALU.mult))
            for i, (shift, quarter) in enumerate(((0.0, 0.0), (0.25, math.pi / 2))):
                link(dve.tensor_scalar(turns[:], ang[:], 1.0 / TWO_PI, shift, ALU.mult, ALU.add))
                link(dve.tensor_scalar(turns[:], turns[:], ROUND, -ROUND, ALU.add, ALU.add))
                if i == 1:
                    dve.wait_ge(sin_ready, 1)
                link(dve.scalar_tensor_tensor(out=red[:], in0=turns[:], scalar=-PI_A, in1=ang[:], op0=ALU.mult, op1=ALU.add))
                link(dve.scalar_tensor_tensor(out=red[:], in0=turns[:], scalar=-PI_B, in1=red[:], op0=ALU.mult, op1=ALU.add))
                link(dve.scalar_tensor_tensor(out=red[:], in0=turns[:], scalar=-PI_C, in1=red[:], op0=ALU.mult, op1=ALU.add))
                if i == 1:
                    link(dve.tensor_scalar(red[:], red[:], quarter, None, ALU.add))
                link(dve.tensor_scalar(red[:], red[:], 3.1415925, -3.1415925, ALU.min, ALU.max))
                dve.tensor_scalar(turns[:], turns[:], 0.0, None, ALU.mult).then_inc(angle_ready, 1)
                dve.wait_ge(angle_ready, i + 1)
            dve.wait_ge(sin_ready, 2)
            for w, (ct, st) in enumerate(((cos_q, sin_q), (cos_k, sin_k))):
                lo, hi = (norm_w[:, w, n * 64:(n + 1) * 64].unsqueeze(1).to_broadcast([P, NB, 64]) for n in range(2))
                dve.tensor_tensor(ct[:, :, 0:64], trig[:, 1], lo, ALU.mult)
                dve.tensor_tensor(ct[:, :, 64:128], trig[:, 1], hi, ALU.mult)
                dve.tensor_tensor(st[:, :, 0:64], trig[:, 0], lo, ALU.mult)
                dve.scalar_tensor_tensor(out=st[:, :, 64:128], in0=trig[:, 0], scalar=-1.0, in1=hi,
                                         op0=ALU.mult, op1=ALU.mult).then_inc(tables_ready, 1)

            link(dve.tensor_tensor(one1[:], lang[:], bc(lang_f[:], E), ALU.is_equal))
            dve.wait_ge(logits_ready, 1)
            link(dve.scalar_tensor_tensor(out=logit[:], in0=one1[:], scalar=5.0,
                                          in1=ps[:, 6, 0:NB * E].rearrange("p (b e) -> p b e", e=E),
                                          op0=ALU.mult, op1=ALU.add))
            for src, top, one in ((logit, top1, one1), (less, top2, one2)):
                link(dve.tensor_reduce(top[:], src[:], AX.X, ALU.max))
                link(dve.tensor_tensor(one[:], src[:], bc(top[:], E), ALU.is_equal))
                link(dve.scalar_tensor_tensor(out=cand[:], in0=one[:], scalar=-16.0, in1=lang[:], op0=ALU.mult, op1=ALU.add))
                link(dve.tensor_reduce(pick[:], cand[:], AX.X, ALU.min))
                link(dve.tensor_tensor(one[:], cand[:], bc(pick[:], E), ALU.is_equal))
                if one is one1:
                    link(dve.scalar_tensor_tensor(out=less[:], in0=one1[:], scalar=-3e38, in1=logit[:],
                                                  op0=ALU.mult, op1=ALU.add))
            dve.tensor_tensor(gap[:], top2[:], top1[:], ALU.subtract).then_inc(gap_ready, 1)
            dve.wait_ge(gap_exp, 1)
            link(dve.tensor_scalar(g2[:], e_gap[:], 1.0, None, ALU.add))
            link(dve.reciprocal(g1[:], g2[:]))
            link(dve.tensor_tensor(g2[:], e_gap[:], g1[:], ALU.mult))
            dve.tensor_tensor(one1[:], one1[:], bc(g1[:], E), ALU.mult)
            link(dve.tensor_tensor(one2[:], one2[:], bc(g2[:], E), ALU.mult))
            link(dve.tensor_tensor(gates[:], one1[:], one2[:], ALU.add))
            dve.tensor_scalar(gate_x[:].rearrange("p b (e r) -> p b e r", r=R),
                              gates[:].unsqueeze(3).to_broadcast([P, NB, E, R]), 2.0, None, ALU.mult
                              ).then_inc(gates_ready, 1)
            for hf in range(2):
                dve.wait_ge(h0_copied, hf + 1)
                dve.wait_ge(gate_t, hf + 1)
                dve.tensor_tensor(h_gated[:, hf * HALF:(hf + 1) * HALF], h_sb[:, hf * HALF:(hf + 1) * HALF],
                                  ps[:, 2 + hf], ALU.mult).then_inc(h_ready, 1)
            for hf in range(2):
                for o in range(KD):
                    n = KD * hf + o
                    dve.wait_ge(l0_out, n + 1)
                    half = slice(hf * HALF, (hf + 1) * HALF)
                    dve.tensor_tensor(xb[:, o, half], xa[:, o, half], ps[:, 4 + n % 2], ALU.add).then_inc(x1_ready, 1)

            def own_rows(dst, bank, hf, done):
                dve.tensor_tensor(dst[:, hf * HALF:(hf + 1) * HALF].rearrange("p (b t) -> p b t", t=T),
                                  ps[:, bank].rearrange("p (b t) -> p b t", t=T),
                                  own[:, 4 * hf:4 * hf + 4].unsqueeze(2).to_broadcast([P, 4, T]), ALU.mult
                                  ).then_inc(done, 1)

            for n, (dst, bank) in enumerate(((t_gate, 4), (t_up, 6))):
                for hf in range(2):
                    dve.wait_ge(t_full, 2 * n + hf + 1)
                    own_rows(dst, bank + hf, hf, t_ready)

            def gated(f, par):
                for hf in range(2):
                    u = 2 * f + hf
                    dve.wait_ge(exp_g, u + 1)
                    dve.tensor_scalar(sil[hf][:], sil[hf][:], 1.0, None, ALU.add).then_inc(silu_step, 1)
                    dve.wait_ge(silu_step, 3 * u + 1)
                    dve.reciprocal(sil[hf][:], sil[hf][:]).then_inc(silu_step, 1)
                    dve.wait_ge(silu_step, 3 * u + 2)
                    dve.tensor_tensor(sil[hf][:], ps[:, hf], sil[hf][:], ALU.mult).then_inc(silu_step, 1)
                    dve.wait_ge(silu_step, 3 * u + 3)
                    dve.wait_ge(up_done, u + 1)
                    dve.tensor_tensor(act[:, ds(f, 1), hf * HALF:(hf + 1) * HALF].rearrange("p o n -> p (o n)"),
                                      ps[:, 2 + hf], sil[hf][:], ALU.mult).then_inc(act_ready, 1)

            over_hidden(dve, gated)
            for hf in range(2):
                dve.wait_ge(td_full, hf + 1)
                own_rows(t_down, 4 + hf, hf, td_ready)
            for o in range(KD):
                for hf in range(2):
                    n = 2 * o + hf
                    dve.wait_ge(l1_out, n + 1)
                    half = slice(hf * HALF, (hf + 1) * HALF)
                    dve.tensor_tensor(xa[:, o, half], xb[:, o, half], ps[:, n % 4], ALU.add).then_inc(x2_ready, 1)

            dve.wait_ge(x2_ready, 2 * KD)

            def add_adapter(b, par):
                dve.wait_ge(l2_out, b + 1)
                wait(dve, x3_turned, b - 1)
                wait(dve, x3_copied, b - 1)
                dve.tensor_tensor(x_sum[par][:], xa[:, :, ds(b * T, T)],
                                  ps[:, 4 + par].rearrange("p (k t) -> p k t", t=T), ALU.add).then_inc(x3_summed, 1)

            over_batches(dve, add_adapter)

            def take_x(m, par):
                wait(dve, q_projected, 2 * m - 2)
                b = m % NB
                dve.tensor_copy(x_now[par][:], xb[:, :, ds(b * T, T)]).then_inc(x_now_ready, 1)
                dve.tensor_scalar(mask[par][:, 0:CACHED], iota[:], len_f[:, ds(b, 1)], NEG, ALU.is_ge, ALU.mult
                                  ).then_inc(mask_ready, 1)

            def rotate_k(m):
                dve.wait_ge(k_raw_ready, m + 1)
                dve.wait_ge(rstd_ready, 3 * m + 1)
                wait(dve, k_roped, m)
                wait(dve, k_turned, m)
                for h in range(HB):
                    for part, table in ((part_ck, cos_k), (part_sk, sin_k)):
                        last = dve.scalar_tensor_tensor(
                            out=part[:, h], in0=k_raw[:, h], scalar=rs_k[:, h:h + 1],
                            in1=table[:, ds(m % NB, 1), :].rearrange("p o d -> p (o d)"), op0=ALU.mult, op1=ALU.mult)
                last.then_inc(k_read, 1)
                dve.wait_ge(k_read, m + 1)
                dve.tensor_tensor(k_rot[:, :, 0:64], part_ck[:, :, 0:64], part_sk[:, :, 64:128], ALU.add)
                dve.tensor_tensor(k_rot[:, :, 64:128], part_ck[:, :, 64:128], part_sk[:, :, 0:64], ALU.add).then_inc(k_roped, 1)

            def rotate_q(m, s):
                dve.wait_ge(q_raw_ready, 2 * m + s + 1)
                wait(dve, q_roped, 2 * m + s)
                wait(dve, q_turned, 2 * m + s)
                dve.tensor_tensor(part_c[:], q_raw[:], cos_q[:, ds(m % NB, 1), :].to_broadcast([P, REP, DH]), ALU.mult
                                  ).then_inc(q_cosine, 1)
                dve.wait_ge(q_cosine, 2 * m + s + 1)
                dve.wait_ge(q_sine, 2 * m + s + 1)
                dve.tensor_tensor(q_rot[:, :, 0:64], part_c[:, :, 0:64], part_s[:, :, 64:128], ALU.add)
                dve.tensor_tensor(q_rot[:, :, 64:128], part_c[:, :, 64:128], part_s[:, :, 0:64], ALU.add).then_inc(q_roped, 1)

            def mask_scores(j, m, par, s, h):
                if h == 0:
                    dve.wait_ge(rstd_ready, 3 * m + 2 + s)
                if h == 0 and s == 0:
                    dve.wait_ge(mask_ready, m + 1)
                dve.wait_ge(scored, 4 * j + h + 1)
                settle(dve, j)
                x = s_ps[:, h % 2, 0:KEYS]
                dve.tensor_tensor_reduce(x, x, mask[par][:], rs_q[:, s, h:h + 1], 3.4e38, ALU.add, ALU.min,
                                         negmax[:, s, h:h + 1]).then_inc(masked, 1)

            def invert_sum(j, s, h):
                dve.wait_ge(exp_done, 4 * j + h + 1)
                dve.reciprocal(rden[:, s, h:h + 1], den[:, s, h:h + 1]).then_inc(rden_ready, 1)

            def copy_probs(i, s, t):
                dve.wait_ge(pt_full, KT * i + t + 1)
                wait(dve, pv_done, KT * (i - 1) + t + 1)
                dve.tensor_copy(prob_t[t][:], ps[:, PT[(s + t) % 2]]).then_inc(pt_dve, 1)

            def take_o(i, s):
                dve.wait_ge(pv_done, KT * (i + 1))
                wait(dve, out_projected, i - 1)
                dve.tensor_copy(o_t[s][:], ps[:, OB]).then_inc(o_taken, 1)

            def add_out(i, b):
                dve.wait_ge(out_projected, i + 1)
                wait(dve, out_added, i)
                to = acc[:, ds(b, 1), :].rearrange("p o n -> p (o n)")
                dve.tensor_tensor(to, ps[:, PJ], to, ALU.add).then_inc(out_added, 1)

            dve.wait_ge(x3_copied, NB)
            dve.wait_ge(acc_ready, NB)
            take_x(0, 0)
            rotate_k(0)
            rotate_q(0, 0)
            rotate_q(0, 1)
            mask_scores(0, 0, 0, 0, 0)
            for h in range(1, REP):
                mask_scores(0, 0, 0, 0, h)
                invert_sum(0, 0, h - 1)
            invert_sum(0, 0, REP - 1)

            def step(n, par, last):
                i, j, m = 2 * n, 2 * n + 1, n + 1
                mask_scores(j, n, par, 1, 0)
                if not last:
                    take_x(m, 1 - par)
                if not (isinstance(n, int) and n == 0):
                    add_out(i - 1, (n - 1) % NB)
                copy_probs(i, 0, 1)
                mask_scores(j, n, par, 1, 1)
                invert_sum(j, 1, 0)
                if not last:
                    rotate_k(m)
                copy_probs(i, 0, 3)
                mask_scores(j, n, par, 1, 2)
                invert_sum(j, 1, 1)
                if not last:
                    rotate_q(m, 0)
                mask_scores(j, n, par, 1, 3)
                invert_sum(j, 1, 2)
                take_o(i, 0)
                if not last:
                    mask_scores(j + 1, m, 1 - par, 0, 0)
                invert_sum(j, 1, 3)
                add_out(i, n % NB)
                copy_probs(i + 1, 1, 1)
                if not last:
                    mask_scores(j + 1, m, 1 - par, 0, 1)
                    invert_sum(j + 1, 0, 0)
                    rotate_q(m, 1)
                copy_probs(i + 1, 1, 3)
                if not last:
                    mask_scores(j + 1, m, 1 - par, 0, 2)
                    invert_sum(j + 1, 0, 1)
                    mask_scores(j + 1, m, 1 - par, 0, 3)
                    invert_sum(j + 1, 0, 2)
                take_o(i + 1, 1)
                if not last:
                    invert_sum(j + 1, 0, 3)

            over_steps(dve, step)
            add_out(GROUPS - 1, NB - 1)


def kernel(**inputs):
    import numpy as np
    import concourse.bacc as bacc
    from concourse.bass_utils import run_bass_kernel_spmd

    g = {n: np.asarray(v) for n, v in inputs.items()}

    def pieces(w):
        return w.T.reshape(KD, P, -1).transpose(1, 0, 2)

    def padded(w, axis):
        widths = [(0, 0)] * w.ndim
        widths[axis] = (0, FP - F)
        return np.pad(w, widths)

    x = g["x"].reshape(NT, D)
    gu = [padded(g[f"L1_cond_W_{n}"], 0).reshape(FT, P, KD, P).transpose(0, 3, 2, 1) for n in ("gate", "up")]
    kvw = [np.stack([pieces(g[f"L3_cond_W{n}"][k * HB * DH:(k + 1) * HB * DH]) for k in range(BLOCKS)]) for n in "kv"]
    arrays = {
        "x": pieces(x),
        "w0": pieces(g["L0_cond_W"]),
        "wr": pieces(g["L0_cond_Wr"]),
        "a0": pieces(g["L0_cond_A"].reshape(E * R, D)),
        "b0": g["L0_cond_B"].transpose(0, 2, 1).reshape(E * R, D),
        "w_gu": np.stack(gu, axis=2),
        "w_down": padded(g["L1_cond_W_down"], 1).reshape(KD, P, FT, P).transpose(0, 3, 2, 1),
        "a_gate": g["L1_cond_A_gate"][0].reshape(-1, R, KD, P).transpose(0, 3, 2, 1),
        "a_up": g["L1_cond_A_up"][0].reshape(-1, R, KD, P).transpose(0, 3, 2, 1),
        "a_down": padded(g["L1_cond_A_down"][0], 2).reshape(-1, R, FT, P).transpose(0, 3, 2, 1),
        "b_gate": padded(g["L1_cond_B_gate"][0], 1).transpose(0, 2, 1),
        "b_up": padded(g["L1_cond_B_up"][0], 1).transpose(0, 2, 1),
        "b_down": g["L1_cond_B_down"][0].transpose(0, 2, 1),
        "w2": g["L2_cond_weight"].reshape(-1, D, KD, P).transpose(0, 3, 2, 1),
        "wq": np.stack([pieces(w) for w in g["L3_cond_Wq"].reshape(BLOCKS, -1, D)]),
        "wkv": np.concatenate(kvw, axis=3),
        "wo": g["L3_cond_Wo"].reshape(D, BLOCKS, HB * REP, DH).transpose(1, 3, 2, 0),
        "k_cache": g["L3_cond_k_cache"].reshape(-1, PAGE, BLOCKS, HB, DH).transpose(0, 2, 4, 3, 1),
        "v_cache": g["L3_cond_v_cache"].reshape(-1, PAGE, BLOCKS, HB * DH).transpose(0, 2, 1, 3),
        "q_norm": g["L3_cond_q_norm_w"],
        "k_norm": g["L3_cond_k_norm_w"],
        "inv_f": np.float32(1.0) / np.power(np.float32(10000.0), np.arange(0, DH, 2, dtype=np.float32) / np.float32(DH)),
        "ids": np.concatenate([g["itok_B_2_6"], g["itok_B_0_15"], g["itok_Bx16_0_63"].reshape(-1)])[None],
        "lens": g["itok_B_207_1644"],
        "lang": g["itok_B_0_7"],
    }
    nc = bacc.Bacc("TRN2", target_bir_lowering=False, num_devices=1)
    feed, aps = {}, {}
    for name, v in arrays.items():
        v = np.ascontiguousarray(v)
        feed[f"in_{name}"] = v
        aps[name] = nc.dram_tensor(f"in_{name}", v.shape, mybir.dt.from_np(v.dtype), kind="ExternalInput").ap()
    o = nc.dram_tensor("result", (NB, T, D), F32, kind="ExternalOutput").ap()
    build(nc, aps, o.rearrange("b t n -> t b n"))
    r = run_bass_kernel_spmd(nc, [feed], core_ids=[0])
    return r.results[0]["result"]
```

```python
import math
from contextlib import ExitStack

import concourse.bass as bass
from concourse import mybir

ALU = mybir.AluOpType
ACT = mybir.ActivationFunctionType
AX = mybir.AxisListType
F32 = mybir.dt.float32
F32R = mybir.dt.float32r
F16 = mybir.dt.float16
BF16 = mybir.dt.bfloat16
I32 = mybir.dt.int32

P = 128
NB, T, D = 8, 128, 512
NT = NB * T
HALF = NT // 2
KD = D // P
E, R = 8, 16
F = 1376
FT = -(-F // P)
FP = FT * P
HK, REP, DH = 8, 4, 128
PAGE, NPAGE = 32, 16
CACHED = PAGE * NPAGE
KEYS = CACHED + T
KT = KEYS // P
HB = 2
BLOCKS = HK // HB
STEPS = BLOCKS * NB
GROUPS = STEPS * HB
SCALE = 1.0 / math.sqrt(DH)
EPS = 1e-6
TWO_PI = 2 * math.pi
PI_A = 6.28125
PI_B = 0.0019350051879882812
PI_C = TWO_PI - PI_A - PI_B
ROUND = 12582912.0
NEG = -1e30


def build(nc, a, out, x3_dram, turn_dram):
    ds = bass.ds
    base = 16512
    KB = 1024

    class Region:
        def __init__(self, start, size):
            self.at, self.end = start, start + size

        def take(self, name, shape, dt=F32):
            size = 2 if dt in (F16, BF16) else 4
            for n in shape[1:]:
                size *= n
            t = nc.alloc_sbuf_tensor_at(name, shape, dt, offset=self.at)
            self.at += -(-size // 32) * 32
            assert self.at <= self.end, name
            return t

    at = [base]

    def region(size):
        at[0] += size
        return at[0] - size

    r_xa, r_xb, r_acc, r_rope, r_kv = (region(16 * KB) for _ in range(5))
    r_w = region(80 * KB)
    r_arena = region(38 * KB + 512)
    r_small = region(nc.sbuf_usable_end - at[0] - 32)

    xa = Region(r_xa, 16 * KB).take("x_even", [P, KD, NT])
    xb = Region(r_xb, 16 * KB).take("x_odd", [P, KD, NT])
    acc = Region(r_acc, 16 * KB).take("acc", [P, NB, D])
    rope = Region(r_rope, 16 * KB)
    tables = [rope.take(n, [P, NB, DH]) for n in ("all_cos_q", "all_sin_q", "all_cos_k", "all_sin_k")]
    kv = Region(r_kv, 16 * KB)
    kc = [kv.take(f"kc{i}", [P, NPAGE, HB, PAGE]) for i in range(2)]
    vc = [kv.take(f"vc{i}", [P, CACHED // P, HB * DH]) for i in (1, 0)][::-1]
    w3 = Region(r_w, 80 * KB)
    W3 = {"wq": (KD, HB * REP * DH), "wkv": (KD, 2 * HB * DH), "wo": (HB * REP, D)}
    w3_at, set_size = {}, 0
    for name, (rows, cols) in W3.items():
        w3_at[name] = set_size
        set_size += rows * cols
    w3_all = w3.take("w3_all", [P, 2, set_size])
    r_w1 = r_w + 4 * set_size

    def w3_set(name, which):
        rows, cols = W3[name]
        one = w3_all[:, which, w3_at[name]:w3_at[name] + rows * cols]
        if len(one.shape) == 3:
            one = one.rearrange("p o n -> p (o n)")
        return one.rearrange("p (k n) -> p k n", n=cols)

    small = Region(r_small, nc.sbuf_usable_end - r_small)
    ident = small.take("ident", [P, P])
    iota = small.take("iota", [P, CACHED], F16)
    mask = [small.take(f"mask{i}", [P, KEYS], BF16) for i in range(2)]
    len_i = small.take("len_i", [P, NB], I32)
    len_f = small.take("len_f", [P, NB])
    lang_i = small.take("lang_i", [P, NB], I32)
    lang_f = small.take("lang_f", [P, NB])
    ids = small.take("ids", [1, 2 * NB + NB * NPAGE], I32)
    own = small.take("own", [P, NB])
    neghalf = small.take("neghalf", [P, REP])
    negmax = small.take("negmax", [P, HB, REP])
    den = small.take("den", [P, HB, REP])
    rden = small.take("rden", [P, HB, REP])
    ss_k = small.take("ss_k", [P, HB])
    ss_q = small.take("ss_q", [P, HB, REP])
    ms = small.take("ms", [P, REP])
    rs_k = small.take("rs_k", [P, HB])
    rs_q = small.take("rs_q", [P, HB, REP])
    part_ck = small.take("part_ck", [P, HB, DH])
    k_raw = small.take("k_raw", [P, HB, DH])
    q_raw = small.take("q_raw", [P, REP, DH])

    ar = Region(r_arena, 38 * KB + 512)
    prob = [ar.take(f"prob{i}", [P, REP, KEYS]) for i in range(2)]
    o_t = [ar.take(f"o_t{i}", [P, REP, T]) for i in range(2)]
    q_t = [ar.take(f"q_t{i}", [P, REP, T]) for i in range(2)]
    k_new = [ar.take(f"k_new{i}", [P, HB, T]) for i in range(2)]
    x_now = [ar.take(f"x_now{i}", [P, KD, T]) for i in range(2)]
    k_rot = ar.take("k_rot", [P, HB, DH])
    junk = ar.take("junk", [P, 2, DH], BF16)
    part_sk = ar.take("part_sk", [P, HB, DH])
    ov = Region(r_xa, 16 * KB)
    pt_h, pt_l = ([ov.take(f"pt_{n}{i}", [P, REP * T], F32R) for i in range(2)] for n in "hl")
    part_c = ov.take("part_c", [P, REP, DH])
    part_s = ov.take("part_s", [P, REP, DH])
    q_rot = ov.take("q_rot", [P, REP, DH])

    ov = Region(r_rope, 16 * KB)
    turn = [ov.take(f"turn{i}", [P, 4, DH]) for i in range(2)]
    q_h, q_l = ([ov.take(f"q_{n}{i}", [P, REP, T], F32R) for i in range(2)] for n in "hl")
    vn_h, vn_l = ([ov.take(f"vn_{n}{i}", [P, HB, DH], F32R) for i in range(2)] for n in "hl")
    ov = Region(r_xb, 16 * KB)
    k_h, k_l = ([ov.take(f"k_{n}{i}", [P, NPAGE, PAGE], F32R) for i in range(2)] for n in "hl")
    v_h, v_l = ([ov.take(f"v_{n}{i}", [P, CACHED // P, DH], F32R) for i in range(2)] for n in "hl")

    z = Region(r_w1, 44 * KB)
    w0 = z.take("w0", [P, KD, D])
    wr = z.take("wr", [P, KD, E])
    a0 = z.take("a0", [P, KD, E * R])
    b0 = z.take("b0", [P, D])
    gate_x = z.take("gate_x", [P, NB, E * R])
    h_sb = z.take("h_sb", [P, NT])
    h_gated = z.take("h_gated", [P, NT])
    ang, turns, red = (z.take(n, [P, NB, DH // 2]) for n in ("ang", "turns", "red"))
    trig = z.take("trig", [P, 2, NB, DH // 2])
    norm_w = z.take("norm_w", [P, 2, DH])
    inv_f = z.take("inv_f", [P, DH // 2])
    pos = z.take("pos", [P, NB])
    logit, cand, one1, one2, less, gates, lang = (
        z.take(n, [P, NB, E]) for n in ("logit", "cand", "one1", "one2", "less", "gates", "lang"))
    top1, top2, pick, gap, e_gap, g1, g2 = (
        z.take(n, [P, NB]) for n in ("top1", "top2", "pick", "gap", "e_gap", "g1", "g2"))
    act = Region(r_w1, 44 * KB).take("act", [P, FT, NT])
    y = Region(r_arena + 4 * KB, 34 * KB)
    w_gu = [y.take(f"w_gu{i}", [P, 2, KD, P]) for i in range(2)]
    t_gate, t_up = y.take("t_gate", [P, NT]), y.take("t_up", [P, NT])
    sil = [y.take(f"sil{i}", [P, HALF]) for i in range(2)]
    a_up, b_up = y.take("a_up", [P, KD, NB * R]), y.take("b_up", [P, FP])
    b_now = [y.take(f"b_now{i}", [P, 2, P]) for i in range(2)]
    y = Region(r_acc, 16 * KB)
    a_down, b_gate = y.take("a_down", [P, FT, NB * R]), y.take("b_gate", [P, FP])
    b_down, a_gate = y.take("b_down", [P, D]), y.take("a_gate", [P, KD, NB * R])
    y = Region(r_kv, 16 * KB)
    w_down = [y.take(f"w_down{i}", [P, FT, P]) for i in range(2)]
    y = Region(r_kv, 16 * KB)
    a_raw = {n: y.take(f"{n}_raw", [P, NB, k, R]) for n, k in (("a_gate", KD), ("a_up", KD), ("a_down", FT))}
    t_down = Region(r_arena + 12 * KB, 4 * KB).take("t_down", [P, NT])
    w2 = [Region(r_arena + 4 * KB, 8 * KB).take("w2_0", [P, KD, D]),
          Region(r_arena + 16 * KB, 8 * KB).take("w2_1", [P, KD, D])]
    y = Region(r_arena + 24 * KB, 4 * KB)
    x_sum = [y.take(f"x_sum{i}", [P, KD, T]) for i in range(2)]

    with ExitStack() as ctx:
        ps = ctx.enter_context(nc.psum_tensor("ps", [P, 8, 512], F32))
        s_ps = ps[:, 0:4, :].rearrange("p (s b) n -> p s (b n)", s=2)
        PT, OB, PJ = (4, 5), 6, 7

        def sem(name):
            return ctx.enter_context(nc.semaphore(name))

        x_loaded = [sem(f"x_loaded{i}") for i in range(2)]
        l0_small_loaded, l0_loaded, ids_loaded, rows_loaded = sem("l0_small_loaded"), sem("l0_loaded"), sem("ids_loaded"), sem("rows_loaded")
        lora_loaded = sem("lora_loaded")
        gu_loaded = [sem(f"gu_loaded{i}") for i in range(2)]
        down_loaded = [sem(f"down_loaded{i}") for i in range(2)]
        w2_loaded = [sem(f"w2_loaded{i}") for i in range(2)]
        w3_loaded = sem("w3_loaded")
        k_loaded, v_loaded = ([sem(f"{n}_loaded{i}") for i in range(2)] for n in "kv")
        stored, passed = sem("stored"), sem("passed")
        pool_step, dve_step, act_step = sem("pool_step"), sem("dve_step"), sem("act_step")
        consts_ready, sin_ready, angle_ready, tables_ready = sem("consts_ready"), sem("sin_ready"), sem("angle_ready"), sem("tables_ready")
        logits_ready, gap_ready, gap_exp, gates_ready = sem("logits_ready"), sem("gap_ready"), sem("gap_exp"), sem("gates_ready")
        h0_ready, h0_copied, gate_t, h_ready, l0_out, x1_ready = (
            sem("h0_ready"), sem("h0_copied"), sem("gate_t"), sem("h_ready"), sem("l0_out"), sem("x1_ready"))
        t_full, t_ready, td_full, td_ready = sem("t_full"), sem("t_ready"), sem("td_full"), sem("td_ready")
        rows_laid = sem("rows_laid")
        slice_ready, gate_done, up_done, exp_g, silu_step, act_ready = (
            sem("slice_ready"), sem("gate_done"), sem("up_done"), sem("exp_g"), sem("silu_step"), sem("act_ready"))
        l1_out, x2_ready = sem("l1_out"), sem("x2_ready")
        l2_out, x3_summed, x3_turned, acc_ready = (
            sem("l2_out"), sem("x3_summed"), sem("x3_turned"), sem("acc_ready"))
        mask_ready = sem("mask_ready")
        tables_stored = sem("tables_stored")
        x3_stored, step_loaded = ([sem(f"{n}{i}") for i in range(2)] for n in ("x3_stored", "step_loaded"))
        kc_high, kc_low, vc_high, vc_low = sem("kc_high"), sem("kc_low"), sem("vc_high"), sem("vc_low")
        vn_high, vn_low, q_low = sem("vn_high"), sem("vn_low"), sem("q_low")
        kv_projected, q_projected = sem("kv_projected"), sem("q_projected")
        squared, ms_ready, rstd_ready = sem("squared"), sem("ms_ready"), sem("rstd_ready")
        k_raw_ready, q_raw_ready, k_read, k_roped, q_sine, q_roped = sem("k_raw_ready"), sem("q_raw_ready"), sem("k_read"), sem("k_roped"), sem("q_sine"), sem("q_roped")
        q_cosine = sem("q_cosine")
        k_turned, k_taken, q_turned, q_taken = sem("k_turned"), sem("k_taken"), sem("q_turned"), sem("q_taken")
        scored, masked, exp_done, rden_ready, prob_ready = (
            sem("scored"), sem("masked"), sem("exp_done"), sem("rden_ready"), sem("prob_ready"))
        pt_full, pt_high, pt_low, pv_done = sem("pt_full"), sem("pt_high"), sem("pt_low"), sem("pv_done")
        o_taken, out_projected, out_added = sem("o_taken"), sem("out_projected"), sem("out_added")

        def wait(eng, s, v):
            if not (isinstance(v, int) and v <= 0):
                eng.wait_ge(s, v)

        def settle(eng, n):
            if not isinstance(n, int):
                eng.sem_inc(passed)

        def over_steps(eng, step):
            step(0, 0, False)
            step(1, 1, False)
            with eng.Fori(1, STEPS // 2 - 1) as c:
                step(2 * c, 0, False)
                step(2 * c + 1, 1, False)
            step(STEPS - 2, 0, False)
            step(STEPS - 1, 1, True)

        def over_hidden(eng, tile):
            tile(0, 0)
            tile(1, 1)
            with eng.Fori(1, FT // 2) as c:
                tile(2 * c, 0)
                tile(2 * c + 1, 1)
            tile(FT - 1, 0)

        def over_batches(eng, batch):
            batch(0, 0)
            batch(1, 1)
            with eng.Fori(1, NB // 2) as c:
                batch(2 * c, 0)
                batch(2 * c + 1, 1)

        def more(n, ahead):
            return not isinstance(n, int) or n + ahead < STEPS

        def key_tile(t):
            return (t - 1) % KT

        block = ctx.enter_context(nc.Block())

        @block.sync
        def _(sp):
            sp.dma_start(ids[:], a["ids"]).then_inc(rows_loaded, 16)
            for dst, name in ((wr, "wr"), (a0, "a0")):
                sp.dma_start(dst[:], a[name]).then_inc(l0_small_loaded, 16)
            for hf in range(2):
                sp.dma_start(xa[:, :, hf * HALF:(hf + 1) * HALF], a["x"][:, :, hf * HALF:(hf + 1) * HALF]
                             ).then_inc(x_loaded[hf], 16)
            for dst, name in ((w0, "w0"), (b0, "b0")):
                sp.dma_start(dst[:], a[name]).then_inc(l0_loaded, 16)
            sp.wait_ge(rows_loaded, 16)
            for b in range(NB):
                row = sp.value_load(ids[0:1, b:b + 1], min_val=0, max_val=15)
                for name, dst in a_raw.items():
                    sp.dma_start(dst[:, b], a[name][ds(row, 1)].rearrange("o p k r -> (o p) k r")).then_inc(lora_loaded, 16)
                for dst, name in ((b_gate, "b_gate"), (b_up, "b_up"), (b_down, "b_down")):
                    sp.dma_start(dst[b * R:(b + 1) * R, :],
                                 a[name][ds(row, 1)].rearrange("o r f -> (o r) f")).then_inc(lora_loaded, 16)

            def load_gu(f, par):
                wait(sp, up_done, 2 * f - 2)
                sp.dma_start(w_gu[par][:], a["w_gu"][ds(f, 1)].rearrange("o p g k n -> (o p) g k n")
                             ).then_inc(gu_loaded[par], 16)

            def load_w3(k):
                for name in W3:
                    sp.dma_start(w3_set(name, k % 2), a[name][k]).then_inc(w3_loaded, 16)

            load_gu(0, 0)
            load_gu(1, 1)
            load_w3(0)
            with sp.Fori(1, FT // 2) as c:
                load_gu(2 * c, 0)
                load_gu(2 * c + 1, 1)
            load_gu(FT - 1, 0)
            def load_w2(b, par):
                wait(sp, l2_out, b - 1)
                row = sp.value_load(ids[0:1, ds(NB + b, 1)], min_val=0, max_val=15)
                sp.dma_start(w2[par][:], a["w2"][ds(row, 1)].rearrange("o p k n -> (o p) k n")
                             ).then_inc(w2_loaded[par], 16)

            def load_keys(m, par):
                b, k = m % NB, m // NB
                wait(sp, kc_low, 2 * m - 2)
                settle(sp, m)
                for j in range(NPAGE):
                    page = sp.value_load(ids[0:1, ds(2 * NB + b * NPAGE + j, 1)], min_val=0, max_val=63)
                    sp.dma_start(kc[par][:, j], a["k_cache"][ds(page, 1), ds(k, 1)].rearrange("g o d s t -> (g o d) s t")
                                 ).then_inc(k_loaded[par], 16)

            def load_values(m, par):
                b, k = m % NB, m // NB
                wait(sp, vc_low, 2 * m - 2)
                settle(sp, m)
                for j in range(NPAGE):
                    page = sp.value_load(ids[0:1, ds(2 * NB + b * NPAGE + j, 1)], min_val=0, max_val=63)
                    q = j % 4 * PAGE
                    sp.dma_start(vc[par][q:q + PAGE, j // 4], a["v_cache"][ds(page, 1), ds(k, 1)].rearrange(
                        "g o t n -> (g o t) n")).then_inc(v_loaded[par], 16)

            sp.wait_ge(slice_ready, 1)
            for o in range(KD):
                wait(sp, l1_out, 2 * (o - 1))
                sp.dma_start(w_down[o % 2][:], a["w_down"][o]).then_inc(down_loaded[o % 2], 16)
                if o == 1:
                    sp.wait_ge(act_ready, 2 * FT)
                    load_w2(0, 0)
                    load_w2(1, 1)
                    load_values(0, 0)
            sp.wait_ge(l1_out, 2 * (KD - 1))
            load_keys(0, 0)
            with sp.Fori(1, NB // 2) as c:
                load_w2(2 * c, 0)
                load_w2(2 * c + 1, 1)
            sp.wait_ge(l1_out, 2 * KD)

            sp.wait_ge(tables_stored, 64)
            sp.wait_ge(x3_stored[0], 16 * NB // 2)

            def load_step(m, par):
                wait(sp, q_projected, 2 * m - 2)
                settle(sp, m)
                wait(sp, q_roped, 2 * m - 2)
                settle(sp, m)
                b, k = m % NB, m // NB
                sp.dma_start(x_now[par][:], x3_dram[ds(b, 1)].rearrange("o p k t -> (o p) k t")).then_inc(step_loaded[par], 16)
                sp.dma_start(turn[par][:], turn_dram[ds(b, 1)].rearrange("o p f d -> (o p) f d")).then_inc(step_loaded[par], 16)
                if not (isinstance(m, int) and m < 1):
                    load_keys(m, par)
                    load_values(m, par)

            load_step(0, 0)
            sp.wait_ge(x3_stored[1], 16 * NB // 2)
            load_step(1, 1)
            for k in range(1, BLOCKS):
                sp.wait_ge(w3_loaded, 48 * k)
                wait(sp, out_projected, 16 * (k - 1))
                load_w3(k)
                with sp.Fori(4 * (k - 1) + 1, 4 * k + 1 if k < BLOCKS - 1 else STEPS // 2) as c:
                    load_step(2 * c, 0)
                    load_step(2 * c + 1, 1)
            sp.wait_ge(out_added, GROUPS)
            sp.dma_start(out, acc[:]).then_inc(stored, 16)
            sp.wait_ge(stored, 16)

        @block.gpsimd
        def _(pool):
            for dst, name in ((len_i, "lens"), (lang_i, "lang")):
                pool.dma_start(dst[:], a[name].partition_broadcast(P)).then_inc(ids_loaded, 16)
            pool.dma_start(inv_f[:], a["inv_f"].partition_broadcast(P)).then_inc(ids_loaded, 16)
            pool.dma_start(norm_w[:, 0, :], a["q_norm"].partition_broadcast(P)).then_inc(ids_loaded, 16)
            pool.dma_start(norm_w[:, 1, :], a["k_norm"].partition_broadcast(P)).then_inc(ids_loaded, 16)
            pool.iota(iota[:], [[1, CACHED]], base=0, channel_multiplier=0, allow_small_or_imprecise_dtypes=True)
            pool.iota(lang[:], [[0, NB], [1, E]], base=0, channel_multiplier=0, allow_small_or_imprecise_dtypes=True)
            pool.iota(pos[:], [[0, NB]], base=0, channel_multiplier=1, allow_small_or_imprecise_dtypes=True)
            pool.memset(neghalf[:], -0.5)
            for i in range(2):
                pool.memset(mask[i][:, CACHED:KEYS], 0.0)
            pool.memset(own[:], 0.5)
            pool.memset(ident[:], 0.0).then_inc(pool_step, 1)
            pool.wait_ge(pool_step, 1)
            pool.affine_select(out=ident[:], in_=ident[:], compare_op=ALU.not_equal, fill=1.0, base=0,
                               pattern=[[-1, P]], channel_multiplier=1)
            pool.affine_select(out=own[:], in_=own[:], compare_op=ALU.is_ge, fill=0.0, base=0,
                               pattern=[[-R, NB]], channel_multiplier=1).then_inc(pool_step, 1)
            pool.wait_ge(pool_step, 2)
            pool.affine_select(out=own[:], in_=own[:], compare_op=ALU.is_ge, fill=0.0, base=R - 1,
                               pattern=[[R, NB]], channel_multiplier=-1).then_inc(consts_ready, 1)

            def b_slices(f, par):
                wait(pool, up_done, 2 * f - 2)
                pool.tensor_copy(b_now[par][:, 0], b_gate[:, ds(f * P, P)])
                pool.tensor_copy(b_now[par][:, 1], b_up[:, ds(f * P, P)]).then_inc(slice_ready, 1)

            pool.wait_ge(lora_loaded, 16 * 6 * NB)
            for name, dst in (("a_gate", a_gate), ("a_up", a_up), ("a_down", a_down)):
                pool.tensor_scalar(dst[:].rearrange("p k (b r) -> p k b r", r=R),
                                   a_raw[name][:].rearrange("p b k r -> p k b r"),
                                   1.0, 1.0, ALU.mult, ALU.mult).then_inc(rows_laid, 1)
            over_hidden(pool, b_slices)

            def rstd_k(m):
                pool.wait_ge(squared, 10 * m + 2)
                wait(pool, rstd_ready, 3 * m)
                settle(pool, m)
                pool.tensor_scalar(ms[:, 0:HB], ss_k[:], 1.0 / DH, EPS, ALU.mult, ALU.add).then_inc(ms_ready, 1)
                pool.wait_ge(ms_ready, 5 * m + 1)
                pool.tensor_tensor(rs_k[:], ms[:, 0:HB], neghalf[:, 0:HB], ALU.pow).then_inc(rstd_ready, 1)

            def rstd_q(m, s):
                pool.wait_ge(squared, 10 * m + 6 + 4 * s)
                pool.wait_ge(rstd_ready, 3 * m + 1 + s)
                if s == 0 or not isinstance(m, int) or m > 0:
                    wait(pool, masked, 8 * m + 4 * s - 4)
                settle(pool, m)
                pool.tensor_scalar(ms[:], ss_q[:, s], 1.0, DH * EPS, ALU.mult, ALU.add).then_inc(ms_ready, 1)
                pool.wait_ge(ms_ready, 5 * m + 2 + 2 * s)
                pool.tensor_tensor(ms[:], ms[:], neghalf[:], ALU.pow).then_inc(ms_ready, 1)
                pool.wait_ge(ms_ready, 5 * m + 3 + 2 * s)
                settle(pool, m)
                pool.tensor_scalar(rs_q[:, s], ms[:], -1.0, 1.0, ALU.mult, ALU.mult).then_inc(rstd_ready, 1)

            def sine_q(m, par, s):
                pool.wait_ge(q_raw_ready, 2 * m + s + 1)
                wait(pool, q_roped, 2 * m + s)
                settle(pool, m)
                pool.tensor_tensor(part_s[:], q_raw[:], turn[par][:, 1:2, :].to_broadcast([P, REP, DH]), ALU.mult
                                   ).then_inc(q_sine, 1)

            def scale_probs(j, s, h):
                pool.wait_ge(rden_ready, 4 * j + h + 1)
                settle(pool, j)
                pool.tensor_scalar(prob[s][:, h], prob[s][:, h], rden[:, s, h:h + 1], 1.0, ALU.mult, ALU.mult
                                   ).then_inc(prob_ready, 1)

            def low_k(m, par, s):
                pool.wait_ge(kc_high, 2 * m + s + 1)
                wait(pool, scored, 8 * m + 4 * s - 4)
                pool.tensor_tensor(k_l[s][:], kc[par][:, :, s, :], k_h[s][:].bitcast(F32), ALU.subtract).then_inc(kc_low, 1)

            def low_v(m, par, s):
                pool.wait_ge(vc_high, 2 * m + s + 1)
                wait(pool, pv_done, KT * (2 * m + s - 1))
                pool.tensor_tensor(v_l[s][:], vc[par][:, :, s * DH:(s + 1) * DH], v_h[s][:].bitcast(F32), ALU.subtract
                                   ).then_inc(vc_low, 1)

            low_k(0, 0, 0)
            low_k(0, 0, 1)
            rstd_k(0)
            sine_q(0, 0, 0)
            rstd_q(0, 0)
            sine_q(0, 0, 1)
            rstd_q(0, 1)
            low_v(0, 0, 0)
            for h in range(REP - 1):
                scale_probs(0, 0, h)

            def half(j, s, v, k):
                scale_probs(j - 1, 1 - s, REP - 1)
                if v is None:
                    return
                if k and s == 1:
                    rstd_k(k[0])
                scale_probs(j, s, 0)
                low_v(*v)
                if k:
                    low_k(*k)
                    sine_q(*k)
                scale_probs(j, s, 1)
                if k:
                    rstd_q(k[0], k[2])
                scale_probs(j, s, 2)

            def step(n, par, last):
                m, j = n + 1, 2 * n + 1
                half(j, 1, (n, par, 1), (m, 1 - par, 0) if not last else None)
                half(j + 1, 0, (m, 1 - par, 0) if not last else None, (m, 1 - par, 1) if not last else None)

            over_steps(pool, step)

        @block.tensor
        def _(pe):
            pe.wait_ge(l0_small_loaded, 32)
            for hf in range(2):
                pe.wait_ge(x_loaded[hf], 16)
                for b in range(4 * hf, 4 * hf + 4):
                    for k in range(KD):
                        mm = pe.matmul(ps[:, 6, b * E:(b + 1) * E], xa[:, k, b * T:(b + 1) * T], wr[:, k],
                                       start=k == 0, stop=k == KD - 1)
                if hf == 1:
                    mm.then_inc(logits_ready, 1)
                for k in range(KD):
                    mm = pe.matmul(ps[:, hf], a0[:, k], xa[:, k, hf * HALF:(hf + 1) * HALF],
                                   start=k == 0, stop=k == KD - 1)
                mm.then_inc(h0_ready, 1)

            def base(n):
                hf, o = n // KD, n % KD
                wait(pe, x1_ready, n - 1)
                for k in range(KD):
                    pe.matmul(ps[:, 4 + n % 2], w0[:, k, o * P:(o + 1) * P], xa[:, k, hf * HALF:(hf + 1) * HALF],
                              start=k == 0, stop=False)

            def low_rank(n):
                hf, o = n // KD, n % KD
                pe.wait_ge(h_ready, hf + 1)
                pe.matmul(ps[:, 4 + n % 2], b0[:, o * P:(o + 1) * P], h_gated[:, hf * HALF:(hf + 1) * HALF],
                          start=False, stop=True).then_inc(l0_out, 1)

            pe.wait_ge(l0_loaded, 32)
            base(0)
            base(1)
            pe.wait_ge(gates_ready, 1)
            pe.wait_ge(consts_ready, 1)
            for hf in range(2):
                for b in range(4 * hf, 4 * hf + 4):
                    mm = pe.transpose(ps[:, 2 + hf, b % 4 * T:(b % 4 + 1) * T], gate_x[:, b], ident[:])
                mm.then_inc(gate_t, 1)
            low_rank(0)
            low_rank(1)
            for n in range(2, 2 * KD):
                base(n)
                low_rank(n)

            pe.wait_ge(rows_laid, 3)
            pe.wait_ge(x1_ready, 2 * KD)
            for w, bank in ((a_gate, 4), (a_up, 6)):
                for hf in range(2):
                    for k in range(KD):
                        mm = pe.matmul(ps[:, bank + hf], w[:, k], xb[:, k, hf * HALF:(hf + 1) * HALF],
                                       start=k == 0, stop=k == KD - 1)
                    mm.then_inc(t_full, 1)
            pe.wait_ge(t_ready, 4)

            def gate_up(f, par):
                pe.wait_ge(gu_loaded[par], 16 * (f // 2 + 1))
                pe.wait_ge(slice_ready, f + 1)
                for hf in range(2):
                    wait(pe, act_ready, 2 * f + hf - 1)
                    for g, t, done in ((0, t_gate, gate_done), (1, t_up, up_done)):
                        for k in range(KD):
                            pe.matmul(ps[:, 2 * g + hf], w_gu[par][:, g, k], xb[:, k, hf * HALF:(hf + 1) * HALF],
                                      start=k == 0, stop=False)
                        pe.matmul(ps[:, 2 * g + hf], b_now[par][:, g], t[:, hf * HALF:(hf + 1) * HALF],
                                  start=False, stop=True).then_inc(done, 1)

            over_hidden(pe, gate_up)
            pe.wait_ge(act_ready, 2 * FT)
            for hf in range(2):
                for f in range(FT):
                    mm = pe.matmul(ps[:, 4 + hf], a_down[:, f], act[:, f, hf * HALF:(hf + 1) * HALF],
                                   start=f == 0, stop=f == FT - 1)
                mm.then_inc(td_full, 1)
            for o in range(KD):
                pe.wait_ge(down_loaded[o % 2], 16 * (o // 2 + 1))
                for hf in range(2):
                    n = 2 * o + hf
                    wait(pe, x2_ready, n - 3)
                    for f in range(FT):
                        pe.matmul(ps[:, n % 4], w_down[o % 2][:, f], act[:, f, hf * HALF:(hf + 1) * HALF],
                                  start=f == 0, stop=False)
                    pe.wait_ge(td_ready, hf + 1)
                    pe.matmul(ps[:, n % 4], b_down[:, o * P:(o + 1) * P], t_down[:, hf * HALF:(hf + 1) * HALF],
                              start=False, stop=True).then_inc(l1_out, 1)

            pe.wait_ge(x2_ready, 2 * KD)

            def adapter(b, par):
                pe.wait_ge(w2_loaded[par], 16 * (b // 2 + 1))
                wait(pe, x3_summed, b - 1)
                for o in range(KD):
                    for k in range(KD):
                        mm = pe.matmul(ps[:, 4 + par, o * T:(o + 1) * T], w2[par][:, k, o * P:(o + 1) * P],
                                       xa[:, k, ds(b * T, T)], start=k == 0, stop=k == KD - 1)
                mm.then_inc(l2_out, 1)

            def turn_x(b, par):
                pe.wait_ge(x3_summed, b + 1)
                wait(pe, acc_ready, b - 1)
                for k in range(KD):
                    mm = pe.transpose(ps[:, 6 + par, k * P:(k + 1) * P], x_sum[par][:, k], ident[:])
                mm.then_inc(x3_turned, 1)

            def layer2(b, par):
                adapter(b, par)
                turn_x(b, par)

            over_batches(pe, layer2)

            pe.wait_ge(acc_ready, NB)

            def project_kv(m, par):
                blk = m // NB
                pe.wait_ge(w3_loaded, 48 * (blk + 1))
                pe.wait_ge(step_loaded[par], 32 * (m // 2 + 1))
                wait(pe, q_taken, 2 * m)
                for k in range(KD):
                    mm = pe.matmul(ps[:, PJ], x_now[par][:, k], w_block("wkv", blk)[:, k, :], start=k == 0, stop=k == KD - 1)
                mm.then_inc(kv_projected, 1)

            def w_block(name, blk):
                return w3_set(name, ds(blk % 2, 1) if not isinstance(blk, int) else blk % 2)

            def project_q(m, par, s, k0, k1):
                if k0 == 0:
                    if s == 0 and isinstance(m, int) and m < 2:
                        pe.wait_ge(k_raw_ready, m + 1)
                        pe.wait_ge(vn_low, m + 1)
                    wait(pe, out_added, 2 * m - 2 + s)
                    if m_is_first(m) and s == 1:
                        pe.wait_ge(k_taken, 1)
                for k in range(k0, k1):
                    mm = pe.matmul(ps[:, PJ], x_now[par][:, k],
                                   w_block("wq", m // NB)[:, k, s * REP * DH:(s + 1) * REP * DH],
                                   start=k == 0, stop=k == KD - 1)
                if k1 == KD:
                    mm.then_inc(q_projected, 1)

            def m_is_first(m):
                return isinstance(m, int) and m == 0

            def turn_k(m):
                pe.wait_ge(q_taken, 2 * m + 1)
                pe.wait_ge(k_roped, m + 1)
                for s in range(HB):
                    mm = pe.transpose(ps[:, PJ, s * T:(s + 1) * T], k_rot[:, s], ident[:])
                mm.then_inc(k_turned, 1)

            def turn_q(m, s):
                pe.wait_ge(q_raw_ready, 2 * m + s + 1)
                pe.wait_ge(q_roped, 2 * m + s + 1)
                for h in range(REP):
                    mm = pe.transpose(ps[:, PJ, h * T:(h + 1) * T], q_rot[:, h], ident[:])
                mm.then_inc(q_turned, 1)

            def score(j, m, par, s, h):
                if h == 0:
                    pe.wait_ge(q_low, j + 1)
                    pe.wait_ge(kc_low, j + 1)
                    if s == 0:
                        pe.wait_ge(k_taken, m + 1)
                wait(pe, exp_done, 4 * j + h - 1)
                slot = h % 2
                to = s_ps[:, slot, 0:CACHED]
                pe.matmul(to, q_h[s][:, h], k_h[s][:].rearrange("p j t -> p (j t)"), start=True, stop=False)
                pe.matmul(to, q_h[s][:, h], k_l[s][:].rearrange("p j t -> p (j t)"), start=False, stop=False)
                pe.matmul(to, q_l[s][:, h], k_h[s][:].rearrange("p j t -> p (j t)"), start=False, stop=True)
                pe.matmul(s_ps[:, slot, CACHED:KEYS], q_t[s][:, h], k_new[par][:, s], start=True, stop=True
                          ).then_inc(scored, 1)

            def turn_probs(i, s, t):
                wait(pe, pt_low, KT * i + t - 1)
                c = key_tile(t) * P
                for h in range(REP):
                    if t == 0:
                        pe.wait_ge(prob_ready, 4 * i + h + 1)
                    mm = pe.transpose(ps[:, PT[(s + t) % 2], h * T:(h + 1) * T], prob[s][:, h, c:c + P], ident[:])
                mm.then_inc(pt_full, 1)

            def weigh(i, m, par, s, t):
                if t == 0:
                    wait(pe, o_taken, i)
                    pe.wait_ge(vn_low, m + 1)
                    vh, vl = vn_h[par][:, s], vn_l[par][:, s]
                else:
                    if t == 1:
                        pe.wait_ge(vc_low, i + 1)
                    vh, vl = v_h[s][:, key_tile(t)], v_l[s][:, key_tile(t)]
                x = (s + t) % 2
                pe.wait_ge(pt_high, KT * i + t + 1)
                pe.matmul(ps[:, OB], vh, pt_h[x][:], start=t == 0, stop=False)
                pe.matmul(ps[:, OB], vl, pt_h[x][:], start=False, stop=False)
                pe.wait_ge(pt_low, KT * i + t + 1)
                pe.matmul(ps[:, OB], vh, pt_l[x][:], start=False, stop=t == KT - 1).then_inc(pv_done, 1)

            def project_out(i, blk, s, *before):
                pe.wait_ge(o_taken, i + 1)
                for semaphore, value in before:
                    pe.wait_ge(semaphore, value)
                for h in range(REP):
                    mm = pe.matmul(ps[:, PJ], o_t[s][:, h], w_block("wo", blk)[:, s * REP + h, :],
                                   start=h == 0, stop=h == REP - 1)
                mm.then_inc(out_projected, 1)

            project_kv(0, 0)
            project_q(0, 0, 0, 0, KD)
            turn_q(0, 0)
            turn_k(0)
            project_q(0, 0, 1, 0, KD)
            turn_q(0, 1)
            project_kv(1, 1)
            for h in range(REP):
                score(0, 0, 0, 0, h)

            def half(i, n, par, s, scores, queries, out_rows):
                if scores:
                    score(*scores, 0)
                if out_rows:
                    project_out(*out_rows)
                turn_probs(i, s, 0)
                turn_probs(i, s, 1)
                if queries:
                    project_q(*queries, 0, 2)
                weigh(i, n, par, s, 0)
                turn_probs(i, s, 2)
                if queries:
                    project_q(*queries, 2, KD)
                if scores:
                    score(*scores, 1)
                weigh(i, n, par, s, 1)
                turn_probs(i, s, 3)
                if scores:
                    score(*scores, 2)
                if queries:
                    turn_q(queries[0], s)
                weigh(i, n, par, s, 2)
                turn_probs(i, s, 4)
                weigh(i, n, par, s, 3)
                if queries and s == 0:
                    turn_k(queries[0])
                if scores:
                    score(*scores, 3)
                weigh(i, n, par, s, 4)

            def step(n, par, last):
                i, m = 2 * n, n + 1
                first = isinstance(n, int) and n == 0
                if more(n, 1):
                    kv_read = ((k_raw_ready, n + 2), (vn_low, n + 2))
                    k_read_out = ((k_taken, n + 2),)
                else:
                    kv_read = ((q_taken, 2 * n + 2),)
                    k_read_out = ((out_added, 2 * n),)
                half(i, n, par, 0, (i + 1, n, par, 1), (m, 1 - par, 0) if not last else None,
                     (i - 1, (n - 1) // NB, 1) + kv_read if not first else None)
                half(i + 1, n, par, 1, (i + 2, m, 1 - par, 0) if not last else None,
                     (m, 1 - par, 1) if not last else None, (i, n // NB, 0) + k_read_out)
                if more(n, 2):
                    project_kv(n + 2, par)

            over_steps(pe, step)
            project_out(GROUPS - 1, BLOCKS - 1, 1, (out_added, GROUPS - 1))

        @block.scalar
        def _(act_e):
            for i in range(2):
                act_e.wait_ge(angle_ready, i + 1)
                act_e.activation(trig[:, i], red[:], ACT.Sin).then_inc(sin_ready, 1)
            act_e.wait_ge(tables_ready, 2)
            for i, table in enumerate(tables):
                act_e.dma_start(turn_dram[:, :, i].rearrange("b p d -> p b d"), table[:]).then_inc(tables_stored, 16)
            for hf in range(2):
                act_e.wait_ge(h0_ready, hf + 1)
                act_e.copy(h_sb[:, hf * HALF:(hf + 1) * HALF], ps[:, hf]).then_inc(h0_copied, 1)
            act_e.wait_ge(gap_ready, 1)
            act_e.activation(e_gap[:], gap[:], ACT.Exp).then_inc(gap_exp, 1)

            def exp_gate(f, par):
                for hf in range(2):
                    u = 2 * f + hf
                    act_e.wait_ge(gate_done, u + 1)
                    wait(act_e, act_ready, u - 1)
                    act_e.activation(sil[hf][:], ps[:, hf], ACT.Exp, scale=-1.0).then_inc(exp_g, 1)

            over_hidden(act_e, exp_gate)

            def keep_x(b, par):
                act_e.wait_ge(x3_summed, b + 1)
                act_e.dma_start(x3_dram[ds(b, 1)].rearrange("o p k t -> (o p) k t"), x_sum[par][:]).then_inc(x3_stored[par], 16)
                act_e.wait_ge(x3_turned, b + 1)
                act_e.copy(acc[:, ds(b, 1), :].rearrange("p o n -> p (o n)"), ps[:, 6 + par]).then_inc(acc_ready, 1)

            over_batches(act_e, keep_x)

            def square(done, src, heads, dst):
                for h in range(heads):
                    wait(act_e, squared, done + h - 1)
                    act_e.activation(junk[:, h % 2], src[:, h], ACT.Square, accum_out=dst[:, h:h + 1]).then_inc(squared, 1)

            def take_kv(m, par):
                act_e.wait_ge(kv_projected, m + 1)
                wait(act_e, pv_done, KT * (2 * m - 3) + 1)
                act_e.copy(vn_h[par][:], ps[:, PJ, HB * DH:2 * HB * DH]).then_inc(vn_high, 1)
                wait(act_e, k_read, m)
                act_e.copy(k_raw[:], ps[:, PJ, 0:HB * DH]).then_inc(k_raw_ready, 1)
                act_e.wait_ge(k_raw_ready, m + 1)
                square(10 * m, k_raw, HB, ss_k[:])

            def take_raw_q(m, s):
                act_e.wait_ge(q_projected, 2 * m + s + 1)
                wait(act_e, q_roped, 2 * m + s)
                act_e.copy(q_raw[:], ps[:, PJ]).then_inc(q_raw_ready, 1)

            def square_q(m, s):
                act_e.wait_ge(q_raw_ready, 2 * m + s + 1)
                square(10 * m + 2 + 4 * s, q_raw, REP, ss_q[:, s])

            def take_k(m, par):
                act_e.wait_ge(k_turned, m + 1)
                wait(act_e, scored, 8 * m - 8)
                act_e.copy(k_new[par][:], ps[:, PJ, 0:HB * T]).then_inc(k_taken, 1)

            def take_q(m, s):
                act_e.wait_ge(q_turned, 2 * m + s + 1)
                wait(act_e, scored, 8 * m + 4 * s - 4)
                act_e.copy(q_h[s][:], ps[:, PJ])
                act_e.copy(q_t[s][:], ps[:, PJ]).then_inc(q_taken, 1)

            def exp_scores(j, s, h):
                act_e.wait_ge(masked, 4 * j + h + 1)
                if h == 0:
                    wait(act_e, pt_full, KT * (j - 1))
                act_e.activation(prob[s][:, h], s_ps[:, h % 2, 0:KEYS], ACT.Exp, bias=negmax[:, s, h:h + 1], scale=-1.0,
                                 accum_out=den[:, s, h:h + 1]).then_inc(exp_done, 1)

            def high_probs(i, s, t):
                act_e.wait_ge(pt_full, KT * i + t + 1)
                wait(act_e, pv_done, KT * i + t - 1)
                act_e.copy(pt_h[(s + t) % 2][:], ps[:, PT[(s + t) % 2]]).then_inc(pt_high, 1)

            def high_k(m, par, s):
                act_e.wait_ge(k_loaded[par], 16 * NPAGE * (m // 2 + 1))
                wait(act_e, scored, 8 * m + 4 * s - 4)
                act_e.copy(k_h[s][:], kc[par][:, :, s, :]).then_inc(kc_high, 1)

            def high_v(m, par, s):
                act_e.wait_ge(v_loaded[par], 16 * NPAGE * (m // 2 + 1))
                wait(act_e, pv_done, KT * (2 * m + s - 1))
                act_e.copy(v_h[s][:], vc[par][:, :, s * DH:(s + 1) * DH]).then_inc(vc_high, 1)

            high_k(0, 0, 0)
            high_k(0, 0, 1)
            take_kv(0, 0)
            take_raw_q(0, 0)
            for i in range(2):
                act_e.wait_ge(x3_stored[i], 16 * NB // 2)
            square_q(0, 0)
            take_q(0, 0)
            take_k(0, 0)
            take_raw_q(0, 1)
            square_q(0, 1)
            take_q(0, 1)
            high_v(0, 0, 0)
            take_kv(1, 1)
            for h in range(REP):
                exp_scores(0, 0, h)

            def half(i, s, v, k):
                if v:
                    exp_scores(i + 1, 1 - s, 0)
                    high_v(*v)
                if k:
                    high_k(*k)
                high_probs(i, s, 0)
                high_probs(i, s, 1)
                high_probs(i, s, 2)
                if k:
                    take_raw_q(k[0], s)
                    square_q(k[0], s)
                if v:
                    exp_scores(i + 1, 1 - s, 1)
                high_probs(i, s, 3)
                if k:
                    take_q(k[0], s)
                high_probs(i, s, 4)
                if v:
                    exp_scores(i + 1, 1 - s, 2)
                if k and s == 0:
                    take_k(k[0], k[1])
                if v:
                    exp_scores(i + 1, 1 - s, 3)

            def step(n, par, last):
                m = n + 1
                half(2 * n, 0, (n, par, 1), (m, 1 - par, 0) if not last else None)
                half(2 * n + 1, 1, (m, 1 - par, 0) if not last else None, (m, 1 - par, 1) if not last else None)
                if more(n, 2):
                    take_kv(n + 2, par)

            over_steps(act_e, step)

        @block.vector
        def _(dve):
            count = [0]

            def link(ins):
                count[0] += 1
                ins.then_inc(dve_step, 1)
                dve.wait_ge(dve_step, count[0])

            def bc(x, n):
                return x.unsqueeze(2).to_broadcast([P, NB, n])

            dve.wait_ge(ids_loaded, 80)
            dve.wait_ge(consts_ready, 1)
            dve.tensor_copy(len_f[:], len_i[:])
            link(dve.tensor_copy(lang_f[:], lang_i[:]))
            link(dve.tensor_tensor(pos[:], pos[:], len_f[:], ALU.add))
            link(dve.tensor_tensor(ang[:], bc(pos[:], DH // 2), inv_f[:].unsqueeze(1).to_broadcast([P, NB, DH // 2]), ALU.mult))
            for i, (shift, quarter) in enumerate(((0.0, 0.0), (0.25, math.pi / 2))):
                link(dve.tensor_scalar(turns[:], ang[:], 1.0 / TWO_PI, shift, ALU.mult, ALU.add))
                link(dve.tensor_scalar(turns[:], turns[:], ROUND, -ROUND, ALU.add, ALU.add))
                if i == 1:
                    dve.wait_ge(sin_ready, 1)
                link(dve.scalar_tensor_tensor(out=red[:], in0=turns[:], scalar=-PI_A, in1=ang[:], op0=ALU.mult, op1=ALU.add))
                link(dve.scalar_tensor_tensor(out=red[:], in0=turns[:], scalar=-PI_B, in1=red[:], op0=ALU.mult, op1=ALU.add))
                link(dve.scalar_tensor_tensor(out=red[:], in0=turns[:], scalar=-PI_C, in1=red[:], op0=ALU.mult, op1=ALU.add))
                if i == 1:
                    link(dve.tensor_scalar(red[:], red[:], quarter, None, ALU.add))
                link(dve.tensor_scalar(red[:], red[:], 3.1415925, -3.1415925, ALU.min, ALU.max))
                dve.tensor_scalar(turns[:], turns[:], 0.0, None, ALU.mult).then_inc(angle_ready, 1)
                dve.wait_ge(angle_ready, i + 1)
            dve.wait_ge(sin_ready, 2)
            for w, (ct, st) in enumerate((tables[0:2], tables[2:4])):
                lo, hi = (norm_w[:, w, n * 64:(n + 1) * 64].unsqueeze(1).to_broadcast([P, NB, 64]) for n in range(2))
                dve.tensor_tensor(ct[:, :, 0:64], trig[:, 1], lo, ALU.mult)
                dve.tensor_tensor(ct[:, :, 64:128], trig[:, 1], hi, ALU.mult)
                dve.tensor_tensor(st[:, :, 0:64], trig[:, 0], lo, ALU.mult)
                dve.scalar_tensor_tensor(out=st[:, :, 64:128], in0=trig[:, 0], scalar=-1.0, in1=hi,
                                         op0=ALU.mult, op1=ALU.mult).then_inc(tables_ready, 1)

            link(dve.tensor_tensor(one1[:], lang[:], bc(lang_f[:], E), ALU.is_equal))
            dve.wait_ge(logits_ready, 1)
            link(dve.scalar_tensor_tensor(out=logit[:], in0=one1[:], scalar=5.0,
                                          in1=ps[:, 6, 0:NB * E].rearrange("p (b e) -> p b e", e=E),
                                          op0=ALU.mult, op1=ALU.add))
            for src, top, one in ((logit, top1, one1), (less, top2, one2)):
                link(dve.tensor_reduce(top[:], src[:], AX.X, ALU.max))
                link(dve.tensor_tensor(one[:], src[:], bc(top[:], E), ALU.is_equal))
                link(dve.scalar_tensor_tensor(out=cand[:], in0=one[:], scalar=-16.0, in1=lang[:], op0=ALU.mult, op1=ALU.add))
                link(dve.tensor_reduce(pick[:], cand[:], AX.X, ALU.min))
                link(dve.tensor_tensor(one[:], cand[:], bc(pick[:], E), ALU.is_equal))
                if one is one1:
                    link(dve.scalar_tensor_tensor(out=less[:], in0=one1[:], scalar=-3e38, in1=logit[:],
                                                  op0=ALU.mult, op1=ALU.add))
            dve.tensor_tensor(gap[:], top2[:], top1[:], ALU.subtract).then_inc(gap_ready, 1)
            dve.wait_ge(gap_exp, 1)
            link(dve.tensor_scalar(g2[:], e_gap[:], 1.0, None, ALU.add))
            link(dve.reciprocal(g1[:], g2[:]))
            link(dve.tensor_tensor(g2[:], e_gap[:], g1[:], ALU.mult))
            dve.tensor_tensor(one1[:], one1[:], bc(g1[:], E), ALU.mult)
            link(dve.tensor_tensor(one2[:], one2[:], bc(g2[:], E), ALU.mult))
            link(dve.tensor_tensor(gates[:], one1[:], one2[:], ALU.add))
            dve.tensor_scalar(gate_x[:].rearrange("p b (e r) -> p b e r", r=R),
                              gates[:].unsqueeze(3).to_broadcast([P, NB, E, R]), 2.0, None, ALU.mult
                              ).then_inc(gates_ready, 1)
            for hf in range(2):
                dve.wait_ge(h0_copied, hf + 1)
                dve.wait_ge(gate_t, hf + 1)
                dve.tensor_tensor(h_gated[:, hf * HALF:(hf + 1) * HALF], h_sb[:, hf * HALF:(hf + 1) * HALF],
                                  ps[:, 2 + hf], ALU.mult).then_inc(h_ready, 1)
            for hf in range(2):
                for o in range(KD):
                    n = KD * hf + o
                    dve.wait_ge(l0_out, n + 1)
                    half = slice(hf * HALF, (hf + 1) * HALF)
                    dve.tensor_tensor(xb[:, o, half], xa[:, o, half], ps[:, 4 + n % 2], ALU.add).then_inc(x1_ready, 1)

            def own_rows(dst, bank, hf, done):
                dve.tensor_tensor(dst[:, hf * HALF:(hf + 1) * HALF].rearrange("p (b t) -> p b t", t=T),
                                  ps[:, bank].rearrange("p (b t) -> p b t", t=T),
                                  own[:, 4 * hf:4 * hf + 4].unsqueeze(2).to_broadcast([P, 4, T]), ALU.mult
                                  ).then_inc(done, 1)

            for n, (dst, bank) in enumerate(((t_gate, 4), (t_up, 6))):
                for hf in range(2):
                    dve.wait_ge(t_full, 2 * n + hf + 1)
                    own_rows(dst, bank + hf, hf, t_ready)

            def gated(f, par):
                for hf in range(2):
                    u = 2 * f + hf
                    dve.wait_ge(exp_g, u + 1)
                    dve.tensor_scalar(sil[hf][:], sil[hf][:], 1.0, None, ALU.add).then_inc(silu_step, 1)
                    dve.wait_ge(silu_step, 3 * u + 1)
                    dve.reciprocal(sil[hf][:], sil[hf][:]).then_inc(silu_step, 1)
                    dve.wait_ge(silu_step, 3 * u + 2)
                    dve.tensor_tensor(sil[hf][:], ps[:, hf], sil[hf][:], ALU.mult).then_inc(silu_step, 1)
                    dve.wait_ge(silu_step, 3 * u + 3)
                    dve.wait_ge(up_done, u + 1)
                    dve.tensor_tensor(act[:, ds(f, 1), hf * HALF:(hf + 1) * HALF].rearrange("p o n -> p (o n)"),
                                      ps[:, 2 + hf], sil[hf][:], ALU.mult).then_inc(act_ready, 1)

            over_hidden(dve, gated)
            for hf in range(2):
                dve.wait_ge(td_full, hf + 1)
                own_rows(t_down, 4 + hf, hf, td_ready)
            for o in range(KD):
                for hf in range(2):
                    n = 2 * o + hf
                    dve.wait_ge(l1_out, n + 1)
                    half = slice(hf * HALF, (hf + 1) * HALF)
                    dve.tensor_tensor(xa[:, o, half], xb[:, o, half], ps[:, n % 4], ALU.add).then_inc(x2_ready, 1)

            dve.wait_ge(x2_ready, 2 * KD)

            def add_adapter(b, par):
                dve.wait_ge(l2_out, b + 1)
                wait(dve, x3_turned, b - 1)
                wait(dve, x3_stored[par], 16 * (b // 2))
                dve.tensor_tensor(x_sum[par][:], xa[:, :, ds(b * T, T)],
                                  ps[:, 4 + par].rearrange("p (k t) -> p k t", t=T), ALU.add).then_inc(x3_summed, 1)

            over_batches(dve, add_adapter)

            def set_mask(m, par):
                dve.tensor_scalar(mask[par][:, 0:CACHED], iota[:], len_f[:, ds(m % NB, 1)], NEG, ALU.is_ge, ALU.mult
                                  ).then_inc(mask_ready, 1)

            def low_vn(m, par):
                dve.wait_ge(vn_high, m + 1)
                dve.wait_ge(k_raw_ready, m + 1)
                wait(dve, pv_done, KT * (2 * m - 3) + 1)
                dve.tensor_tensor(vn_l[par][:].rearrange("p s d -> p (s d)"), ps[:, PJ, HB * DH:2 * HB * DH],
                                  vn_h[par][:].rearrange("p s d -> p (s d)").bitcast(F32), ALU.subtract).then_inc(vn_low, 1)

            def low_q(m, s):
                dve.wait_ge(q_taken, 2 * m + s + 1)
                wait(dve, scored, 8 * m + 4 * s - 4)
                dve.tensor_tensor(q_l[s][:], q_t[s][:], q_h[s][:].bitcast(F32), ALU.subtract).then_inc(q_low, 1)

            def rotate_k(m, par):
                dve.wait_ge(k_raw_ready, m + 1)
                dve.wait_ge(rstd_ready, 3 * m + 1)
                wait(dve, k_roped, m)
                wait(dve, k_turned, m)
                for h in range(HB):
                    for part, f in ((part_ck, 2), (part_sk, 3)):
                        last = dve.scalar_tensor_tensor(
                            out=part[:, h], in0=k_raw[:, h], scalar=rs_k[:, h:h + 1],
                            in1=turn[par][:, f], op0=ALU.mult, op1=ALU.mult)
                last.then_inc(k_read, 1)
                dve.wait_ge(k_read, m + 1)
                dve.tensor_tensor(k_rot[:, :, 0:64], part_ck[:, :, 0:64], part_sk[:, :, 64:128], ALU.add)
                dve.tensor_tensor(k_rot[:, :, 64:128], part_ck[:, :, 64:128], part_sk[:, :, 0:64], ALU.add).then_inc(k_roped, 1)

            def cosine_q(m, par, s):
                dve.wait_ge(q_raw_ready, 2 * m + s + 1)
                wait(dve, q_roped, 2 * m + s)
                dve.tensor_tensor(part_c[:], q_raw[:], turn[par][:, 0:1, :].to_broadcast([P, REP, DH]), ALU.mult
                                  ).then_inc(q_cosine, 1)

            def sum_q(m, s):
                wait(dve, q_turned, 2 * m + s)
                dve.wait_ge(q_cosine, 2 * m + s + 1)
                dve.wait_ge(q_sine, 2 * m + s + 1)
                dve.tensor_tensor(q_rot[:, :, 0:64], part_c[:, :, 0:64], part_s[:, :, 64:128], ALU.add)
                dve.tensor_tensor(q_rot[:, :, 64:128], part_c[:, :, 64:128], part_s[:, :, 0:64], ALU.add).then_inc(q_roped, 1)

            def mask_scores(j, m, par, s, h):
                if h == 0:
                    dve.wait_ge(rstd_ready, 3 * m + 2 + s)
                if h == 0 and s == 0:
                    dve.wait_ge(mask_ready, m + 1)
                dve.wait_ge(scored, 4 * j + h + 1)
                settle(dve, j)
                x = s_ps[:, h % 2, 0:KEYS]
                dve.tensor_tensor_reduce(x, x, mask[par][:], rs_q[:, s, h:h + 1], 3.4e38, ALU.add, ALU.min,
                                         negmax[:, s, h:h + 1]).then_inc(masked, 1)

            def invert_sum(j, s, h):
                dve.wait_ge(exp_done, 4 * j + h + 1)
                dve.reciprocal(rden[:, s, h:h + 1], den[:, s, h:h + 1]).then_inc(rden_ready, 1)

            def low_probs(i, s, t):
                dve.wait_ge(pt_high, KT * i + t + 1)
                wait(dve, pv_done, KT * i + t - 1)
                x = (s + t) % 2
                dve.tensor_tensor(pt_l[x][:], ps[:, PT[x]], pt_h[x][:].bitcast(F32), ALU.subtract).then_inc(pt_low, 1)

            def take_o(i, s):
                dve.wait_ge(pv_done, KT * (i + 1))
                wait(dve, out_projected, i - 1)
                dve.tensor_copy(o_t[s][:], ps[:, OB]).then_inc(o_taken, 1)

            def add_out(i, b):
                dve.wait_ge(out_projected, i + 1)
                wait(dve, out_added, i)
                to = acc[:, ds(b, 1), :].rearrange("p o n -> p (o n)")
                dve.tensor_tensor(to, ps[:, PJ], to, ALU.add).then_inc(out_added, 1)

            dve.wait_ge(acc_ready, NB)
            for i in range(2):
                dve.wait_ge(x3_stored[i], 16 * NB // 2)
            set_mask(0, 0)
            low_vn(0, 0)
            cosine_q(0, 0, 0)
            sum_q(0, 0)
            rotate_k(0, 0)
            low_q(0, 0)
            cosine_q(0, 0, 1)
            sum_q(0, 1)
            low_q(0, 1)
            for h in range(REP):
                mask_scores(0, 0, 0, 0, h)
                if h > 0:
                    invert_sum(0, 0, h - 1)

            def half(i, s, scores, queries, out_rows):
                if queries and s == 0:
                    low_vn(queries[0], queries[1])
                if scores:
                    mask_scores(*scores, 0)
                invert_sum(i, s, REP - 1)
                if scores:
                    invert_sum(i + 1, 1 - s, 0)
                if out_rows:
                    add_out(*out_rows)
                low_probs(i, s, 0)
                low_probs(i, s, 1)
                if queries and s == 0:
                    set_mask(queries[0], queries[1])
                    rotate_k(queries[0], queries[1])
                low_probs(i, s, 2)
                if queries:
                    cosine_q(*queries)
                if scores:
                    mask_scores(*scores, 1)
                if queries:
                    sum_q(queries[0], s)
                if scores:
                    invert_sum(i + 1, 1 - s, 1)
                low_probs(i, s, 3)
                if scores:
                    mask_scores(*scores, 2)
                if queries:
                    low_q(queries[0], s)
                low_probs(i, s, 4)
                if scores:
                    invert_sum(i + 1, 1 - s, 2)
                    mask_scores(*scores, 3)
                take_o(i, s)

            def step(n, par, last):
                i, m = 2 * n, n + 1
                first = isinstance(n, int) and n == 0
                half(i, 0, (i + 1, n, par, 1), (m, 1 - par, 0) if not last else None,
                     (i - 1, (n - 1) % NB) if not first else None)
                half(i + 1, 1, (i + 2, m, 1 - par, 0) if not last else None,
                     (m, 1 - par, 1) if not last else None, (i, n % NB))

            over_steps(dve, step)
            add_out(GROUPS - 1, NB - 1)


def kernel(**inputs):
    import numpy as np
    import concourse.bacc as bacc
    from concourse.bass_utils import run_bass_kernel_spmd

    g = {n: np.asarray(v) for n, v in inputs.items()}

    def pieces(w):
        return w.T.reshape(KD, P, -1).transpose(1, 0, 2)

    def padded(w, axis):
        widths = [(0, 0)] * w.ndim
        widths[axis] = (0, FP - F)
        return np.pad(w, widths)

    x = g["x"].reshape(NT, D)
    gu = [padded(g[f"L1_cond_W_{n}"], 0).reshape(FT, P, KD, P).transpose(0, 3, 2, 1) for n in ("gate", "up")]
    kvw = [np.stack([pieces(g[f"L3_cond_W{n}"][k * HB * DH:(k + 1) * HB * DH]) for k in range(BLOCKS)]) for n in "kv"]
    arrays = {
        "x": pieces(x),
        "w0": pieces(g["L0_cond_W"]),
        "wr": pieces(g["L0_cond_Wr"]),
        "a0": pieces(g["L0_cond_A"].reshape(E * R, D)),
        "b0": g["L0_cond_B"].transpose(0, 2, 1).reshape(E * R, D),
        "w_gu": np.stack(gu, axis=2),
        "w_down": padded(g["L1_cond_W_down"], 1).reshape(KD, P, FT, P).transpose(0, 3, 2, 1),
        "a_gate": g["L1_cond_A_gate"][0].reshape(-1, R, KD, P).transpose(0, 3, 2, 1),
        "a_up": g["L1_cond_A_up"][0].reshape(-1, R, KD, P).transpose(0, 3, 2, 1),
        "a_down": padded(g["L1_cond_A_down"][0], 2).reshape(-1, R, FT, P).transpose(0, 3, 2, 1),
        "b_gate": padded(g["L1_cond_B_gate"][0], 1).transpose(0, 2, 1),
        "b_up": padded(g["L1_cond_B_up"][0], 1).transpose(0, 2, 1),
        "b_down": g["L1_cond_B_down"][0].transpose(0, 2, 1),
        "w2": g["L2_cond_weight"].reshape(-1, D, KD, P).transpose(0, 3, 2, 1),
        "wq": np.stack([pieces(w) for w in g["L3_cond_Wq"].reshape(BLOCKS, -1, D)]),
        "wkv": np.concatenate(kvw, axis=3),
        "wo": g["L3_cond_Wo"].reshape(D, BLOCKS, HB * REP, DH).transpose(1, 3, 2, 0),
        "k_cache": g["L3_cond_k_cache"].reshape(-1, PAGE, BLOCKS, HB, DH).transpose(0, 2, 4, 3, 1),
        "v_cache": g["L3_cond_v_cache"].reshape(-1, PAGE, BLOCKS, HB * DH).transpose(0, 2, 1, 3),
        "q_norm": g["L3_cond_q_norm_w"],
        "k_norm": g["L3_cond_k_norm_w"],
        "inv_f": np.float32(1.0) / np.power(np.float32(10000.0), np.arange(0, DH, 2, dtype=np.float32) / np.float32(DH)),
        "ids": np.concatenate([g["itok_B_2_6"], g["itok_B_0_15"], g["itok_Bx16_0_63"].reshape(-1)])[None],
        "lens": g["itok_B_207_1644"],
        "lang": g["itok_B_0_7"],
    }
    nc = bacc.Bacc("TRN2", target_bir_lowering=False, num_devices=1)
    feed, aps = {}, {}
    for name, v in arrays.items():
        v = np.ascontiguousarray(v)
        feed[f"in_{name}"] = v
        aps[name] = nc.dram_tensor(f"in_{name}", v.shape, mybir.dt.from_np(v.dtype), kind="ExternalInput").ap()
    o = nc.dram_tensor("result", (NB, T, D), F32, kind="ExternalOutput").ap()
    x3 = nc.dram_tensor("x3_scratch", (NB, P, KD, T), F32, kind="Internal").ap()
    turn = nc.dram_tensor("turn_scratch", (NB, P, 4, DH), F32, kind="Internal").ap()
    build(nc, aps, o.rearrange("b t n -> t b n"), x3, turn)
    r = run_bass_kernel_spmd(nc, [feed], core_ids=[0])
    return r.results[0]["result"]
```

```python
import math
from contextlib import ExitStack

import concourse.bass as bass
from concourse import mybir

ALU = mybir.AluOpType
ACT = mybir.ActivationFunctionType
AX = mybir.AxisListType
F32 = mybir.dt.float32
F32R = mybir.dt.float32r
F16 = mybir.dt.float16
BF16 = mybir.dt.bfloat16
I32 = mybir.dt.int32

P = 128
NB, T, D = 8, 128, 512
NT = NB * T
HALF = NT // 2
KD = D // P
E, R = 8, 16
F = 1376
FT = -(-F // P)
FP = FT * P
HK, REP, DH = 8, 4, 128
PAGE, NPAGE = 32, 16
CACHED = PAGE * NPAGE
KEYS = CACHED + T
KT = KEYS // P
HB = 2
BLOCKS = HK // HB
STEPS = BLOCKS * NB
GROUPS = STEPS * HB
SCALE = 1.0 / math.sqrt(DH)
EPS = 1e-6
TWO_PI = 2 * math.pi
PI_A = 6.28125
PI_B = 0.0019350051879882812
PI_C = TWO_PI - PI_A - PI_B
ROUND = 12582912.0
NEG = -1e30


def build(nc, a, out, x3_dram, turn_dram):
    ds = bass.ds
    base = 16512
    KB = 1024

    class Region:
        def __init__(self, start, size):
            self.at, self.end = start, start + size

        def take(self, name, shape, dt=F32):
            size = 2 if dt in (F16, BF16) else 4
            for n in shape[1:]:
                size *= n
            t = nc.alloc_sbuf_tensor_at(name, shape, dt, offset=self.at)
            self.at += -(-size // 32) * 32
            assert self.at <= self.end, name
            return t

    at = [base]

    def region(size):
        at[0] += size
        return at[0] - size

    r_xa, r_xb, r_acc, r_rope, r_kv = (region(16 * KB) for _ in range(5))
    r_w = region(80 * KB)
    r_arena = region(38 * KB + 512)
    r_small = region(nc.sbuf_usable_end - at[0] - 32)

    xa = Region(r_xa, 16 * KB).take("x_even", [P, KD, NT])
    xb = Region(r_xb, 16 * KB).take("x_odd", [P, KD, NT])
    acc = Region(r_acc, 16 * KB).take("acc", [P, NB, D])
    rope = Region(r_rope, 16 * KB)
    tables = [rope.take(n, [P, NB, DH]) for n in ("all_cos_q", "all_sin_q", "all_cos_k", "all_sin_k")]
    kv = Region(r_kv, 16 * KB)
    kc = [kv.take(f"kc{i}", [P, NPAGE, HB, PAGE]) for i in range(2)]
    vc = [kv.take(f"vc{i}", [P, CACHED // P, HB * DH]) for i in (1, 0)][::-1]
    w3 = Region(r_w, 80 * KB)
    W_KV, W_Q, W_O = 0, (1, 2), (3, 4)
    w_h, w_l, w_raw = [], [], []
    for u in range(5):
        w_h.append(w3.take(f"w_h{u}", [P, KD, 4 * DH], F32R))
        w_raw.append(Region(w3.at, 8 * KB).take(f"w_raw{u}", [P, KD, 4 * DH]))
        w_l.append(w3.take(f"w_l{u}", [P, KD, 4 * DH], F32R))
    r_w1 = r_w + 40 * KB

    small = Region(r_small, nc.sbuf_usable_end - r_small)
    ident = small.take("ident", [P, P])
    iota = small.take("iota", [P, CACHED], F16)
    mask = [small.take(f"mask{i}", [P, KEYS], BF16) for i in range(2)]
    len_i = small.take("len_i", [P, NB], I32)
    len_f = small.take("len_f", [P, NB])
    lang_i = small.take("lang_i", [P, NB], I32)
    lang_f = small.take("lang_f", [P, NB])
    ids = small.take("ids", [1, 2 * NB + NB * NPAGE], I32)
    own = small.take("own", [P, NB])
    neghalf = small.take("neghalf", [P, REP])
    negmax = small.take("negmax", [P, HB, REP])
    den = small.take("den", [P, HB, REP])
    rden = small.take("rden", [P, HB, REP])
    ss_k = small.take("ss_k", [P, HB])
    ss_q = small.take("ss_q", [P, HB, REP])
    ms = small.take("ms", [P, REP])
    rs_k = small.take("rs_k", [P, HB])
    rs_q = small.take("rs_q", [P, HB, REP])
    part_ck = small.take("part_ck", [P, HB, DH])
    k_raw = small.take("k_raw", [P, HB, DH])
    q_raw = small.take("q_raw", [P, REP, DH])

    ar = Region(r_arena, 38 * KB + 512)
    prob = [ar.take(f"prob{i}", [P, REP, KEYS]) for i in range(2)]
    o_h, o_l = (ar.take(f"o_{n}", [P, REP, T], F32R) for n in "hl")
    q_t = [ar.take(f"q_t{i}", [P, REP, T]) for i in range(2)]
    k_new = [ar.take(f"k_new{i}", [P, HB, T]) for i in range(2)]
    x_hl = [ar.take(f"x_hl{i}", [P, 2, KD, T], F32R) for i in range(2)]
    x_h, x_l = ([x_hl[i][:, n] for i in range(2)] for n in range(2))
    junk = ar.take("junk", [P, 2, DH], BF16)
    ov = Region(r_xa, 16 * KB)
    pt_h, pt_l = ([ov.take(f"pt_{n}{i}", [P, REP * T], F32R) for i in range(2)] for n in "hl")
    part_c = ov.take("part_c", [P, REP, DH])
    part_s = ov.take("part_s", [P, REP, DH])
    q_rot = ov.take("q_rot", [P, REP, DH])
    k_rot = ov.take("k_rot", [P, HB, DH])
    part_sk = ov.take("part_sk", [P, HB, DH])

    ov = Region(r_rope, 16 * KB)
    turn = [ov.take(f"turn{i}", [P, 4, DH]) for i in range(2)]
    q_h, q_l = ([ov.take(f"q_{n}{i}", [P, REP, T], F32R) for i in range(2)] for n in "hl")
    vn_h, vn_l = ([ov.take(f"vn_{n}{i}", [P, HB, DH], F32R) for i in range(2)] for n in "hl")
    ov = Region(r_xb, 16 * KB)
    k_h, k_l = ([ov.take(f"k_{n}{i}", [P, NPAGE, PAGE], F32R) for i in range(2)] for n in "hl")
    v_h, v_l = ([ov.take(f"v_{n}{i}", [P, CACHED // P, DH], F32R) for i in range(2)] for n in "hl")

    z = Region(r_w1, 44 * KB)
    w0 = z.take("w0", [P, KD, D])
    wr = z.take("wr", [P, KD, E])
    a0 = z.take("a0", [P, KD, E * R])
    b0 = z.take("b0", [P, D])
    gate_x = z.take("gate_x", [P, NB, E * R])
    h_sb = z.take("h_sb", [P, NT])
    h_gated = z.take("h_gated", [P, NT])
    ang, turns, red = (z.take(n, [P, NB, DH // 2]) for n in ("ang", "turns", "red"))
    trig = z.take("trig", [P, 2, NB, DH // 2])
    norm_w = z.take("norm_w", [P, 2, DH])
    inv_f = z.take("inv_f", [P, DH // 2])
    pos = z.take("pos", [P, NB])
    logit, cand, one1, one2, less, gates, lang = (
        z.take(n, [P, NB, E]) for n in ("logit", "cand", "one1", "one2", "less", "gates", "lang"))
    top1, top2, pick, gap, e_gap, g1, g2 = (
        z.take(n, [P, NB]) for n in ("top1", "top2", "pick", "gap", "e_gap", "g1", "g2"))
    act = Region(r_w1, 44 * KB).take("act", [P, FT, NT])
    x1_h = Region(r_xa, 16 * KB).take("x1_h", [P, KD, NT], F32R)
    x1_l = Region(r_rope, 16 * KB).take("x1_l", [P, KD, NT], F32R)
    y = Region(r_w + 32 * KB, 8 * KB)
    gu_h = [y.take(f"gu_h{i}", [P, 2, KD, P], F32R) for i in range(2)]
    y = Region(r_arena + 4 * KB, 8 * KB)
    gu_l = [y.take(f"gu_l{i}", [P, 2, KD, P], F32R) for i in range(2)]
    y = Region(r_arena + 4 * KB, 34 * KB)
    w_gu = [y.take(f"w_gu{i}", [P, 2, KD, P]) for i in range(2)]
    t_gate, t_up = y.take("t_gate", [P, NT]), y.take("t_up", [P, NT])
    sil = [y.take(f"sil{i}", [P, HALF]) for i in range(2)]
    a_up, b_up = y.take("a_up", [P, KD, NB * R]), y.take("b_up", [P, FP])
    b_now = [y.take(f"b_now{i}", [P, 2, P]) for i in range(2)]
    y = Region(r_acc, 16 * KB)
    a_down, b_gate = y.take("a_down", [P, FT, NB * R]), y.take("b_gate", [P, FP])
    b_down, a_gate = y.take("b_down", [P, D]), y.take("a_gate", [P, KD, NB * R])
    y = Region(r_kv, 16 * KB)
    w_down = [y.take(f"w_down{i}", [P, FT, P]) for i in range(2)]
    y = Region(r_kv, 16 * KB)
    a_raw = {n: y.take(f"{n}_raw", [P, NB, k, R]) for n, k in (("a_gate", KD), ("a_up", KD), ("a_down", FT))}
    t_down = Region(r_arena + 12 * KB, 4 * KB).take("t_down", [P, NT])
    w2 = [Region(r_arena + 4 * KB, 8 * KB).take("w2_0", [P, KD, D]),
          Region(r_arena + 16 * KB, 8 * KB).take("w2_1", [P, KD, D])]
    y = Region(r_arena + 24 * KB, 4 * KB)
    x_sum = [y.take(f"x_sum{i}", [P, KD, T]) for i in range(2)]
    y = Region(r_kv + 4 * KB, 8 * KB)
    x_split = [y.take(f"x_split{i}", [P, 2, KD, T], F32R) for i in range(2)]

    with ExitStack() as ctx:
        ps = ctx.enter_context(nc.psum_tensor("ps", [P, 8, 512], F32))
        s_ps = ps[:, 0:4, :].rearrange("p (s b) n -> p s (b n)", s=2)
        PT, OB, PJ = (4, 5), 6, 7

        def sem(name):
            return ctx.enter_context(nc.semaphore(name))

        x_loaded = [sem(f"x_loaded{i}") for i in range(2)]
        l0_small_loaded, l0_loaded, ids_loaded, rows_loaded = sem("l0_small_loaded"), sem("l0_loaded"), sem("ids_loaded"), sem("rows_loaded")
        lora_loaded = sem("lora_loaded")
        gu_loaded = [sem(f"gu_loaded{i}") for i in range(2)]
        down_loaded = [sem(f"down_loaded{i}") for i in range(2)]
        w2_loaded = [sem(f"w2_loaded{i}") for i in range(2)]
        w_first, w_loaded, w_high, w_low = ([sem(f"w_{n}{u}") for u in range(5)] for n in ("first", "loaded", "high", "low"))
        x3_high, x3_low, o_high = sem("x3_high"), sem("x3_low"), sem("o_high")
        k_loaded, v_loaded = ([sem(f"{n}_loaded{i}") for i in range(2)] for n in "kv")
        stored, passed = sem("stored"), sem("passed")
        pool_step, dve_step = sem("pool_step"), sem("dve_step")
        consts_ready, sin_ready, angle_ready, tables_ready = sem("consts_ready"), sem("sin_ready"), sem("angle_ready"), sem("tables_ready")
        logits_ready, gap_ready, gap_exp, gates_ready = sem("logits_ready"), sem("gap_ready"), sem("gap_exp"), sem("gates_ready")
        h0_ready, h0_copied, gate_t, h_ready, l0_out, x1_ready = (
            sem("h0_ready"), sem("h0_copied"), sem("gate_t"), sem("h_ready"), sem("l0_out"), sem("x1_ready"))
        t_full, t_ready, td_full, td_ready = sem("t_full"), sem("t_ready"), sem("td_full"), sem("td_ready")
        rows_laid = sem("rows_laid")
        x1_high, x1_low, gu_high, gu_low = sem("x1_high"), sem("x1_low"), sem("gu_high"), sem("gu_low")
        slice_ready, gate_done, up_done, exp_g, silu_step, act_ready = (
            sem("slice_ready"), sem("gate_done"), sem("up_done"), sem("exp_g"), sem("silu_step"), sem("act_ready"))
        l1_out, x2_ready = sem("l1_out"), sem("x2_ready")
        l2_out, x3_summed, x3_turned, acc_ready = (
            sem("l2_out"), sem("x3_summed"), sem("x3_turned"), sem("acc_ready"))
        mask_ready = sem("mask_ready")
        tables_stored = sem("tables_stored")
        x3_stored, x3_loaded, turn_loaded = ([sem(f"{n}{i}") for i in range(2)] for n in ("x3_stored", "x3_loaded", "turn_loaded"))
        kc_high, kc_low, vc_high, vc_low = sem("kc_high"), sem("kc_low"), sem("vc_high"), sem("vc_low")
        vn_high, vn_low, q_low = sem("vn_high"), sem("vn_low"), sem("q_low")
        kv_projected, q_projected = sem("kv_projected"), sem("q_projected")
        squared, ms_ready, rstd_ready = sem("squared"), sem("ms_ready"), sem("rstd_ready")
        k_raw_ready, q_raw_ready, k_read, k_roped, q_sine, q_roped = sem("k_raw_ready"), sem("q_raw_ready"), sem("k_read"), sem("k_roped"), sem("q_sine"), sem("q_roped")
        q_cosine = sem("q_cosine")
        k_turned, k_taken, q_turned, q_taken = sem("k_turned"), sem("k_taken"), sem("q_turned"), sem("q_taken")
        scored, masked, exp_done, rden_ready, prob_ready = (
            sem("scored"), sem("masked"), sem("exp_done"), sem("rden_ready"), sem("prob_ready"))
        pt_full, pt_high, pt_low, pv_done = sem("pt_full"), sem("pt_high"), sem("pt_low"), sem("pv_done")
        o_taken, out_projected, out_added = sem("o_taken"), sem("out_projected"), sem("out_added")

        def wait(eng, s, v):
            if not (isinstance(v, int) and v <= 0):
                eng.wait_ge(s, v)

        def settle(eng, n):
            if not isinstance(n, int):
                eng.sem_inc(passed)

        def over_steps(eng, step):
            step(0, 0, 0, 0)
            step(1, 1, 1, 0)
            with eng.Fori(1, NB // 2 - 1) as c:
                step(2 * c, 0, None, 0)
                step(2 * c + 1, 1, None, 0)
            with eng.Fori(1, BLOCKS) as k:
                for phase in range(-2, 2):
                    step(NB * k + phase, phase % 2, phase, k)
                with eng.Fori(1, NB // 2 - 1) as c:
                    step(NB * k + 2 * c, 0, None, k)
                    step(NB * k + 2 * c + 1, 1, None, k)
            step(STEPS - 2, 0, None, BLOCKS)
            step(STEPS - 1, 1, None, BLOCKS)

        def over_hidden(eng, tile):
            tile(0, 0)
            tile(1, 1)
            with eng.Fori(1, FT // 2) as c:
                tile(2 * c, 0)
                tile(2 * c + 1, 1)
            tile(FT - 1, 0)

        def over_batches(eng, batch):
            batch(0, 0)
            batch(1, 1)
            with eng.Fori(1, NB // 2) as c:
                batch(2 * c, 0)
                batch(2 * c + 1, 1)

        def load_weights(eng, u, k):
            used, value = {W_KV: (kv_projected, NB * k), W_Q[0]: (q_projected, 2 * NB * k - 1),
                           W_Q[1]: (q_projected, 2 * NB * k), W_O[0]: (out_projected, 2 * NB * k - 1),
                           W_O[1]: (out_projected, 2 * NB * k)}[u]
            wait(eng, used, value)
            settle(eng, k)
            if u == W_KV:
                src = a["wkv"][ds(k, 1)]
            elif u in W_Q:
                src = a["wq"][ds(k, 1)][:, :, :, (u - W_Q[0]) * REP * DH:(u - W_Q[0] + 1) * REP * DH]
            else:
                src = a["wo"][ds(k, 1)][:, :, (u - W_O[0]) * REP:(u - W_O[0] + 1) * REP]
            loaded = w_first[u] if isinstance(k, int) and k == 0 else w_loaded[u]
            eng.dma_start(w_raw[u][:], src.rearrange("o p k n -> (o p) k n")).then_inc(loaded, 16)

        def split_tokens(b, par):
            return x_hl[par] if isinstance(b, int) and b < 2 else x_split[par]

        def more(n, ahead):
            return not isinstance(n, int) or n + ahead < STEPS

        SPLITS = {
            (-2, 0): ((), (), ((W_KV, 0),), ((W_KV, 1),)),
            (-2, 1): (((W_KV, 2),), ((W_KV, 3),), ((W_Q[0], 0), (W_Q[0], 1)), ((W_Q[0], 2), (W_Q[0], 3))),
            (-1, 0): ((), ((W_Q[1], 0),), ((W_Q[1], 1),), ((W_Q[1], 2), (W_Q[1], 3))),
            (0, 0): tuple(((W_O[0], c),) for c in range(KD)),
            (0, 1): ((), ((W_O[1], 0),), ((W_O[1], 1),), ((W_O[1], 2), (W_O[1], 3))),
        }

        def splits(phase, s):
            return SPLITS.get((phase, s), ((), (), (), ()))

        def key_tile(t):
            return (t - 1) % KT

        block = ctx.enter_context(nc.Block())

        @block.sync
        def _(sp):
            sp.dma_start(ids[:], a["ids"]).then_inc(rows_loaded, 16)
            for dst, name in ((wr, "wr"), (a0, "a0")):
                sp.dma_start(dst[:], a[name]).then_inc(l0_small_loaded, 16)
            for hf in range(2):
                sp.dma_start(xa[:, :, hf * HALF:(hf + 1) * HALF], a["x"][:, :, hf * HALF:(hf + 1) * HALF]
                             ).then_inc(x_loaded[hf], 16)
            for dst, name in ((w0, "w0"), (b0, "b0")):
                sp.dma_start(dst[:], a[name]).then_inc(l0_loaded, 16)
            sp.wait_ge(rows_loaded, 16)
            for b in range(NB):
                row = sp.value_load(ids[0:1, b:b + 1], min_val=0, max_val=15)
                for name, dst in a_raw.items():
                    sp.dma_start(dst[:, b], a[name][ds(row, 1)].rearrange("o p k r -> (o p) k r")).then_inc(lora_loaded, 16)
                for dst, name in ((b_gate, "b_gate"), (b_up, "b_up"), (b_down, "b_down")):
                    sp.dma_start(dst[b * R:(b + 1) * R, :],
                                 a[name][ds(row, 1)].rearrange("o r f -> (o r) f")).then_inc(lora_loaded, 16)

            def load_gu(f, par):
                wait(sp, up_done, 2 * f - 2)
                sp.dma_start(w_gu[par][:], a["w_gu"][ds(f, 1)].rearrange("o p g k n -> (o p) g k n")
                             ).then_inc(gu_loaded[par], 16)

            load_gu(0, 0)
            load_gu(1, 1)
            load_weights(sp, W_KV, 0)
            load_weights(sp, W_Q[0], 0)
            with sp.Fori(1, FT // 2) as c:
                load_gu(2 * c, 0)
                load_gu(2 * c + 1, 1)
            load_gu(FT - 1, 0)
            def load_w2(b, par):
                wait(sp, l2_out, b - 1)
                row = sp.value_load(ids[0:1, ds(NB + b, 1)], min_val=0, max_val=15)
                sp.dma_start(w2[par][:], a["w2"][ds(row, 1)].rearrange("o p k n -> (o p) k n")
                             ).then_inc(w2_loaded[par], 16)

            def load_cache(m, par, keys=True, values=True):
                if keys:
                    wait(sp, kc_low, 2 * m - 2)
                    settle(sp, m)
                if values:
                    wait(sp, vc_low, 2 * m - 2)
                    settle(sp, m)
                b, k = m % NB, m // NB
                for j in range(NPAGE):
                    page = sp.value_load(ids[0:1, ds(2 * NB + b * NPAGE + j, 1)], min_val=0, max_val=63)
                    if keys:
                        sp.dma_start(kc[par][:, j], a["k_cache"][ds(page, 1), ds(k, 1)].rearrange("g o d s t -> (g o d) s t")
                                     ).then_inc(k_loaded[par], 16)
                    if values:
                        q = j % 4 * PAGE
                        sp.dma_start(vc[par][q:q + PAGE, j // 4], a["v_cache"][ds(page, 1), ds(k, 1)].rearrange(
                            "g o t n -> (g o t) n")).then_inc(v_loaded[par], 16)

            sp.wait_ge(slice_ready, 1)
            for o in range(KD):
                wait(sp, l1_out, 2 * (o - 1))
                sp.dma_start(w_down[o % 2][:], a["w_down"][o]).then_inc(down_loaded[o % 2], 16)
                if o == 1:
                    sp.wait_ge(act_ready, 2 * FT)
                    load_w2(0, 0)
                    load_w2(1, 1)
                    load_cache(0, 0, keys=False)
            sp.wait_ge(l1_out, 2 * (KD - 1))
            load_cache(0, 0, values=False)
            with sp.Fori(1, NB // 2 - 1) as c:
                load_w2(2 * c, 0)
                load_w2(2 * c + 1, 1)
            sp.wait_ge(l1_out, 2 * KD)
            load_weights(sp, W_Q[1], 0)
            load_w2(NB - 2, 0)
            load_w2(NB - 1, 1)

            sp.wait_ge(tables_stored, 64)

            def load_step(m, par):
                wait(sp, q_roped, 2 * m - 2)
                settle(sp, m)
                b = m % NB
                sp.dma_start(turn[par][:], turn_dram[ds(b, 1)].rearrange("o p f d -> (o p) f d")).then_inc(turn_loaded[par], 16)
                if not (isinstance(m, int) and m < 1):
                    load_cache(m, par)

            load_step(0, 0)
            load_weights(sp, W_O[0], 0)
            load_weights(sp, W_O[1], 0)
            for i in range(2):
                sp.wait_ge(x3_stored[i], 16 * NB // 2)
            load_step(1, 1)
            with sp.Fori(1, STEPS // 2) as c:
                load_step(2 * c, 0)
                load_step(2 * c + 1, 1)
            sp.wait_ge(out_added, GROUPS)
            sp.dma_start(out, acc[:]).then_inc(stored, 16)
            sp.wait_ge(stored, 16)

        @block.gpsimd
        def _(pool):
            for dst, name in ((len_i, "lens"), (lang_i, "lang")):
                pool.dma_start(dst[:], a[name].partition_broadcast(P)).then_inc(ids_loaded, 16)
            pool.dma_start(inv_f[:], a["inv_f"].partition_broadcast(P)).then_inc(ids_loaded, 16)
            pool.dma_start(norm_w[:, 0, :], a["q_norm"].partition_broadcast(P)).then_inc(ids_loaded, 16)
            pool.dma_start(norm_w[:, 1, :], a["k_norm"].partition_broadcast(P)).then_inc(ids_loaded, 16)
            pool.iota(iota[:], [[1, CACHED]], base=0, channel_multiplier=0, allow_small_or_imprecise_dtypes=True)
            pool.iota(lang[:], [[0, NB], [1, E]], base=0, channel_multiplier=0, allow_small_or_imprecise_dtypes=True)
            pool.iota(pos[:], [[0, NB]], base=0, channel_multiplier=1, allow_small_or_imprecise_dtypes=True)
            pool.memset(neghalf[:], -0.5)
            for i in range(2):
                pool.memset(mask[i][:, CACHED:KEYS], 0.0)
            pool.memset(own[:], 0.5)
            pool.memset(ident[:], 0.0).then_inc(pool_step, 1)
            pool.wait_ge(pool_step, 1)
            pool.affine_select(out=ident[:], in_=ident[:], compare_op=ALU.not_equal, fill=1.0, base=0,
                               pattern=[[-1, P]], channel_multiplier=1)
            pool.affine_select(out=own[:], in_=own[:], compare_op=ALU.is_ge, fill=0.0, base=0,
                               pattern=[[-R, NB]], channel_multiplier=1).then_inc(pool_step, 1)
            pool.wait_ge(pool_step, 2)
            pool.affine_select(out=own[:], in_=own[:], compare_op=ALU.is_ge, fill=0.0, base=R - 1,
                               pattern=[[R, NB]], channel_multiplier=-1).then_inc(consts_ready, 1)

            def b_slices(f, par):
                wait(pool, up_done, 2 * f - 2)
                pool.tensor_copy(b_now[par][:, 0], b_gate[:, ds(f * P, P)])
                pool.tensor_copy(b_now[par][:, 1], b_up[:, ds(f * P, P)]).then_inc(slice_ready, 1)

            pool.wait_ge(lora_loaded, 16 * 6 * NB)
            for name, dst in (("a_gate", a_gate), ("a_up", a_up), ("a_down", a_down)):
                pool.tensor_scalar(dst[:].rearrange("p k (b r) -> p k b r", r=R),
                                   a_raw[name][:].rearrange("p b k r -> p k b r"),
                                   1.0, 1.0, ALU.mult, ALU.mult).then_inc(rows_laid, 1)
            over_hidden(pool, b_slices)

            def rstd_k(m):
                pool.wait_ge(squared, 10 * m + 2)
                wait(pool, rstd_ready, 3 * m)
                settle(pool, m)
                pool.tensor_scalar(ms[:, 0:HB], ss_k[:], 1.0 / DH, EPS, ALU.mult, ALU.add).then_inc(ms_ready, 1)
                pool.wait_ge(ms_ready, 5 * m + 1)
                pool.tensor_tensor(rs_k[:], ms[:, 0:HB], neghalf[:, 0:HB], ALU.pow).then_inc(rstd_ready, 1)

            def rstd_q(m, s):
                pool.wait_ge(squared, 10 * m + 6 + 4 * s)
                pool.wait_ge(rstd_ready, 3 * m + 1 + s)
                if s == 0 or not isinstance(m, int) or m > 0:
                    wait(pool, masked, 8 * m + 4 * s - 4)
                settle(pool, m)
                pool.tensor_scalar(ms[:], ss_q[:, s], 1.0, DH * EPS, ALU.mult, ALU.add).then_inc(ms_ready, 1)
                pool.wait_ge(ms_ready, 5 * m + 2 + 2 * s)
                pool.tensor_tensor(ms[:], ms[:], neghalf[:], ALU.pow).then_inc(ms_ready, 1)
                pool.wait_ge(ms_ready, 5 * m + 3 + 2 * s)
                settle(pool, m)
                pool.tensor_scalar(rs_q[:, s], ms[:], -1.0, 1.0, ALU.mult, ALU.mult).then_inc(rstd_ready, 1)

            def sine_q(m, par, s):
                pool.wait_ge(q_raw_ready, 2 * m + s + 1)
                if s == 0:
                    pool.wait_ge(turn_loaded[par], 16 * (m // 2 + 1))
                wait(pool, q_roped, 2 * m + s)
                settle(pool, m)
                pool.tensor_tensor(part_s[:], q_raw[:], turn[par][:, 1:2, :].to_broadcast([P, REP, DH]), ALU.mult
                                   ).then_inc(q_sine, 1)

            def scale_probs(j, s, h):
                pool.wait_ge(rden_ready, 4 * j + h + 1)
                settle(pool, j)
                pool.tensor_scalar(prob[s][:, h], prob[s][:, h], rden[:, s, h:h + 1], 1.0, ALU.mult, ALU.mult
                                   ).then_inc(prob_ready, 1)

            def low_k(m, par, s):
                pool.wait_ge(kc_high, 2 * m + s + 1)
                wait(pool, scored, 8 * m + 4 * s - 4)
                pool.tensor_tensor(k_l[s][:], kc[par][:, :, s, :], k_h[s][:].bitcast(F32), ALU.subtract).then_inc(kc_low, 1)

            def low_v(m, par, s):
                pool.wait_ge(vc_high, 2 * m + s + 1)
                wait(pool, pv_done, KT * (2 * m + s - 1))
                pool.tensor_tensor(v_l[s][:], vc[par][:, :, s * DH:(s + 1) * DH], v_h[s][:].bitcast(F32), ALU.subtract
                                   ).then_inc(vc_low, 1)

            def load_tokens(m, par):
                wait(pool, q_projected, 2 * m - 2)
                settle(pool, m)
                pool.dma_start(x_hl[par][:], x3_dram[ds(m % NB, 1)].rearrange("o p h k t -> (o p) h k t")
                               ).then_inc(x3_loaded[par], 16)

            low_k(0, 0, 0)
            low_k(0, 0, 1)
            rstd_k(0)
            sine_q(0, 0, 0)
            rstd_q(0, 0)
            sine_q(0, 0, 1)
            rstd_q(0, 1)
            low_v(0, 0, 0)
            for i in range(2):
                pool.wait_ge(x3_stored[i], 16 * NB // 2)
            for h in range(REP - 1):
                scale_probs(0, 0, h)

            LOADS = {(-2, 1, 0): W_KV, (-2, 1, 2): W_Q[0], (-2, 0, 2): W_Q[1], (-1, 0, 1): W_O[0], (0, 1, 1): W_O[1]}

            def next_weights(phase, s, point, blk):
                if (phase, s, point) in LOADS and not (isinstance(blk, int) and blk == 0):
                    load_weights(pool, LOADS[phase, s, point], blk)

            def half(j, s, v, k, phase, blk):
                next_weights(phase, s, 0, blk)
                scale_probs(j - 1, 1 - s, REP - 1)
                if v is None:
                    return
                if k and s == 1:
                    rstd_k(k[0])
                low_v(*v)
                scale_probs(j, s, 0)
                next_weights(phase, s, 1, blk)
                if k:
                    sine_q(*k)
                    low_k(*k)
                scale_probs(j, s, 1)
                if k:
                    rstd_q(k[0], k[2])
                next_weights(phase, s, 2, blk)
                scale_probs(j, s, 2)

            def step(n, par, phase, k):
                last = not more(n, 1)
                m, j = n + 1, 2 * n + 1
                if more(n, 2):
                    load_tokens(n + 2, par)
                half(j, 1, (n, par, 1), (m, 1 - par, 0) if not last else None, phase, k)
                half(j + 1, 0, (m, 1 - par, 0) if not last else None, (m, 1 - par, 1) if not last else None, phase, k)

            over_steps(pool, step)

        @block.tensor
        def _(pe):
            pe.wait_ge(l0_small_loaded, 32)
            for hf in range(2):
                pe.wait_ge(x_loaded[hf], 16)
                for b in range(4 * hf, 4 * hf + 4):
                    for k in range(KD):
                        mm = pe.matmul(ps[:, 6, b * E:(b + 1) * E], xa[:, k, b * T:(b + 1) * T], wr[:, k],
                                       start=k == 0, stop=k == KD - 1)
                if hf == 1:
                    mm.then_inc(logits_ready, 1)
                for k in range(KD):
                    mm = pe.matmul(ps[:, hf], a0[:, k], xa[:, k, hf * HALF:(hf + 1) * HALF],
                                   start=k == 0, stop=k == KD - 1)
                mm.then_inc(h0_ready, 1)

            def base(n):
                hf, o = n // KD, n % KD
                wait(pe, x1_ready, n - 1)
                for k in range(KD):
                    pe.matmul(ps[:, 4 + n % 2], w0[:, k, o * P:(o + 1) * P], xa[:, k, hf * HALF:(hf + 1) * HALF],
                              start=k == 0, stop=False)

            def low_rank(n):
                hf, o = n // KD, n % KD
                pe.wait_ge(h_ready, hf + 1)
                pe.matmul(ps[:, 4 + n % 2], b0[:, o * P:(o + 1) * P], h_gated[:, hf * HALF:(hf + 1) * HALF],
                          start=False, stop=True).then_inc(l0_out, 1)

            pe.wait_ge(l0_loaded, 32)
            base(0)
            base(1)
            pe.wait_ge(gates_ready, 1)
            pe.wait_ge(consts_ready, 1)
            for hf in range(2):
                for b in range(4 * hf, 4 * hf + 4):
                    mm = pe.transpose(ps[:, 2 + hf, b % 4 * T:(b % 4 + 1) * T], gate_x[:, b], ident[:])
                mm.then_inc(gate_t, 1)
            low_rank(0)
            low_rank(1)
            for n in range(2, 2 * KD):
                base(n)
                low_rank(n)

            pe.wait_ge(rows_laid, 3)
            pe.wait_ge(x1_ready, 2 * KD)
            for w, bank in ((a_gate, 4), (a_up, 6)):
                for hf in range(2):
                    for k in range(KD):
                        mm = pe.matmul(ps[:, bank + hf], w[:, k], xb[:, k, hf * HALF:(hf + 1) * HALF],
                                       start=k == 0, stop=k == KD - 1)
                    mm.then_inc(t_full, 1)
            pe.wait_ge(t_ready, 4)
            pe.wait_ge(x1_low, 2)

            def split_products(to, operands, first=True, last=True):
                for n, (ah, al, bh, bl) in enumerate(operands):
                    pe.matmul(to, ah, bh, start=first and n == 0, stop=False)
                    pe.matmul(to, ah, bl, start=False, stop=False)
                    mm = pe.matmul(to, al, bh, start=False, stop=last and n == len(operands) - 1)
                return mm

            def gate_up(f, par):
                pe.wait_ge(gu_low, f + 1)
                pe.wait_ge(slice_ready, f + 1)
                for hf in range(2):
                    wait(pe, act_ready, 2 * f + hf - 1)
                    for g, t, done in ((0, t_gate, gate_done), (1, t_up, up_done)):
                        half = slice(hf * HALF, (hf + 1) * HALF)
                        split_products(ps[:, 2 * g + hf],
                                       [(gu_h[par][:, g, k], gu_l[par][:, g, k], x1_h[:, k, half], x1_l[:, k, half])
                                        for k in range(KD)], last=False)
                        pe.matmul(ps[:, 2 * g + hf], b_now[par][:, g], t[:, hf * HALF:(hf + 1) * HALF],
                                  start=False, stop=True).then_inc(done, 1)

            over_hidden(pe, gate_up)
            pe.wait_ge(act_ready, 2 * FT)
            for hf in range(2):
                for f in range(FT):
                    mm = pe.matmul(ps[:, 4 + hf], a_down[:, f], act[:, f, hf * HALF:(hf + 1) * HALF],
                                   start=f == 0, stop=f == FT - 1)
                mm.then_inc(td_full, 1)
            for o in range(KD):
                pe.wait_ge(down_loaded[o % 2], 16 * (o // 2 + 1))
                for hf in range(2):
                    n = 2 * o + hf
                    wait(pe, x2_ready, n - 3)
                    for f in range(FT):
                        pe.matmul(ps[:, n % 4], w_down[o % 2][:, f], act[:, f, hf * HALF:(hf + 1) * HALF],
                                  start=f == 0, stop=False)
                    pe.wait_ge(td_ready, hf + 1)
                    pe.matmul(ps[:, n % 4], b_down[:, o * P:(o + 1) * P], t_down[:, hf * HALF:(hf + 1) * HALF],
                              start=False, stop=True).then_inc(l1_out, 1)

            pe.wait_ge(x2_ready, 2 * KD)

            def adapter(b, par):
                pe.wait_ge(w2_loaded[par], 16 * (b // 2 + 1))
                wait(pe, x3_summed, b - 1)
                for o in range(KD):
                    for k in range(KD):
                        mm = pe.matmul(ps[:, 4 + par, o * T:(o + 1) * T], w2[par][:, k, o * P:(o + 1) * P],
                                       xa[:, k, ds(b * T, T)], start=k == 0, stop=k == KD - 1)
                mm.then_inc(l2_out, 1)

            def turn_x(b, par):
                pe.wait_ge(x3_summed, b + 1)
                wait(pe, acc_ready, b - 1)
                for k in range(KD):
                    mm = pe.transpose(ps[:, 6 + par, k * P:(k + 1) * P], x_sum[par][:, k], ident[:])
                mm.then_inc(x3_turned, 1)

            def layer2(b, par):
                adapter(b, par)
                if not (isinstance(b, int) and b == 0):
                    turn_x(b - 1, 1 - par)

            over_batches(pe, layer2)
            turn_x(NB - 1, 1)

            pe.wait_ge(acc_ready, NB)

            def project_kv(m, par, new=None):
                if new is not None:
                    pe.wait_ge(w_low[W_KV], KD * new + KD)
                if isinstance(m, int) and m < 2:
                    pe.wait_ge(x3_low, m + 1)
                else:
                    pe.wait_ge(x3_loaded[par], 16 * (m // 2))
                wait(pe, q_taken, 2 * m)
                u = W_KV
                mm = split_products(ps[:, PJ], [(x_h[par][:, k], x_l[par][:, k], w_h[u][:, k], w_l[u][:, k])
                                                for k in range(KD)])
                mm.then_inc(kv_projected, 1)

            def project_q(m, par, s, new, k0, k1):
                u = W_Q[s]
                if k0 == 0:
                    if new is not None:
                        pe.wait_ge(w_low[u], KD * new + KD)
                    if s == 0 and isinstance(m, int) and m < 2:
                        pe.wait_ge(k_raw_ready, m + 1)
                        pe.wait_ge(vn_low, m + 1)
                    wait(pe, out_added, 2 * m - 2 + s)
                    if isinstance(m, int) and m == 0 and s == 1:
                        pe.wait_ge(k_taken, 1)
                mm = split_products(ps[:, PJ], [(x_h[par][:, k], x_l[par][:, k], w_h[u][:, k], w_l[u][:, k])
                                                for k in range(k0, k1)], k0 == 0, k1 == KD)
                if k1 == KD:
                    mm.then_inc(q_projected, 1)

            def turn_k(m):
                pe.wait_ge(q_taken, 2 * m + 1)
                pe.wait_ge(k_roped, m + 1)
                for s in range(HB):
                    mm = pe.transpose(ps[:, PJ, s * T:(s + 1) * T], k_rot[:, s], ident[:])
                mm.then_inc(k_turned, 1)

            def turn_q(m, s):
                pe.wait_ge(q_raw_ready, 2 * m + s + 1)
                pe.wait_ge(q_roped, 2 * m + s + 1)
                for h in range(REP):
                    mm = pe.transpose(ps[:, PJ, h * T:(h + 1) * T], q_rot[:, h], ident[:])
                mm.then_inc(q_turned, 1)

            def score(j, m, par, s, h):
                if h == 0:
                    pe.wait_ge(q_low, j + 1)
                    pe.wait_ge(kc_low, j + 1)
                wait(pe, exp_done, 4 * j + h - 1)
                slot = h % 2
                to = s_ps[:, slot, 0:CACHED]
                pe.matmul(to, q_h[s][:, h], k_h[s][:].rearrange("p j t -> p (j t)"), start=True, stop=False)
                pe.matmul(to, q_h[s][:, h], k_l[s][:].rearrange("p j t -> p (j t)"), start=False, stop=False)
                pe.matmul(to, q_l[s][:, h], k_h[s][:].rearrange("p j t -> p (j t)"), start=False, stop=True)
                if h == 0 and s == 0:
                    pe.wait_ge(k_taken, m + 1)
                pe.matmul(s_ps[:, slot, CACHED:KEYS], q_t[s][:, h], k_new[par][:, s], start=True, stop=True
                          ).then_inc(scored, 1)

            def turn_probs(i, s, t):
                wait(pe, pt_low, KT * i + t - 1)
                c = key_tile(t) * P
                for h in range(REP):
                    if t == 0:
                        pe.wait_ge(prob_ready, 4 * i + h + 1)
                    mm = pe.transpose(ps[:, PT[(s + t) % 2], h * T:(h + 1) * T], prob[s][:, h, c:c + P], ident[:])
                mm.then_inc(pt_full, 1)

            def weigh(i, m, par, s, t):
                if t == 0:
                    wait(pe, o_taken, i)
                    pe.wait_ge(vn_low, m + 1)
                    vh, vl = vn_h[par][:, s], vn_l[par][:, s]
                else:
                    if t == 1:
                        pe.wait_ge(vc_low, i + 1)
                    vh, vl = v_h[s][:, key_tile(t)], v_l[s][:, key_tile(t)]
                x = (s + t) % 2
                pe.wait_ge(pt_high, KT * i + t + 1)
                pe.matmul(ps[:, OB], vh, pt_h[x][:], start=t == 0, stop=False)
                pe.matmul(ps[:, OB], vl, pt_h[x][:], start=False, stop=False)
                pe.wait_ge(pt_low, KT * i + t + 1)
                pe.matmul(ps[:, OB], vh, pt_l[x][:], start=False, stop=t == KT - 1).then_inc(pv_done, 1)

            def project_out(i, s, new, *before):
                u = W_O[s]
                if new is not None:
                    pe.wait_ge(w_low[u], KD * new + KD)
                pe.wait_ge(o_taken, i + 1)
                for semaphore, value in before:
                    pe.wait_ge(semaphore, value)
                mm = split_products(ps[:, PJ], [(o_h[:, h], o_l[:, h], w_h[u][:, h], w_l[u][:, h])
                                                for h in range(REP)])
                mm.then_inc(out_projected, 1)

            project_kv(0, 0, 0)
            project_q(0, 0, 0, 0, 0, KD)
            turn_q(0, 0)
            turn_k(0)
            project_q(0, 0, 1, 0, 0, KD)
            turn_q(0, 1)
            project_kv(1, 1)
            for h in range(REP):
                score(0, 0, 0, 0, h)

            def half(i, n, par, s, scores, queries, out_rows, keys=None):
                if scores:
                    score(*scores, 0)
                if out_rows:
                    project_out(*out_rows)
                turn_probs(i, s, 0)
                turn_probs(i, s, 1)
                if scores:
                    score(*scores, 1)
                if queries:
                    project_q(*queries, 0, 2)
                weigh(i, n, par, s, 0)
                turn_probs(i, s, 2)
                if queries:
                    project_q(*queries, 2, KD)
                weigh(i, n, par, s, 1)
                turn_probs(i, s, 3)
                weigh(i, n, par, s, 2)
                turn_probs(i, s, 4)
                if scores:
                    score(*scores, 2)
                if queries:
                    turn_q(queries[0], s)
                weigh(i, n, par, s, 3)
                weigh(i, n, par, s, 4)
                if queries and s == 0:
                    turn_k(queries[0])
                if keys:
                    project_kv(*keys)
                if scores:
                    score(*scores, 3)

            def step(n, par, phase, k):
                last = not more(n, 1)
                i, m = 2 * n, n + 1
                first = isinstance(n, int) and n == 0
                if more(n, 1):
                    kv_read = ((k_raw_ready, n + 2), (vn_low, n + 2))
                    k_read_out = ((k_taken, n + 2),)
                else:
                    kv_read = ((q_taken, 2 * n + 2),)
                    k_read_out = ((out_added, 2 * n),)
                new_q, new_kv = (k if phase == p else None for p in (-1, -2))
                new_o = [k if phase == p else None for p in (0, 1)]
                half(i, n, par, 0, (i + 1, n, par, 1), (m, 1 - par, 0, new_q) if not last else None,
                     (i - 1, 1, new_o[1]) + kv_read if not first else None)
                half(i + 1, n, par, 1, (i + 2, m, 1 - par, 0) if not last else None,
                     (m, 1 - par, 1, new_q) if not last else None, (i, 0, new_o[0]) + k_read_out,
                     (n + 2, par, new_kv) if more(n, 2) else None)

            over_steps(pe, step)
            project_out(GROUPS - 1, 1, None, (out_added, GROUPS - 1))

        @block.scalar
        def _(act_e):
            for i in range(2):
                act_e.wait_ge(angle_ready, i + 1)
                act_e.activation(trig[:, i], red[:], ACT.Sin).then_inc(sin_ready, 1)
            act_e.wait_ge(tables_ready, 2)
            for i, table in enumerate(tables):
                act_e.dma_start(turn_dram[:, :, i].rearrange("b p d -> p b d"), table[:]).then_inc(tables_stored, 16)
            for hf in range(2):
                act_e.wait_ge(h0_ready, hf + 1)
                act_e.copy(h_sb[:, hf * HALF:(hf + 1) * HALF], ps[:, hf]).then_inc(h0_copied, 1)
            act_e.wait_ge(gap_ready, 1)
            act_e.activation(e_gap[:], gap[:], ACT.Exp).then_inc(gap_exp, 1)

            act_e.wait_ge(x1_ready, 2 * KD)
            for hf in range(2):
                half = slice(hf * HALF, (hf + 1) * HALF)
                act_e.copy(x1_h[:, :, half], xb[:, :, half]).then_inc(x1_high, 1)

            def split_gu(f, par):
                act_e.wait_ge(gu_loaded[par], 16 * (f // 2 + 1))
                act_e.copy(gu_h[par][:], w_gu[par][:]).then_inc(gu_high, 1)

            split_gu(0, 0)

            def exp_gate(f, par):
                for hf in range(2):
                    if hf == 1 and not (isinstance(f, int) and f == FT - 1):
                        split_gu(f + 1, 1 - par)
                    u = 2 * f + hf
                    act_e.wait_ge(gate_done, u + 1)
                    wait(act_e, act_ready, u - 1)
                    act_e.activation(sil[hf][:], ps[:, hf], ACT.Exp, scale=-1.0).then_inc(exp_g, 1)

            over_hidden(act_e, exp_gate)

            def split_piece(u, c, k):
                if isinstance(k, int) and k == 0:
                    act_e.wait_ge(w_first[u], 16)
                else:
                    act_e.wait_ge(w_loaded[u], 16 * k)
                act_e.copy(w_h[u][:, c], w_raw[u][:, c]).then_inc(w_high[u], 1)

            def split_weights(u, k):
                for c in range(KD):
                    split_piece(u, c, k)

            def keep_x(b, par):
                act_e.wait_ge(x3_summed, b + 1)
                wait(act_e, x3_stored[par], 16 * (b // 2))
                act_e.copy(split_tokens(b, par)[:, 0], x_sum[par][:]).then_inc(x3_high, 1)
                act_e.wait_ge(x3_low, b + 1)
                act_e.dma_start(x3_dram[ds(b, 1)].rearrange("o p h k t -> (o p) h k t"),
                                split_tokens(b, par)[:].bitcast(F32)).then_inc(x3_stored[par], 16)
                act_e.wait_ge(x3_turned, b + 1)
                act_e.copy(acc[:, ds(b, 1), :].rearrange("p o n -> p (o n)"), ps[:, 6 + par]).then_inc(acc_ready, 1)

            split_weights(W_KV, 0)
            split_weights(W_Q[0], 0)
            over_batches(act_e, keep_x)

            def square(done, src, heads, dst):
                for h in range(heads):
                    wait(act_e, squared, done + h - 1)
                    act_e.activation(junk[:, h % 2], src[:, h], ACT.Square, accum_out=dst[:, h:h + 1]).then_inc(squared, 1)

            def take_kv(m, par):
                act_e.wait_ge(kv_projected, m + 1)
                wait(act_e, pv_done, KT * (2 * m - 3) + 1)
                act_e.copy(vn_h[par][:], ps[:, PJ, HB * DH:2 * HB * DH]).then_inc(vn_high, 1)
                wait(act_e, k_read, m)
                act_e.copy(k_raw[:], ps[:, PJ, 0:HB * DH]).then_inc(k_raw_ready, 1)
                act_e.wait_ge(k_raw_ready, m + 1)
                square(10 * m, k_raw, HB, ss_k[:])

            def take_raw_q(m, s):
                act_e.wait_ge(q_projected, 2 * m + s + 1)
                wait(act_e, q_roped, 2 * m + s)
                act_e.copy(q_raw[:], ps[:, PJ]).then_inc(q_raw_ready, 1)

            def square_q(m, s):
                act_e.wait_ge(q_raw_ready, 2 * m + s + 1)
                square(10 * m + 2 + 4 * s, q_raw, REP, ss_q[:, s])

            def take_k(m, par):
                act_e.wait_ge(k_turned, m + 1)
                wait(act_e, scored, 8 * m - 8)
                act_e.copy(k_new[par][:], ps[:, PJ, 0:HB * T]).then_inc(k_taken, 1)

            def take_q(m, s):
                act_e.wait_ge(q_turned, 2 * m + s + 1)
                wait(act_e, scored, 8 * m + 4 * s - 4)
                act_e.copy(q_h[s][:], ps[:, PJ])
                act_e.copy(q_t[s][:], ps[:, PJ]).then_inc(q_taken, 1)

            def exp_scores(j, s, h):
                act_e.wait_ge(masked, 4 * j + h + 1)
                if h == 0:
                    wait(act_e, pt_full, KT * (j - 1))
                act_e.activation(prob[s][:, h], s_ps[:, h % 2, 0:KEYS], ACT.Exp, bias=negmax[:, s, h:h + 1], scale=-1.0,
                                 accum_out=den[:, s, h:h + 1]).then_inc(exp_done, 1)

            def high_probs(i, s, t):
                act_e.wait_ge(pt_full, KT * i + t + 1)
                wait(act_e, pv_done, KT * i + t - 1)
                act_e.copy(pt_h[(s + t) % 2][:], ps[:, PT[(s + t) % 2]]).then_inc(pt_high, 1)

            def high_k(m, par, s):
                act_e.wait_ge(k_loaded[par], 16 * NPAGE * (m // 2 + 1))
                wait(act_e, scored, 8 * m + 4 * s - 4)
                act_e.copy(k_h[s][:], kc[par][:, :, s, :]).then_inc(kc_high, 1)

            def high_v(m, par, s):
                act_e.wait_ge(v_loaded[par], 16 * NPAGE * (m // 2 + 1))
                wait(act_e, pv_done, KT * (2 * m + s - 1))
                act_e.copy(v_h[s][:], vc[par][:, :, s * DH:(s + 1) * DH]).then_inc(vc_high, 1)

            high_k(0, 0, 0)
            high_k(0, 0, 1)
            take_kv(0, 0)
            take_raw_q(0, 0)
            square_q(0, 0)
            take_q(0, 0)
            take_k(0, 0)
            split_weights(W_Q[1], 0)
            take_raw_q(0, 1)
            square_q(0, 1)
            take_q(0, 1)
            high_v(0, 0, 0)
            take_kv(1, 1)
            for h in range(REP):
                exp_scores(0, 0, h)

            def high_o(i):
                act_e.wait_ge(pv_done, KT * (i + 1))
                wait(act_e, out_projected, i)
                act_e.copy(o_h[:].rearrange("p h t -> p (h t)"), ps[:, OB]).then_inc(o_high, 1)

            def half(i, s, v, k, phase, blk, keys=None):
                if v:
                    exp_scores(i + 1, 1 - s, 0)
                    high_v(*v)
                high_probs(i, s, 0)
                high_probs(i, s, 1)
                if v:
                    exp_scores(i + 1, 1 - s, 1)
                for u, c in splits(phase, s)[0]:
                    split_piece(u, c, blk)
                high_probs(i, s, 2)
                for u, c in splits(phase, s)[1]:
                    split_piece(u, c, blk)
                if k:
                    high_k(*k)
                    take_raw_q(k[0], s)
                    square_q(k[0], s)
                high_probs(i, s, 3)
                for u, c in splits(phase, s)[2]:
                    split_piece(u, c, blk)
                high_probs(i, s, 4)
                if k:
                    take_q(k[0], s)
                if v:
                    exp_scores(i + 1, 1 - s, 2)
                for u, c in splits(phase, s)[3]:
                    split_piece(u, c, blk)
                high_o(i)
                if k and s == 0:
                    take_k(k[0], k[1])
                if keys:
                    take_kv(*keys)
                if v:
                    exp_scores(i + 1, 1 - s, 3)

            def step(n, par, phase, k):
                last = not more(n, 1)
                m = n + 1
                half(2 * n, 0, (n, par, 1), (m, 1 - par, 0) if not last else None, phase, k)
                half(2 * n + 1, 1, (m, 1 - par, 0) if not last else None, (m, 1 - par, 1) if not last else None,
                     phase, k, (n + 2, par) if more(n, 2) else None)

            over_steps(act_e, step)

        @block.vector
        def _(dve):
            count = [0]

            def link(ins):
                count[0] += 1
                ins.then_inc(dve_step, 1)
                dve.wait_ge(dve_step, count[0])

            def bc(x, n):
                return x.unsqueeze(2).to_broadcast([P, NB, n])

            dve.wait_ge(ids_loaded, 80)
            dve.wait_ge(consts_ready, 1)
            dve.tensor_copy(len_f[:], len_i[:])
            link(dve.tensor_copy(lang_f[:], lang_i[:]))
            link(dve.tensor_tensor(pos[:], pos[:], len_f[:], ALU.add))
            link(dve.tensor_tensor(ang[:], bc(pos[:], DH // 2), inv_f[:].unsqueeze(1).to_broadcast([P, NB, DH // 2]), ALU.mult))
            for i, (shift, quarter) in enumerate(((0.0, 0.0), (0.25, math.pi / 2))):
                link(dve.tensor_scalar(turns[:], ang[:], 1.0 / TWO_PI, shift, ALU.mult, ALU.add))
                link(dve.tensor_scalar(turns[:], turns[:], ROUND, -ROUND, ALU.add, ALU.add))
                if i == 1:
                    dve.wait_ge(sin_ready, 1)
                link(dve.scalar_tensor_tensor(out=red[:], in0=turns[:], scalar=-PI_A, in1=ang[:], op0=ALU.mult, op1=ALU.add))
                link(dve.scalar_tensor_tensor(out=red[:], in0=turns[:], scalar=-PI_B, in1=red[:], op0=ALU.mult, op1=ALU.add))
                link(dve.scalar_tensor_tensor(out=red[:], in0=turns[:], scalar=-PI_C, in1=red[:], op0=ALU.mult, op1=ALU.add))
                if i == 1:
                    link(dve.tensor_scalar(red[:], red[:], quarter, None, ALU.add))
                link(dve.tensor_scalar(red[:], red[:], 3.1415925, -3.1415925, ALU.min, ALU.max))
                dve.tensor_scalar(turns[:], turns[:], 0.0, None, ALU.mult).then_inc(angle_ready, 1)
                dve.wait_ge(angle_ready, i + 1)
            dve.wait_ge(sin_ready, 2)
            for w, (ct, st) in enumerate((tables[0:2], tables[2:4])):
                lo, hi = (norm_w[:, w, n * 64:(n + 1) * 64].unsqueeze(1).to_broadcast([P, NB, 64]) for n in range(2))
                dve.tensor_tensor(ct[:, :, 0:64], trig[:, 1], lo, ALU.mult)
                dve.tensor_tensor(ct[:, :, 64:128], trig[:, 1], hi, ALU.mult)
                dve.tensor_tensor(st[:, :, 0:64], trig[:, 0], lo, ALU.mult)
                dve.scalar_tensor_tensor(out=st[:, :, 64:128], in0=trig[:, 0], scalar=-1.0, in1=hi,
                                         op0=ALU.mult, op1=ALU.mult).then_inc(tables_ready, 1)

            link(dve.tensor_tensor(one1[:], lang[:], bc(lang_f[:], E), ALU.is_equal))
            dve.wait_ge(logits_ready, 1)
            link(dve.scalar_tensor_tensor(out=logit[:], in0=one1[:], scalar=5.0,
                                          in1=ps[:, 6, 0:NB * E].rearrange("p (b e) -> p b e", e=E),
                                          op0=ALU.mult, op1=ALU.add))
            for src, top, one in ((logit, top1, one1), (less, top2, one2)):
                link(dve.tensor_reduce(top[:], src[:], AX.X, ALU.max))
                link(dve.tensor_tensor(one[:], src[:], bc(top[:], E), ALU.is_equal))
                link(dve.scalar_tensor_tensor(out=cand[:], in0=one[:], scalar=-16.0, in1=lang[:], op0=ALU.mult, op1=ALU.add))
                link(dve.tensor_reduce(pick[:], cand[:], AX.X, ALU.min))
                link(dve.tensor_tensor(one[:], cand[:], bc(pick[:], E), ALU.is_equal))
                if one is one1:
                    link(dve.scalar_tensor_tensor(out=less[:], in0=one1[:], scalar=-3e38, in1=logit[:],
                                                  op0=ALU.mult, op1=ALU.add))
            dve.tensor_tensor(gap[:], top2[:], top1[:], ALU.subtract).then_inc(gap_ready, 1)
            dve.wait_ge(gap_exp, 1)
            link(dve.tensor_scalar(g2[:], e_gap[:], 1.0, None, ALU.add))
            link(dve.reciprocal(g1[:], g2[:]))
            link(dve.tensor_tensor(g2[:], e_gap[:], g1[:], ALU.mult))
            dve.tensor_tensor(one1[:], one1[:], bc(g1[:], E), ALU.mult)
            link(dve.tensor_tensor(one2[:], one2[:], bc(g2[:], E), ALU.mult))
            link(dve.tensor_tensor(gates[:], one1[:], one2[:], ALU.add))
            dve.tensor_scalar(gate_x[:].rearrange("p b (e r) -> p b e r", r=R),
                              gates[:].unsqueeze(3).to_broadcast([P, NB, E, R]), 2.0, None, ALU.mult
                              ).then_inc(gates_ready, 1)
            for hf in range(2):
                dve.wait_ge(h0_copied, hf + 1)
                dve.wait_ge(gate_t, hf + 1)
                dve.tensor_tensor(h_gated[:, hf * HALF:(hf + 1) * HALF], h_sb[:, hf * HALF:(hf + 1) * HALF],
                                  ps[:, 2 + hf], ALU.mult).then_inc(h_ready, 1)
            for hf in range(2):
                for o in range(KD):
                    n = KD * hf + o
                    dve.wait_ge(l0_out, n + 1)
                    half = slice(hf * HALF, (hf + 1) * HALF)
                    dve.tensor_tensor(xb[:, o, half], xa[:, o, half], ps[:, 4 + n % 2], ALU.add).then_inc(x1_ready, 1)

            dve.wait_ge(tables_stored, 64)
            for hf in range(2):
                half = slice(hf * HALF, (hf + 1) * HALF)
                dve.wait_ge(x1_ready, 2 * KD)
                dve.wait_ge(x1_high, hf + 1)
                dve.tensor_tensor(x1_l[:, :, half], xb[:, :, half], x1_h[:, :, half].bitcast(F32), ALU.subtract).then_inc(x1_low, 1)

            def split_gu(f, par):
                dve.wait_ge(gu_high, f + 1)
                dve.tensor_tensor(gu_l[par][:], w_gu[par][:], gu_h[par][:].bitcast(F32), ALU.subtract).then_inc(gu_low, 1)

            split_gu(0, 0)

            def own_rows(dst, bank, hf, done):
                dve.tensor_tensor(dst[:, hf * HALF:(hf + 1) * HALF].rearrange("p (b t) -> p b t", t=T),
                                  ps[:, bank].rearrange("p (b t) -> p b t", t=T),
                                  own[:, 4 * hf:4 * hf + 4].unsqueeze(2).to_broadcast([P, 4, T]), ALU.mult
                                  ).then_inc(done, 1)

            for n, (dst, bank) in enumerate(((t_gate, 4), (t_up, 6))):
                for hf in range(2):
                    dve.wait_ge(t_full, 2 * n + hf + 1)
                    own_rows(dst, bank + hf, hf, t_ready)

            def gated(f, par):
                for hf in range(2):
                    u = 2 * f + hf
                    if hf == 1 and not (isinstance(f, int) and f == FT - 1):
                        split_gu(f + 1, 1 - par)
                    dve.wait_ge(exp_g, u + 1)
                    dve.tensor_scalar(sil[hf][:], sil[hf][:], 1.0, None, ALU.add).then_inc(silu_step, 1)
                    dve.wait_ge(silu_step, 3 * u + 1)
                    dve.reciprocal(sil[hf][:], sil[hf][:]).then_inc(silu_step, 1)
                    dve.wait_ge(silu_step, 3 * u + 2)
                    dve.tensor_tensor(sil[hf][:], ps[:, hf], sil[hf][:], ALU.mult).then_inc(silu_step, 1)
                    dve.wait_ge(silu_step, 3 * u + 3)
                    dve.wait_ge(up_done, u + 1)
                    dve.tensor_tensor(act[:, ds(f, 1), hf * HALF:(hf + 1) * HALF].rearrange("p o n -> p (o n)"),
                                      ps[:, 2 + hf], sil[hf][:], ALU.mult).then_inc(act_ready, 1)

            over_hidden(dve, gated)
            for hf in range(2):
                dve.wait_ge(td_full, hf + 1)
                own_rows(t_down, 4 + hf, hf, td_ready)
            for o in range(KD):
                for hf in range(2):
                    n = 2 * o + hf
                    dve.wait_ge(l1_out, n + 1)
                    half = slice(hf * HALF, (hf + 1) * HALF)
                    dve.tensor_tensor(xa[:, o, half], xb[:, o, half], ps[:, n % 4], ALU.add).then_inc(x2_ready, 1)

            dve.wait_ge(x2_ready, 2 * KD)

            def add_adapter(b, par):
                dve.wait_ge(l2_out, b + 1)
                wait(dve, x3_turned, b - 1)
                wait(dve, x3_high, b - 1)
                dve.tensor_tensor(x_sum[par][:], xa[:, :, ds(b * T, T)],
                                  ps[:, 4 + par].rearrange("p (k t) -> p k t", t=T), ALU.add).then_inc(x3_summed, 1)
                dve.wait_ge(x3_high, b + 1)
                dve.tensor_tensor(split_tokens(b, par)[:, 1], x_sum[par][:], split_tokens(b, par)[:, 0].bitcast(F32), ALU.subtract
                                  ).then_inc(x3_low, 1)

            def split_piece(u, c, k):
                dve.wait_ge(w_high[u], KD * k + c + 1)
                dve.tensor_tensor(w_l[u][:, c], w_raw[u][:, c], w_h[u][:, c].bitcast(F32), ALU.subtract).then_inc(w_low[u], 1)

            def split_weights(u, k):
                for c in range(KD):
                    split_piece(u, c, k)

            split_weights(W_KV, 0)
            split_weights(W_Q[0], 0)
            over_batches(dve, add_adapter)

            def set_mask(m, par):
                dve.tensor_scalar(mask[par][:, 0:CACHED], iota[:], len_f[:, ds(m % NB, 1)], NEG, ALU.is_ge, ALU.mult
                                  ).then_inc(mask_ready, 1)

            def low_vn(m, par):
                dve.wait_ge(vn_high, m + 1)
                dve.wait_ge(k_raw_ready, m + 1)
                wait(dve, pv_done, KT * (2 * m - 3) + 1)
                dve.tensor_tensor(vn_l[par][:].rearrange("p s d -> p (s d)"), ps[:, PJ, HB * DH:2 * HB * DH],
                                  vn_h[par][:].rearrange("p s d -> p (s d)").bitcast(F32), ALU.subtract).then_inc(vn_low, 1)

            def low_q(m, s):
                dve.wait_ge(q_taken, 2 * m + s + 1)
                wait(dve, scored, 8 * m + 4 * s - 4)
                dve.tensor_tensor(q_l[s][:], q_t[s][:], q_h[s][:].bitcast(F32), ALU.subtract).then_inc(q_low, 1)

            def rotate_k(m, par):
                dve.wait_ge(k_raw_ready, m + 1)
                dve.wait_ge(rstd_ready, 3 * m + 1)
                wait(dve, k_roped, m)
                wait(dve, k_turned, m)
                dve.wait_ge(turn_loaded[par], 16 * (m // 2 + 1))
                for h in range(HB):
                    for part, f in ((part_ck, 2), (part_sk, 3)):
                        last = dve.scalar_tensor_tensor(
                            out=part[:, h], in0=k_raw[:, h], scalar=rs_k[:, h:h + 1],
                            in1=turn[par][:, f], op0=ALU.mult, op1=ALU.mult)
                last.then_inc(k_read, 1)
                dve.wait_ge(k_read, m + 1)
                dve.tensor_tensor(k_rot[:, :, 0:64], part_ck[:, :, 0:64], part_sk[:, :, 64:128], ALU.add)
                dve.tensor_tensor(k_rot[:, :, 64:128], part_ck[:, :, 64:128], part_sk[:, :, 0:64], ALU.add).then_inc(k_roped, 1)

            def cosine_q(m, par, s):
                dve.wait_ge(q_raw_ready, 2 * m + s + 1)
                wait(dve, q_roped, 2 * m + s)
                if s == 0:
                    dve.wait_ge(turn_loaded[par], 16 * (m // 2 + 1))
                dve.tensor_tensor(part_c[:], q_raw[:], turn[par][:, 0:1, :].to_broadcast([P, REP, DH]), ALU.mult
                                  ).then_inc(q_cosine, 1)

            def sum_q(m, s):
                wait(dve, q_turned, 2 * m + s)
                dve.wait_ge(q_cosine, 2 * m + s + 1)
                dve.wait_ge(q_sine, 2 * m + s + 1)
                dve.tensor_tensor(q_rot[:, :, 0:64], part_c[:, :, 0:64], part_s[:, :, 64:128], ALU.add)
                dve.tensor_tensor(q_rot[:, :, 64:128], part_c[:, :, 64:128], part_s[:, :, 0:64], ALU.add).then_inc(q_roped, 1)

            def mask_scores(j, m, par, s, h):
                if h == 0:
                    dve.wait_ge(rstd_ready, 3 * m + 2 + s)
                if h == 0 and s == 0:
                    dve.wait_ge(mask_ready, m + 1)
                dve.wait_ge(scored, 4 * j + h + 1)
                settle(dve, j)
                x = s_ps[:, h % 2, 0:KEYS]
                dve.tensor_tensor_reduce(x, x, mask[par][:], rs_q[:, s, h:h + 1], 3.4e38, ALU.add, ALU.min,
                                         negmax[:, s, h:h + 1]).then_inc(masked, 1)

            def invert_sum(j, s, h):
                dve.wait_ge(exp_done, 4 * j + h + 1)
                dve.reciprocal(rden[:, s, h:h + 1], den[:, s, h:h + 1]).then_inc(rden_ready, 1)

            def low_probs(i, s, t):
                dve.wait_ge(pt_high, KT * i + t + 1)
                wait(dve, pv_done, KT * i + t - 1)
                x = (s + t) % 2
                dve.tensor_tensor(pt_l[x][:], ps[:, PT[x]], pt_h[x][:].bitcast(F32), ALU.subtract).then_inc(pt_low, 1)

            def low_o(i):
                dve.wait_ge(o_high, i + 1)
                wait(dve, out_projected, i)
                dve.tensor_tensor(o_l[:].rearrange("p h t -> p (h t)"), ps[:, OB],
                                  o_h[:].rearrange("p h t -> p (h t)").bitcast(F32), ALU.subtract).then_inc(o_taken, 1)

            def add_out(i, b):
                dve.wait_ge(out_projected, i + 1)
                wait(dve, out_added, i)
                to = acc[:, ds(b, 1), :].rearrange("p o n -> p (o n)")
                dve.tensor_tensor(to, ps[:, PJ], to, ALU.add).then_inc(out_added, 1)

            dve.wait_ge(acc_ready, NB)
            set_mask(0, 0)
            low_vn(0, 0)
            cosine_q(0, 0, 0)
            sum_q(0, 0)
            rotate_k(0, 0)
            low_q(0, 0)
            split_weights(W_Q[1], 0)
            cosine_q(0, 0, 1)
            sum_q(0, 1)
            low_q(0, 1)
            low_vn(1, 1)
            for h in range(REP):
                mask_scores(0, 0, 0, 0, h)
                if h > 0:
                    invert_sum(0, 0, h - 1)

            def half(i, s, scores, queries, out_rows, phase, blk, keys=None):
                if scores:
                    mask_scores(*scores, 0)
                invert_sum(i, s, REP - 1)
                if scores:
                    invert_sum(i + 1, 1 - s, 0)
                if out_rows:
                    add_out(*out_rows)
                low_probs(i, s, 0)
                if scores:
                    mask_scores(*scores, 1)
                low_probs(i, s, 1)
                if queries and s == 0:
                    set_mask(queries[0], queries[1])
                    rotate_k(queries[0], queries[1])
                if scores:
                    invert_sum(i + 1, 1 - s, 1)
                for u, c in splits(phase, s)[0]:
                    split_piece(u, c, blk)
                low_probs(i, s, 2)
                for u, c in splits(phase, s)[1]:
                    split_piece(u, c, blk)
                if queries:
                    cosine_q(*queries)
                    sum_q(queries[0], s)
                low_probs(i, s, 3)
                for u, c in splits(phase, s)[2]:
                    split_piece(u, c, blk)
                low_probs(i, s, 4)
                if scores:
                    mask_scores(*scores, 2)
                if queries:
                    low_q(queries[0], s)
                for u, c in splits(phase, s)[3]:
                    split_piece(u, c, blk)
                if scores:
                    invert_sum(i + 1, 1 - s, 2)
                low_o(i)
                if keys:
                    low_vn(*keys)
                if scores:
                    mask_scores(*scores, 3)

            def step(n, par, phase, k):
                last = not more(n, 1)
                i, m = 2 * n, n + 1
                first = isinstance(n, int) and n == 0
                half(i, 0, (i + 1, n, par, 1), (m, 1 - par, 0) if not last else None,
                     (i - 1, (n - 1) % NB) if not first else None, phase, k)
                half(i + 1, 1, (i + 2, m, 1 - par, 0) if not last else None,
                     (m, 1 - par, 1) if not last else None, (i, n % NB), phase, k,
                     (n + 2, par) if more(n, 2) else None)

            over_steps(dve, step)
            add_out(GROUPS - 1, NB - 1)


def kernel(**inputs):
    import numpy as np
    import concourse.bacc as bacc
    from concourse.bass_utils import run_bass_kernel_spmd

    g = {n: np.asarray(v) for n, v in inputs.items()}

    def pieces(w):
        return w.T.reshape(KD, P, -1).transpose(1, 0, 2)

    def padded(w, axis):
        widths = [(0, 0)] * w.ndim
        widths[axis] = (0, FP - F)
        return np.pad(w, widths)

    x = g["x"].reshape(NT, D)
    gu = [padded(g[f"L1_cond_W_{n}"], 0).reshape(FT, P, KD, P).transpose(0, 3, 2, 1) for n in ("gate", "up")]
    kvw = [np.stack([pieces(g[f"L3_cond_W{n}"][k * HB * DH:(k + 1) * HB * DH]) for k in range(BLOCKS)]) for n in "kv"]
    arrays = {
        "x": pieces(x),
        "w0": pieces(g["L0_cond_W"]),
        "wr": pieces(g["L0_cond_Wr"]),
        "a0": pieces(g["L0_cond_A"].reshape(E * R, D)),
        "b0": g["L0_cond_B"].transpose(0, 2, 1).reshape(E * R, D),
        "w_gu": np.stack(gu, axis=2),
        "w_down": padded(g["L1_cond_W_down"], 1).reshape(KD, P, FT, P).transpose(0, 3, 2, 1),
        "a_gate": g["L1_cond_A_gate"][0].reshape(-1, R, KD, P).transpose(0, 3, 2, 1),
        "a_up": g["L1_cond_A_up"][0].reshape(-1, R, KD, P).transpose(0, 3, 2, 1),
        "a_down": padded(g["L1_cond_A_down"][0], 2).reshape(-1, R, FT, P).transpose(0, 3, 2, 1),
        "b_gate": padded(g["L1_cond_B_gate"][0], 1).transpose(0, 2, 1),
        "b_up": padded(g["L1_cond_B_up"][0], 1).transpose(0, 2, 1),
        "b_down": g["L1_cond_B_down"][0].transpose(0, 2, 1),
        "w2": g["L2_cond_weight"].reshape(-1, D, KD, P).transpose(0, 3, 2, 1),
        "wq": np.stack([pieces(w) for w in g["L3_cond_Wq"].reshape(BLOCKS, -1, D)]),
        "wkv": np.concatenate(kvw, axis=3),
        "wo": g["L3_cond_Wo"].reshape(D, BLOCKS, HB * REP, DH).transpose(1, 3, 2, 0),
        "k_cache": g["L3_cond_k_cache"].reshape(-1, PAGE, BLOCKS, HB, DH).transpose(0, 2, 4, 3, 1),
        "v_cache": g["L3_cond_v_cache"].reshape(-1, PAGE, BLOCKS, HB * DH).transpose(0, 2, 1, 3),
        "q_norm": g["L3_cond_q_norm_w"],
        "k_norm": g["L3_cond_k_norm_w"],
        "inv_f": np.float32(1.0) / np.power(np.float32(10000.0), np.arange(0, DH, 2, dtype=np.float32) / np.float32(DH)),
        "ids": np.concatenate([g["itok_B_2_6"], g["itok_B_0_15"], g["itok_Bx16_0_63"].reshape(-1)])[None],
        "lens": g["itok_B_207_1644"],
        "lang": g["itok_B_0_7"],
    }
    nc = bacc.Bacc("TRN2", target_bir_lowering=False, num_devices=1)
    feed, aps = {}, {}
    for name, v in arrays.items():
        v = np.ascontiguousarray(v)
        feed[f"in_{name}"] = v
        aps[name] = nc.dram_tensor(f"in_{name}", v.shape, mybir.dt.from_np(v.dtype), kind="ExternalInput").ap()
    o = nc.dram_tensor("result", (NB, T, D), F32, kind="ExternalOutput").ap()
    x3 = nc.dram_tensor("x3_scratch", (NB, P, 2, KD, T), F32, kind="Internal").ap()
    turn = nc.dram_tensor("turn_scratch", (NB, P, 4, DH), F32, kind="Internal").ap()
    build(nc, aps, o.rearrange("b t n -> t b n"), x3, turn)
    r = run_bass_kernel_spmd(nc, [feed], core_ids=[0])
    return r.results[0]["result"]
```
